# Optimizing a Trainium2 kernel written in Bass

```python
import numpy as np
import jax
import jax.numpy as jnp

def _softmax(x, axis=-1):
    return jax.nn.softmax(x, axis=axis)

def _gelu(x):
    return jax.nn.gelu(x, approximate=True)

def _silu(x):
    return jax.nn.silu(x)

def _sigmoid(x):
    return jax.nn.sigmoid(x)

def _layernorm(x, axis=-1, eps=1e-05):
    m = jnp.mean(x, axis=axis, keepdims=True)
    v = jnp.var(x, axis=axis, keepdims=True)
    return (x - m) / jnp.sqrt(v + eps)

def _scatter_add(tgt, idx, src, axis=0):
    return tgt.at[idx].add(src)

def _segment_sum(src, seg, n):
    return jax.ops.segment_sum(src, seg, n)
kernel_name = 'mk_macaron_d2_jaxref_r8_b6cd3a'

def setup_inputs(seed: int=0):
    np.random.seed(seed)
    _w = jnp.asarray

    def _L0_attn_setup():
        import jax, jax.numpy as jnp
        import numpy as np
        HEAD = 16
        THETA = 30000.0

        def _layernorm(x, g, b, eps=1e-05):
            mu = jnp.mean(x, axis=-1, keepdims=True)
            var = jnp.mean((x - mu) ** 2, axis=-1, keepdims=True)
            return (x - mu) * jax.lax.rsqrt(var + eps) * g + b

        def _rotary(t, xa):
            B, H, C, D = t.shape
            pos = jnp.arange(C, dtype=t.dtype)
            freqs = jnp.arange(0, D, 2, dtype=t.dtype) / D * jnp.log(jnp.asarray(THETA, t.dtype))
            ang = pos[:, None] * freqs[None, :]
            m = jnp.linalg.norm(xa, axis=-1, keepdims=True)
            fre = (m * jnp.cos(ang))[:, None]
            fim = (m * jnp.sin(ang))[:, None]
            tp = t.reshape(B, H, C, D // 2, 2)
            a, b = (tp[..., 0], tp[..., 1])
            out = jnp.stack([a * fre - b * fim, a * fim + b * fre], axis=-1)
            return out.reshape(B, H, C, D)
        key = jax.random.key(seed)
        ks = jax.random.split(key, 4)
        B, C, Dm = (1, 256, 256)
        hd = Dm // HEAD
        w = 0.02
        return {'x': jax.random.normal(ks[0], (B, C, Dm), jnp.float32), 'qn_g': jnp.ones((Dm,), jnp.float32), 'qn_b': jnp.zeros((Dm,), jnp.float32), 'kvn_g': jnp.ones((Dm,), jnp.float32), 'kvn_b': jnp.zeros((Dm,), jnp.float32), 'Wq': w * jax.random.normal(ks[1], (Dm, Dm), jnp.float32), 'bq': jnp.zeros((Dm,), jnp.float32), 'Wkv': w * jax.random.normal(ks[2], (Dm, 2 * Dm), jnp.float32), 'bkv': jnp.zeros((2 * Dm,), jnp.float32), 'Wo': w * jax.random.normal(ks[3], (Dm, Dm), jnp.float32), 'bo': jnp.zeros((Dm,), jnp.float32), 'ln_g': jnp.ones((hd,), jnp.float32), 'ln_b': jnp.zeros((hd,), jnp.float32)}
    _L0_attn_in = _L0_attn_setup()

    def _L0_ffn_setup():
        import jax, jax.numpy as jnp
        import numpy as np
        B, S, D, H = (4, 256, 256, 1024)

        def fwht(x):
            orig_shape = x.shape
            n = orig_shape[-1]
            x = x.reshape(-1, n)
            h = 1
            while h < n:
                xb = x.reshape(-1, n // (2 * h), 2, h)
                a = xb[:, :, 0, :]
                b = xb[:, :, 1, :]
                x = jnp.stack([a + b, a - b], axis=2).reshape(-1, n)
                h *= 2
            scale = jnp.asarray(1.0 / np.sqrt(n), dtype=x.dtype)
            return (x * scale).reshape(orig_shape)
        key = jax.random.key(seed)
        kx, k1, k2, k3 = jax.random.split(key, 4)
        x = jax.random.normal(kx, (B, S, D), dtype=jnp.float32)
        W1 = jax.random.normal(k1, (H, D), dtype=jnp.float32) * (1.0 / np.sqrt(D))
        W2 = jax.random.normal(k2, (D, H), dtype=jnp.float32) * (1.0 / np.sqrt(H))
        W3 = jax.random.normal(k3, (H, D), dtype=jnp.float32) * (1.0 / np.sqrt(D))
        return {'x': x, 'W1': W1, 'W2': W2, 'W3': W3}
    _L0_ffn_in = _L0_ffn_setup()

    def _L1_attn_setup():
        import jax, jax.numpy as jnp
        import numpy as np
        NUM_HEADS = 16
        ROPE_BASE = 10000.0

        def _rotate_half(x):
            half = x.shape[-1] // 2
            x1, x2 = (x[..., :half], x[..., half:])
            return jnp.concatenate((-x2, x1), axis=-1)

        def _rope_cos_sin(seq_len, dim, dtype):
            inv_freq = 1.0 / ROPE_BASE ** (jnp.arange(0, dim, 2, dtype=jnp.float32) / dim)
            t = jnp.arange(seq_len, dtype=jnp.float32)
            freqs = jnp.einsum('i,j->ij', t, inv_freq)
            emb = jnp.concatenate((freqs, freqs), axis=-1)
            return (emb.astype(dtype), None)
        key = jax.random.key(seed)
        k1, k2, k3 = jax.random.split(key, 3)
        B, S, D = (4, 128, 256)
        return {'hidden_states': jax.random.normal(k1, (B, S, D), dtype=jnp.float32), 'w_qkv': jax.random.normal(k2, (3 * D, D), dtype=jnp.float32) * 0.02, 'b_qkv': jax.random.normal(k3, (3 * D,), dtype=jnp.float32) * 0.02}
    _L1_attn_in = _L1_attn_setup()

    def _L1_ffn_setup():
        import jax, jax.numpy as jnp
        import numpy as np
        ALPHA = 1.702
        LIMIT = 7.0
        TOP_K = 4
        B, S, H = (1, 128, 256)
        E, D = (16, 256)
        key = jax.random.key(seed)
        ks = jax.random.split(key, 7)
        s = 0.02
        return {'hidden_states': jax.random.normal(ks[0], (B, S, H), dtype=jnp.float32), 'router_weight': jax.random.normal(ks[1], (E, H), dtype=jnp.float32) * s, 'router_bias': jax.random.normal(ks[2], (E,), dtype=jnp.float32) * s, 'gate_up_proj': jax.random.normal(ks[3], (E, H, 2 * D), dtype=jnp.float32) * s, 'gate_up_proj_bias': jax.random.normal(ks[4], (E, 2 * D), dtype=jnp.float32) * s, 'down_proj': jax.random.normal(ks[5], (E, D, H), dtype=jnp.float32) * s, 'down_proj_bias': jax.random.normal(ks[6], (E, H), dtype=jnp.float32) * s}
    _L1_ffn_in = _L1_ffn_setup()
    _d = {'L0_attn_x': _L0_attn_in['x'], 'L0_attn_qn_g': _L0_attn_in['qn_g'], 'L0_attn_qn_b': _L0_attn_in['qn_b'], 'L0_attn_kvn_g': _L0_attn_in['kvn_g'], 'L0_attn_kvn_b': _L0_attn_in['kvn_b'], 'L0_attn_Wq': _L0_attn_in['Wq'], 'L0_attn_bq': _L0_attn_in['bq'], 'L0_attn_Wkv': _L0_attn_in['Wkv'], 'L0_attn_bkv': _L0_attn_in['bkv'], 'L0_attn_Wo': _L0_attn_in['Wo'], 'L0_attn_bo': _L0_attn_in['bo'], 'L0_attn_ln_g': _L0_attn_in['ln_g'], 'L0_attn_ln_b': _L0_attn_in['ln_b'], 'L0_ffn_W1': _L0_ffn_in['W1'], 'L0_ffn_W2': _L0_ffn_in['W2'], 'L0_ffn_W3': _L0_ffn_in['W3'], 'L1_attn_w_qkv': _L1_attn_in['w_qkv'], 'L1_attn_b_qkv': _L1_attn_in['b_qkv'], 'L1_ffn_router_weight': _L1_ffn_in['router_weight'], 'L1_ffn_router_bias': _L1_ffn_in['router_bias'], 'L1_ffn_gate_up_proj': _L1_ffn_in['gate_up_proj'], 'L1_ffn_gate_up_proj_bias': _L1_ffn_in['gate_up_proj_bias'], 'L1_ffn_down_proj': _L1_ffn_in['down_proj'], 'L1_ffn_down_proj_bias': _L1_ffn_in['down_proj_bias']}
    _x0 = _d['L0_attn_x']
    _d['L0_attn_x'] = jax.random.normal(jax.random.fold_in(jax.random.key(seed), 1), (1, 1024, 256), dtype=_x0.dtype)
    del _x0
    return _d

def reference(L0_attn_x, L0_attn_qn_g, L0_attn_qn_b, L0_attn_kvn_g, L0_attn_kvn_b, L0_attn_Wq, L0_attn_bq, L0_attn_Wkv, L0_attn_bkv, L0_attn_Wo, L0_attn_bo, L0_attn_ln_g, L0_attn_ln_b, L0_ffn_W1, L0_ffn_W2, L0_ffn_W3, L1_attn_w_qkv, L1_attn_b_qkv, L1_ffn_router_weight, L1_ffn_router_bias, L1_ffn_gate_up_proj, L1_ffn_gate_up_proj_bias, L1_ffn_down_proj, L1_ffn_down_proj_bias):

    def _L0_attn_ref(x, qn_g, qn_b, kvn_g, kvn_b, Wq, bq, Wkv, bkv, Wo, bo, ln_g, ln_b):
        import jax, jax.numpy as jnp
        import numpy as np
        HEAD = 16
        THETA = 30000.0

        def _layernorm(x, g, b, eps=1e-05):
            mu = jnp.mean(x, axis=-1, keepdims=True)
            var = jnp.mean((x - mu) ** 2, axis=-1, keepdims=True)
            return (x - mu) * jax.lax.rsqrt(var + eps) * g + b

        def _rotary(t, xa):
            B, H, C, D = t.shape
            pos = jnp.arange(C, dtype=t.dtype)
            freqs = jnp.arange(0, D, 2, dtype=t.dtype) / D * jnp.log(jnp.asarray(THETA, t.dtype))
            ang = pos[:, None] * freqs[None, :]
            m = jnp.linalg.norm(xa, axis=-1, keepdims=True)
            fre = (m * jnp.cos(ang))[:, None]
            fim = (m * jnp.sin(ang))[:, None]
            tp = t.reshape(B, H, C, D // 2, 2)
            a, b = (tp[..., 0], tp[..., 1])
            out = jnp.stack([a * fre - b * fim, a * fim + b * fre], axis=-1)
            return out.reshape(B, H, C, D)
        B, C, Dm = x.shape
        H = HEAD
        hd = Dm // H
        scale = hd ** (-0.25)
        q = (_layernorm(x, qn_g, qn_b) @ Wq + bq).reshape(B, C, H, hd).transpose(0, 2, 1, 3)
        kv = (_layernorm(x, kvn_g, kvn_b) @ Wkv + bkv).reshape(B, C, 2, H, hd)
        kv = kv.transpose(2, 0, 3, 1, 4)
        k, v = (kv[0], kv[1])
        q = q * scale
        k = k * scale
        q = _rotary(q, x)
        k = _rotary(k, x)
        qn = _layernorm(q, ln_g, ln_b)
        kn = _layernorm(k, ln_g, ln_b)
        scores = jnp.einsum('bhqd,bhkd->bhqk', qn, kn) / jnp.sqrt(jnp.asarray(hd, x.dtype))
        causal = jnp.tril(jnp.ones((C, C), bool))
        scores = jnp.where(causal, scores, jnp.finfo(scores.dtype).min)
        w = jax.nn.softmax(scores, axis=-1)
        a = jnp.einsum('bhqk,bhkd->bhqd', w, v)
        out = a.transpose(0, 2, 1, 3).reshape(B, C, Dm) @ Wo + bo
        return out

    def _L0_ffn_ref(x, W1, W2, W3):
        import jax, jax.numpy as jnp
        import numpy as np
        B, S, D, H = (4, 256, 256, 1024)

        def fwht(x):
            orig_shape = x.shape
            n = orig_shape[-1]
            x = x.reshape(-1, n)
            h = 1
            while h < n:
                xb = x.reshape(-1, n // (2 * h), 2, h)
                a = xb[:, :, 0, :]
                b = xb[:, :, 1, :]
                x = jnp.stack([a + b, a - b], axis=2).reshape(-1, n)
                h *= 2
            scale = jnp.asarray(1.0 / np.sqrt(n), dtype=x.dtype)
            return (x * scale).reshape(orig_shape)
        up_gate = jnp.einsum('bsd,hd->bsh', x, W1)
        up_lin = jnp.einsum('bsd,hd->bsh', x, W3)
        hidden = jax.nn.silu(up_gate) * up_lin
        hidden = fwht(hidden)
        out = jnp.einsum('bsh,dh->bsd', hidden, W2)
        return out

    def _L1_attn_ref(hidden_states, w_qkv, b_qkv):
        import jax, jax.numpy as jnp
        import numpy as np
        NUM_HEADS = 16
        ROPE_BASE = 10000.0

        def _rotate_half(x):
            half = x.shape[-1] // 2
            x1, x2 = (x[..., :half], x[..., half:])
            return jnp.concatenate((-x2, x1), axis=-1)

        def _rope_cos_sin(seq_len, dim, dtype):
            inv_freq = 1.0 / ROPE_BASE ** (jnp.arange(0, dim, 2, dtype=jnp.float32) / dim)
            t = jnp.arange(seq_len, dtype=jnp.float32)
            freqs = jnp.einsum('i,j->ij', t, inv_freq)
            emb = jnp.concatenate((freqs, freqs), axis=-1)
            return (emb.astype(dtype), None)
        B, S, D = hidden_states.shape
        H = NUM_HEADS
        hd = D // H
        qkv = jnp.einsum('bsd,ed->bse', hidden_states, w_qkv) + b_qkv
        qkv = qkv.reshape(B, S, H, 3 * hd)
        q = jnp.transpose(qkv[..., :hd], (0, 2, 1, 3))
        k = jnp.transpose(qkv[..., hd:2 * hd], (0, 2, 1, 3))
        v = jnp.transpose(qkv[..., 2 * hd:], (0, 2, 1, 3))
        emb, _ = _rope_cos_sin(S, hd, hidden_states.dtype)
        cos = jnp.cos(emb)[None, None, :, :]
        sin = jnp.sin(emb)[None, None, :, :]
        q = q * cos + _rotate_half(q) * sin
        k = k * cos + _rotate_half(k) * sin
        norm = jnp.sqrt(jnp.asarray(hd, dtype=jnp.float32)).astype(q.dtype)
        scores = jnp.einsum('bhqd,bhkd->bhqk', q, k) / norm
        causal = jnp.tril(jnp.ones((S, S), dtype=bool))[None, None]
        mask_value = jnp.finfo(scores.dtype).min
        scores = jnp.where(causal, scores, mask_value)
        attn = jax.nn.softmax(scores, axis=-1)
        out = jnp.einsum('bhqk,bhkd->bhqd', attn, v)
        return jnp.transpose(out, (0, 2, 1, 3)).reshape(B, S, D)

    def _L1_ffn_ref(hidden_states, router_weight, router_bias, gate_up_proj, gate_up_proj_bias, down_proj, down_proj_bias):
        import jax, jax.numpy as jnp
        import numpy as np
        ALPHA = 1.702
        LIMIT = 7.0
        TOP_K = 4
        B, S, H = (1, 128, 256)
        E, D = (16, 256)
        batch, seq, hdim = hidden_states.shape
        x = hidden_states.reshape(-1, hdim)
        T = x.shape[0]
        logits = x @ router_weight.T + router_bias
        top_val, top_idx = jax.lax.top_k(logits, TOP_K)
        top_val = jax.nn.softmax(top_val, axis=-1)
        router_scores = jnp.zeros_like(logits).at[jnp.arange(T)[:, None], top_idx].set(top_val)
        gate_up = jnp.einsum('th,ehd->etd', x, gate_up_proj) + gate_up_proj_bias[:, None, :]
        gate = gate_up[..., ::2]
        up = gate_up[..., 1::2]
        gate = jnp.minimum(gate, LIMIT)
        up = jnp.clip(up, -LIMIT, LIMIT)
        glu = gate * jax.nn.sigmoid(gate * ALPHA)
        out = jnp.einsum('etd,edh->eth', (up + 1.0) * glu, down_proj) + down_proj_bias[:, None, :]
        out = out * router_scores.T[:, :, None]
        out = out.sum(axis=0)
        return out.reshape(batch, seq, hdim)
    x = L0_attn_x
    x = x + 0.5 * _L0_ffn_ref(_layernorm(x, axis=-1), L0_ffn_W1, L0_ffn_W2, L0_ffn_W3)
    x = x + _L0_attn_ref(_layernorm(x, axis=-1), L0_attn_qn_g, L0_attn_qn_b, L0_attn_kvn_g, L0_attn_kvn_b, L0_attn_Wq, L0_attn_bq, L0_attn_Wkv, L0_attn_bkv, L0_attn_Wo, L0_attn_bo, L0_attn_ln_g, L0_attn_ln_b)
    x = x + 0.5 * _L0_ffn_ref(_layernorm(x, axis=-1), L0_ffn_W1, L0_ffn_W2, L0_ffn_W3)
    x = x + 0.5 * _L1_ffn_ref(_layernorm(x, axis=-1), L1_ffn_router_weight, L1_ffn_router_bias, L1_ffn_gate_up_proj, L1_ffn_gate_up_proj_bias, L1_ffn_down_proj, L1_ffn_down_proj_bias)
    x = x + _L1_attn_ref(_layernorm(x, axis=-1), L1_attn_w_qkv, L1_attn_b_qkv)
    x = x + 0.5 * _L1_ffn_ref(_layernorm(x, axis=-1), L1_ffn_router_weight, L1_ffn_router_bias, L1_ffn_gate_up_proj, L1_ffn_gate_up_proj_bias, L1_ffn_down_proj, L1_ffn_down_proj_bias)
    return x

_drawn_inputs = setup_inputs


def setup_inputs(seed=0):
    import zlib

    import numpy as np

    out = dict(_drawn_inputs(seed))
    spreads = {'L0_attn_qn_g': (1.0, 0.6),
     'L0_attn_qn_b': (0.0, 0.8),
     'L0_attn_kvn_g': (1.0, 0.6),
     'L0_attn_kvn_b': (0.0, 0.8),
     'L0_attn_bq': (0.0, 0.8),
     'L0_attn_bkv': (0.0, 0.1),
     'L0_attn_bo': (0.0, 0.1),
     'L0_attn_ln_g': (1.0, 0.6),
     'L0_attn_ln_b': (0.0, 0.8)}
    factors = {'L0_attn_Wq': 4.539,
     'L0_attn_Wkv': 3.29,
     'L1_attn_b_qkv': 3.255,
     'L1_ffn_router_bias': 8.0,
     'L1_ffn_gate_up_proj_bias': 34.0,
     'L1_ffn_down_proj_bias': 6.803}
    for name, (base, spread) in spreads.items():
        noise = np.random.default_rng([zlib.crc32(name.encode()), seed]).standard_normal(out[name].shape)
        drawn = base * np.exp(spread * noise) if base else spread * noise
        out[name] = jnp.asarray(drawn.astype(out[name].dtype))
    for name, factor in factors.items():
        out[name] = (out[name] * factor).astype(out[name].dtype)
    return out
```

```python
import math
from contextlib import ExitStack

import numpy as np

import concourse.bass as bass
from concourse import mybir

F32 = mybir.dt.float32
F32R = mybir.dt.float32r
BF16 = mybir.dt.bfloat16
ALU = mybir.AluOpType
ACT = mybir.ActivationFunctionType
AX_X = mybir.AxisListType.X

P = 128
D = 256
KC = D // P
T = 1024
TB = T // P
HALF = 512
NHALF = T // HALF
FF = 1024
FB = FF // P
HEADS = 16
HD = D // HEADS
STRIP = 32
GH = P // STRIP
GROUPS = HEADS // GH
E = 16
TOPK = 4
EW = 2 * KC * 2 * P
ED = KC * D
EB = 2 * KC
ALPHA_LIMIT = 7.0
EPS = 1e-5
MASKED = -1.0e30
SENTINEL = -3.0e38
TAKEN = -3.3e38


def bcast(ap, axis, n):
    wide = ap.unsqueeze(axis)
    shape = list(wide.shape)
    shape[axis] = n
    return wide.broadcast_to(shape)


def build(nc, a, out, stages):
    ctx = ExitStack()
    with ctx:
        def sb(name, shape, dt=F32):
            return ctx.enter_context(nc.sbuf_tensor(name, shape, dt))

        def sem(name):
            return ctx.enter_context(nc.semaphore(name))

        banks = [ctx.enter_context(nc.psum_tensor(f"bank{i}", [P, 512], F32)) for i in range(8)]
        score_rows = nc.dram_tensor("score_rows", (2, E, T), F32, kind="Internal").ap()

        x = sb("x", [P, TB, D])
        xn = sb("xn", [P, TB, D])
        xt_hi = sb("xt_hi", [P, KC, T], F32R)
        xt_lo = sb("xt_lo", [P, KC, T], F32R)
        w1 = [sb(f"w1_{k}", [P, KC, FF], F32R) for k in ("hi", "lo")]
        w3 = [sb(f"w3_{k}", [P, KC, FF], F32R) for k in ("hi", "lo")]
        w2 = [sb(f"w2_{k}", [P, FB, D], F32R) for k in ("hi", "lo")]
        wr = [[sb(f"wr{i}_{k}", [P, EW + ED], F32R) for k in ("hi", "lo")] for i in range(2)]
        hid = [[sb(f"hid{i}_{k}", [P, HALF], F32R) for k in ("hi", "lo")] for i in range(2)]
        ident = sb("ident", [P, P])
        ident_b = sb("ident_b", [P, P], BF16)
        had_r = sb("had_r", [P, P], F32R)
        mask_qk = sb("mask_qk", [P, P], BF16)
        mask_kq = sb("mask_kq", [P, P], BF16)
        half_neg = sb("half_neg", [P, 32])
        half_pos = sb("half_pos", [P, 32])
        stats = sb("stats", [P, TB, 6])
        meanvar = sb("meanvar", [P, TB, 2])
        vareps = sb("vareps", [P, TB])
        rstd = sb("rstd", [P, TB])
        router_raw = sb("router_raw", [P, KC, E])
        router_w = [sb(f"router_{k}", [P, KC, E], F32R) for k in ("hi", "lo")]
        router_b = sb("router_b", [P, E])
        down_b = sb("down_b", [E, D])
        bias_one = sb("bias_one", [P, EB])
        qkv_b = sb("qkv_b", [P, 3 * D])
        out_b = sb("out_b", [P, D])
        head_g = sb("head_g", [P, HD])
        head_b = sb("head_b", [P, HD])
        in_gb = sb("in_gb", [P, 4, KC])
        cosine = sb("cosine", [P, TB, HD // 2])
        sine = sb("sine", [P, TB, HD // 2])
        row_max = sb("row_max", [P, TB, HEADS, 2])
        group_max = sb("group_max", [P, TB, GH])
        head_sum = sb("head_sum", [P, 2 * HEADS])
        head_var = sb("head_var", [P, 2 * HEADS])
        head_rstd = sb("head_rstd", [P, 2 * HEADS])
        inv_den = sb("inv_den", [P, 4, GH])
        xnorm = sb("xnorm", [P, TB])
        arena = sb("arena", [P, 20 * 1024])
        at = [0]

        def cut(n, *shape):
            s = arena[:, at[0]:at[0] + n]
            at[0] += n
            assert at[0] <= 20 * 1024
            if len(shape) == 2:
                return s.rearrange("p (a b) -> p a b", a=shape[0])
            if len(shape) == 3:
                return s.rearrange("p (a b c) -> p a b c", a=shape[0], b=shape[1])
            return s

        chain_sem = {k: sem(f"{k}_chain") for k in ("dve", "act", "pool")}
        chained = {k: 0 for k in chain_sem}

        def link(eng, k, ins):
            chained[k] += 1
            ins.then_inc(chain_sem[k], 1)
            eng.wait_ge(chain_sem[k], chained[k])

        at[0] = 0
        raw1 = cut(KC * FF, KC, FF)
        raw3 = cut(KC * FF, KC, FF)
        raw2 = cut(FB * D, FB, D)
        fly = [cut(FB * D, FB, D) for _ in range(2)]
        mask_raw = cut(3 * P, 3, P)
        c_loaded = sem("c_loaded")
        x_loaded = sem("x_loaded")
        w_loaded = [sem(f"w_loaded{i}") for i in range(3)]
        w_hi = sem("w_hi")
        w_lo = sem("w_lo")
        had_done = sem("had_done")
        had_copied = sem("had_copied")
        fly_done = sem("fly_done")
        pool_consts = sem("pool_consts")

        def load_sync(sp):
            sp.dma_start(x[:], a["x"].rearrange("(b p) d -> p b d", p=P)).then_inc(x_loaded, 16)
            sp.dma_start(raw2, a["w2t"].rearrange("(b p) d -> p b d", p=P)).then_inc(w_loaded[0], 16)
            sp.dma_start(raw1, a["w1t"].rearrange("(c p) h -> p c h", p=P)).then_inc(w_loaded[1], 16)
            sp.dma_start(raw3, a["w3t"].rearrange("(c p) h -> p c h", p=P)).then_inc(w_loaded[2], 16)

        def load_act(act):
            act.dma_start(ident[:], a["ident"]).then_inc(c_loaded, 16)
            act.dma_start(mask_raw[:, 0, :], a["hadamard"]).then_inc(c_loaded, 16)
            act.dma_start(mask_raw[:, 1, :], a["mask_qk"]).then_inc(c_loaded, 16)
            act.dma_start(mask_raw[:, 2, :], a["mask_kq"]).then_inc(c_loaded, 16)
            act.dma_start(router_raw[:], a["router_t"].rearrange("(c p) e -> p c e", p=P)).then_inc(c_loaded, 16)
            act.dma_start(router_b[:], a["router_b"].partition_broadcast(P)).then_inc(c_loaded, 16)
            act.dma_start(down_b[:], a["down_b"]).then_inc(c_loaded, 16)

        C_ALL = 7 * 16
        w2_raw = [xt_hi[:].rearrange("p c t -> p (c t)"), xt_lo[:].rearrange("p c t -> p (c t)")]
        flat2 = raw2.rearrange("p b d -> p (b d)")

        def prep_act(act):
            act.wait_ge(w_loaded[0], 16)
            act.activation(w2_raw[0], flat2, ACT.Copy).then_inc(w_hi, 1)
            act.wait_ge(w_loaded[1], 16)
            act.activation(w1[0][:], raw1, ACT.Copy).then_inc(w_hi, 1)
            act.wait_ge(w_loaded[2], 16)
            act.activation(w3[0][:], raw3, ACT.Copy).then_inc(w_hi, 1)
            for i in range(4):
                act.wait_ge(had_done, i + 1)
                act.activation(fly[0][:, 2 * i:2 * i + 2, :].rearrange("p b d -> p (b d)"), banks[i][:], ACT.Copy)\
                   .then_inc(had_copied, 1)
            act.wait_ge(fly_done, 1)
            act.activation(w2[0][:], fly[1], ACT.Copy, scale=1.0 / 64.0).then_inc(w_hi, 1)

        def prep_pool(pool):
            pool.memset(half_neg[:], -0.5).then_inc(pool_consts, 1)
            pool.memset(half_pos[:], 0.5).then_inc(pool_consts, 1)
            pool.memset(bias_one[:, 0:KC], 0.0).then_inc(pool_consts, 1)
            pool.memset(bias_one[:, KC:EB], 1.0).then_inc(pool_consts, 1)

        def prep_dve(dve):
            dve.wait_ge(c_loaded, C_ALL)
            dve.tensor_copy(had_r[:], mask_raw[:, 0, :]).then_inc(w_lo, 1)
            dve.tensor_copy(mask_qk[:], mask_raw[:, 1, :]).then_inc(w_lo, 1)
            dve.tensor_copy(mask_kq[:], mask_raw[:, 2, :]).then_inc(w_lo, 1)
            dve.tensor_copy(ident_b[:], ident[:]).then_inc(w_lo, 1)
            dve.wait_ge(w_hi, 1)
            dve.tensor_tensor(w2_raw[1], flat2, w2_raw[0].bitcast(F32), ALU.subtract).then_inc(w_lo, 1)
            dve.wait_ge(w_hi, 2)
            dve.tensor_tensor(w1[1][:], raw1, w1[0][:].bitcast(F32), ALU.subtract).then_inc(w_lo, 1)
            dve.wait_ge(w_hi, 3)
            dve.tensor_tensor(w3[1][:], raw3, w3[0][:].bitcast(F32), ALU.subtract).then_inc(w_lo, 1)
            link(dve, "dve", dve.tensor_copy(router_w[0][:], router_raw[:]))
            dve.tensor_tensor(router_w[1][:], router_raw[:], router_w[0][:].bitcast(F32), ALU.subtract).then_inc(w_lo, 1)
            dve.wait_ge(had_copied, 4)
            for k in range(3):
                s, d = fly[k % 2], fly[1 - k % 2]
                step = 1 << k
                sv = s.rearrange("p (a two b) d -> p a two (b d)", two=2, b=step)
                dv = d.rearrange("p (a two b) d -> p a two (b d)", two=2, b=step)
                link(dve, "dve", dve.tensor_tensor(dv[:, :, 0, :], sv[:, :, 0, :], sv[:, :, 1, :], ALU.add))
                ins = dve.tensor_tensor(dv[:, :, 1, :], sv[:, :, 0, :], sv[:, :, 1, :], ALU.subtract)
                if k < 2:
                    link(dve, "dve", ins)
                else:
                    ins.then_inc(fly_done, 1)
            dve.wait_ge(w_hi, 4)
            dve.scalar_tensor_tensor(w2[1][:].rearrange("p b d -> p (b d)"), fly[1].rearrange("p b d -> p (b d)"), 1.0 / 64.0,
                                     w2[0][:].rearrange("p b d -> p (b d)").bitcast(F32), ALU.mult, ALU.subtract).then_inc(w_lo, 1)

        def prep_pe(pe):
            pe.wait_ge(w_hi, 1)
            pe.wait_ge(w_lo, 5)
            for i in range(4):
                for k in range(2):
                    ins = pe.matmul(banks[i][:], had_r[:], w2_raw[k][:, 512 * i:512 * i + 512], start=k == 0, stop=k == 1)
                ins.then_inc(had_done, 1)

        class Sems:

            def __init__(self, stage, totals, before=None):
                self.sems = before.sems if before else {n: sem(f"{stage}_{n}") for n in totals}
                self.base = totals if before else dict.fromkeys(totals, 0)

            def __getitem__(self, n):
                return self.sems[n]

            def after(self, n, value):
                return self.sems[n], self.base[n] + value

        def norm_dve(dve, s, src, dst, waits):
            for w in waits:
                dve.wait_ge(*w)
            for b in range(TB):
                ins = dve.bn_stats(stats[:, b, :], src[:, b, :])
            link(dve, "dve", ins)
            for b in range(TB):
                ins = dve.bn_aggr(meanvar[:, b, :], stats[:, b, :])
            link(dve, "dve", ins)
            dve.tensor_scalar(vareps[:], meanvar[:, :, 1], EPS, None, ALU.add).then_inc(s["var"], 1)
            dve.wait_ge(*s.after("rstd", 1))
            for b in range(TB):
                dve.tensor_scalar(dst[:, b, :], src[:, b, :], meanvar[:, b, 0:1], rstd[:, b:b + 1],
                                  ALU.subtract, ALU.mult).then_inc(s["normed"], 1)

        def norm_pool(pool, s):
            pool.wait_ge(*s.after("var", 1))
            pool.tensor_tensor(rstd[:], vareps[:], half_neg[:, 0:TB], ALU.pow).then_inc(s["rstd"], 1)

        def turn_pe(pe, s, src):
            for i in range(NHALF * KC):
                n, c = i // KC, i % KC
                pe.wait_ge(*s.after("normed", TB // NHALF * (n + 1)))
                for b in range(4):
                    ins = pe.transpose(banks[i][:, b * P:(b + 1) * P], src[:, 4 * n + b, c * P:(c + 1) * P], ident[:])
                ins.then_inc(s["turned"], 1)

        def turn_act(act, s):
            for i in range(NHALF * KC):
                n, c = i // KC, i % KC
                act.wait_ge(*s.after("turned", i + 1))
                act.activation(xt_hi[:, c, n * HALF:(n + 1) * HALF], banks[i][:], ACT.Copy).then_inc(s["xt_hi"], 1)

        def turn_dve(dve, s):
            for i in range(NHALF * KC):
                n, c = i // KC, i % KC
                dve.wait_ge(*s.after("xt_hi", i + 1))
                q = slice(n * HALF, (n + 1) * HALF)
                dve.tensor_tensor(xt_lo[:, c, q], banks[i][:], xt_hi[:, c, q].bitcast(F32), ALU.subtract)\
                   .then_inc(s["xt_lo"], 1)

        NORM = dict(var=1, rstd=1, normed=TB, turned=4, xt_hi=4, xt_lo=4)

        def three(pe, dst, w, m, kcs, first=True, last=True):
            n = len(kcs) * 3
            for i, k in enumerate(kcs):
                for j, (hw, hm) in enumerate(((0, 0), (0, 1), (1, 0))):
                    ins = pe.matmul(dst, w[hw](k), m[hm](k), start=first and i + j == 0, stop=last and 3 * i + j == n - 1,
                                    skip_group_check=not (first and last))
            return ins

        def moving(n):
            q = slice(n * HALF, (n + 1) * HALF)
            return [lambda k: xt_hi[:, k, q], lambda k: xt_lo[:, k, q]]

        def finish_act(act, s, outT, scale, done):
            for n in range(NHALF):
                for c in range(KC):
                    act.wait_ge(*s.after("down", done(n)))
                    act.activation(outT[:, c, n * HALF:(n + 1) * HALF], banks[4 + 2 * n + c][:], ACT.Copy, scale=scale)\
                       .then_inc(s["out_copied"], 1)

        def finish_pe(pe, s, outT):
            for i in range(4):
                pe.wait_ge(*s.after("out_copied", KC * (i // 2 + 1)))
                for b in range(2):
                    for c in range(KC):
                        ins = pe.transpose(banks[i][:, b * D + c * P:b * D + (c + 1) * P],
                                           outT[:, c, (2 * i + b) * P:(2 * i + b + 1) * P], ident[:])
                ins.then_inc(s["out_turned"], 1)

        def finish_dve(dve, s):
            for i in range(4):
                dve.wait_ge(*s.after("out_turned", i + 1))
                v = x[:, 2 * i:2 * i + 2, :].rearrange("p b d -> p (b d)")
                dve.tensor_tensor(v, banks[i][:], v, ALU.add).then_inc(s["x_done"], 1)

        at[0] = 0
        f_silu = [cut(HALF) for _ in range(2)]
        f_hid = [cut(HALF) for _ in range(2)]
        at[0] = max(at[0], 16 * 1024)
        f_out = cut(KC * T, KC, T)
        UNITS = NHALF * FB
        FFN = NORM | dict.fromkeys("gate up silu hidden hid_hi hid_lo down".split(), UNITS) | dict.fromkeys(
            "out_copied out_turned x_done".split(), 4)

        def ffn_pe(pe, s, waits):
            def gate_up(i):
                n, h = i // FB, i % FB
                if i >= 2:
                    pe.wait_ge(*s.after("silu", i - 1))
                three(pe, banks[i % 2][:], [lambda k: w1[0][:, k, h * P:(h + 1) * P], lambda k: w1[1][:, k, h * P:(h + 1) * P]],
                      moving(n), range(KC)).then_inc(s["gate"], 1)
                if i >= 2:
                    pe.wait_ge(*s.after("hidden", i - 1))
                three(pe, banks[2 + i % 2][:], [lambda k: w3[0][:, k, h * P:(h + 1) * P], lambda k: w3[1][:, k, h * P:(h + 1) * P]],
                      moving(n), range(KC)).then_inc(s["up"], 1)

            turn_pe(pe, s, xn)
            pe.wait_ge(*s.after("xt_lo", 4))
            for w in waits:
                pe.wait_ge(*w)
            gate_up(0)
            gate_up(1)
            for i in range(UNITS):
                if i + 2 < UNITS:
                    gate_up(i + 2)
                n, h = i // FB, i % FB
                pe.wait_ge(*s.after("hid_lo", i + 1))
                for c in range(KC):
                    ins = three(pe, banks[4 + 2 * n + c][:],
                                [lambda k: w2[0][:, h, c * P:(c + 1) * P], lambda k: w2[1][:, h, c * P:(c + 1) * P]],
                                [lambda k: hid[i % 2][0][:], lambda k: hid[i % 2][1][:]], [0], first=h == 0, last=h == FB - 1)
                ins.then_inc(s["down"], 1)
            finish_pe(pe, s, f_out)

        def ffn_act(act, s):
            turn_act(act, s)
            for i in range(UNITS + 1):
                if i < UNITS:
                    act.wait_ge(*s.after("gate", i + 1))
                    if i >= 2:
                        act.wait_ge(*s.after("hidden", i - 1))
                    act.activation(f_silu[i % 2], banks[i % 2][:], ACT.Silu).then_inc(s["silu"], 1)
                if i >= 1:
                    j = i - 1
                    act.wait_ge(*s.after("hidden", j + 1))
                    if j >= 2:
                        act.wait_ge(*s.after("down", j - 1))
                    act.activation(hid[j % 2][0][:], f_hid[j % 2], ACT.Copy).then_inc(s["hid_hi"], 1)
            finish_act(act, s, f_out, 1.0, lambda n: FB * (n + 1))

        def ffn_dve(dve, s, waits):
            norm_dve(dve, s, x, xn, waits)
            turn_dve(dve, s)
            for i in range(UNITS + 1):
                if i < UNITS:
                    dve.wait_ge(*s.after("up", i + 1))
                    dve.wait_ge(*s.after("silu", i + 1))
                    if i >= 2:
                        dve.wait_ge(*s.after("hid_lo", i - 1))
                    dve.tensor_tensor(f_hid[i % 2], banks[2 + i % 2][:], f_silu[i % 2], ALU.mult).then_inc(s["hidden"], 1)
                if i >= 1:
                    j = i - 1
                    dve.wait_ge(*s.after("hid_hi", j + 1))
                    if j >= 2:
                        dve.wait_ge(*s.after("down", j - 1))
                    dve.tensor_tensor(hid[j % 2][1][:], f_hid[j % 2], hid[j % 2][0][:].bitcast(F32), ALU.subtract)\
                       .then_inc(s["hid_lo"], 1)
            finish_dve(dve, s)

        UE = NHALF * KC
        at[0] = 0
        raw = [cut(EW + EB + ED) for _ in range(2)]
        score_wide = [cut(T) for _ in range(2)]
        m_gate = [cut(HALF) for _ in range(2)]
        m_glu = [cut(HALF) for _ in range(2)]
        m_up = [cut(HALF) for _ in range(2)]
        m_hid = [cut(HALF) for _ in range(2)]
        m_scaled = [cut(HALF) for _ in range(2)]
        m_bias = [cut(EB) for _ in range(2)]
        m_scores_t = cut(T)
        m_logits = cut(TB * (E + TOPK), TB, E + TOPK)
        m_top = cut(TB * 8, TB, 8)
        m_taken = cut(TB * 8, TB, 8)
        m_marked = cut(TB * (E + TOPK), TB, E + TOPK)
        m_exp = cut(TB * E, TB, E)
        m_chosen = cut(TB * E, TB, E)
        m_sum = cut(TB)
        m_scores = cut(TB * E, TB, E)
        at[0] = max(at[0], 16 * 1024)
        m_out = cut(KC * T, KC, T)
        MOE = NORM | dict.fromkeys("gate up clipped up_read glu product scaled hid_hi hid_lo down".split(), UE * E)
        MOE |= dict.fromkeys("logits centred exped scored scores_turned".split(), 1)
        MOE |= dict.fromkeys("raw_in0 raw_in1 wide_in0 wide_in1".split(), 16 * E // 2)
        MOE |= dict(scores_copied=NHALF, scores_out=16, w_hi=E, w_lo=E, out_copied=4, out_turned=4, x_done=4)

        def router_pe(pe, s):
            for b in range(TB):
                q = slice(b * P, (b + 1) * P)
                ins = three(pe, banks[4][:, b * E:(b + 1) * E], [lambda k: xt_hi[:, k, q], lambda k: xt_lo[:, k, q]],
                            [lambda k: router_w[0][:, k, :], lambda k: router_w[1][:, k, :]], range(KC))
            ins.then_inc(s["logits"], 1)
            pe.wait_ge(*s.after("scored", 1))
            for b in range(TB):
                ins = pe.transpose(banks[5 + b // 4][0:E, (b % 4) * P:(b % 4 + 1) * P], m_scores[:, b, :], ident[:])
            ins.then_inc(s["scores_turned"], 1)

        def router_dve(dve, s):
            dve.memset(m_taken, SENTINEL)
            link(dve, "dve", dve.memset(m_logits[:, :, E:E + TOPK], SENTINEL))
            dve.wait_ge(*s.after("logits", 1))
            link(dve, "dve", dve.tensor_tensor(m_logits[:, :, 0:E], banks[4][:, 0:TB * E].rearrange("p (b e) -> p b e", b=TB),
                                               bcast(router_b[:], 1, TB), ALU.add))
            for b in range(TB):
                ins = dve.max(m_top[:, b, :], m_logits[:, b, 0:E])
            link(dve, "dve", ins)
            dve.tensor_tensor(m_exp, m_logits[:, :, 0:E], bcast(m_top[:, :, 0], 2, E), ALU.subtract).then_inc(s["centred"], 1)
            link(dve, "dve", dve.tensor_copy(m_taken[:, :, 0:TOPK], m_top[:, :, 0:TOPK]))
            for b in range(TB):
                ins = dve.match_replace(out=m_marked[:, b, :], in_to_replace=m_taken[:, b, :], in_values=m_logits[:, b, :],
                                        imm_value=TAKEN)
            link(dve, "dve", ins)
            link(dve, "dve", dve.tensor_tensor(m_chosen, m_marked[:, :, 0:E], m_logits[:, :, 0:E], ALU.not_equal))
            dve.wait_ge(*s.after("exped", 1))
            link(dve, "dve", dve.tensor_tensor(m_chosen, m_chosen, m_exp, ALU.mult))
            link(dve, "dve", dve.reduce_sum(m_sum, m_chosen, axis=AX_X))
            link(dve, "dve", dve.reciprocal(m_sum, m_sum))
            dve.tensor_tensor(m_scores, m_chosen, bcast(m_sum, 2, E), ALU.mult).then_inc(s["scored"], 1)

        def router_act(act, s):
            act.wait_ge(*s.after("centred", 1))
            act.activation(m_exp, m_exp, ACT.Exp).then_inc(s["exped"], 1)
            act.wait_ge(*s.after("scores_turned", 1))
            for n in range(NHALF):
                act.activation(m_scores_t[0:E, n * HALF:(n + 1) * HALF], banks[5 + n][0:E, :], ACT.Copy)\
                   .then_inc(s["scores_copied"], 1)

        def experts(eng, body):
            for e in (0, 1):
                body(e, e % 2, False)
            with eng.Fori(2, E - 2, 2) as e:
                body(e, 0, False)
                body(e + 1, 1, False)
            for e in (E - 2, E - 1):
                body(e, e % 2, e == E - 1)

        def behind(eng, s, name, value):
            if not isinstance(value, int) or value > 0:
                eng.wait_ge(*s.after(name, value))

        def moe_sync(sp, s, call, waits):
            for w in waits:
                sp.wait_ge(*w)

            weights = a["moe_w"].rearrange("(pair par) p w -> par pair p w", par=2)
            rows = score_rows[call].rearrange("(pair par) t -> par pair t", par=2)

            def load(pair, par):
                behind(sp, s, "w_lo", 2 * pair + par - 1)
                sp.dma_start(raw[par], weights[par][pair]).then_inc(s[f"raw_in{par}"], 16)

            def widen(pair, par):
                behind(sp, s, "scaled", UE * (2 * pair + par - 1))
                sp.dma_start(score_wide[par], rows[par][pair].partition_broadcast(P)).then_inc(s[f"wide_in{par}"], 16)

            load(0, 0)
            load(0, 1)
            sp.wait_ge(*s.after("scores_copied", NHALF))
            sp.dma_start(score_rows[call], m_scores_t[0:E, :]).then_inc(s["scores_out"], 16)
            sp.wait_ge(*s.after("scores_out", 16))
            widen(0, 0)
            widen(0, 1)
            with sp.Fori(1, E // 2) as pair:
                for par in range(2):
                    load(pair, par)
                    widen(pair, par)

        def moe_pe(pe, s, waits):
            turn_pe(pe, s, xn)
            pe.wait_ge(*s.after("xt_lo", 4))
            router_pe(pe, s)

            def gate_up(e, par, u):
                n, q = u // KC, u % KC
                if u == 0:
                    pe.wait_ge(*s.after("w_lo", e + 1))
                for part, ready, read in ((0, "gate", "clipped"), (1, "up", "up_read")):
                    behind(pe, s, read, UE * e + u - 1)
                    o = part * D + q * P
                    three(pe, banks[2 * part + u % 2][:],
                          [lambda k: wr[par][0][:, k * 2 * D + o:k * 2 * D + o + P],
                           lambda k: wr[par][1][:, k * 2 * D + o:k * 2 * D + o + P]],
                          moving(n), range(KC)).then_inc(s[ready], 1)

            def down(e, par, u, last):
                n, q = u // KC, u % KC
                pe.wait_ge(*s.after("hid_lo", UE * e + u + 1))
                for c in range(KC):
                    o = EW + q * D + c * P
                    ins = three(pe, banks[4 + 2 * n + c][:],
                                [lambda k: wr[par][0][:, o:o + P], lambda k: wr[par][1][:, o:o + P]],
                                [lambda k: hid[u % 2][0][:], lambda k: hid[u % 2][1][:]], [0],
                                first=False, last=last and q == KC - 1)
                ins.then_inc(s["down"], 1)

            pe.wait_ge(*s.after("scores_copied", NHALF))
            for n in range(NHALF):
                for c in range(KC):
                    pe.matmul(banks[4 + 2 * n + c][:], down_b[:, c * P:(c + 1) * P],
                              m_scores_t[0:E, n * HALF:(n + 1) * HALF], start=True, stop=False, skip_group_check=True)
            gate_up(0, 0, 0)
            gate_up(0, 0, 1)

            def body(e, par, last):
                for u in range(UE):
                    if u < 2:
                        gate_up(e, par, u + 2)
                    elif not last:
                        gate_up(e + 1, 1 - par, u - 2)
                    down(e, par, u, last)

            experts(pe, body)
            finish_pe(pe, s, m_out)

        def split_hi(act, s, e, par):
            act.wait_ge(*s.after(f"raw_in{par}", 8 * (e - par) + 16))
            behind(act, s, "down", UE * (e - 1))
            act.activation(wr[par][0][:, 0:EW], raw[par][:, 0:EW], ACT.Copy)
            act.activation(wr[par][0][:, EW:], raw[par][:, EW + EB:], ACT.Copy).then_inc(s["w_hi"], 1)

        def split_lo(dve, s, e, par):
            dve.wait_ge(*s.after("w_hi", e + 1))
            behind(dve, s, "clipped", UE * (e - 1))
            dve.tensor_tensor(m_bias[par], raw[par][:, EW:EW + EB], bias_one[:], ALU.add)
            dve.tensor_tensor(wr[par][1][:, 0:EW], raw[par][:, 0:EW], wr[par][0][:, 0:EW].bitcast(F32), ALU.subtract)
            dve.tensor_tensor(wr[par][1][:, EW:], raw[par][:, EW + EB:], wr[par][0][:, EW:].bitcast(F32), ALU.subtract)\
               .then_inc(s["w_lo"], 1)

        def moe_act(act, s):
            turn_act(act, s)
            router_act(act, s)
            split_hi(act, s, 0, 0)

            def body(e, par, last):
                for u in range(UE):
                    g = UE * e + u
                    act.wait_ge(*s.after("clipped", g + 1))
                    behind(act, s, "product", g - 1)
                    act.activation(m_glu[u % 2], m_gate[u % 2], ACT.Gelu_apprx_sigmoid).then_inc(s["glu"], 1)
                    act.wait_ge(*s.after("scaled", g + 1))
                    behind(act, s, "down", g - 1)
                    act.activation(hid[u % 2][0][:], m_scaled[u % 2], ACT.Copy).then_inc(s["hid_hi"], 1)
                    if u == 0 and not last:
                        split_hi(act, s, e + 1, 1 - par)

            experts(act, body)
            finish_act(act, s, m_out, 0.5, lambda n: UE * (E - 1) + KC * (n + 1))

        def moe_dve(dve, s, waits):
            norm_dve(dve, s, x, xn, waits)
            turn_dve(dve, s)
            router_dve(dve, s)
            split_lo(dve, s, 0, 0)

            def body(e, par, last):
                for u in range(UE):
                    g = UE * e + u
                    n, q = u // KC, u % KC
                    dve.wait_ge(*s.after("gate", g + 1))
                    behind(dve, s, "glu", g - 1)
                    dve.tensor_scalar(m_gate[u % 2], banks[u % 2][:], m_bias[par][:, q:q + 1], ALPHA_LIMIT, ALU.add, ALU.min)\
                       .then_inc(s["clipped"], 1)
                    dve.wait_ge(*s.after("up", g + 1))
                    dve.tensor_scalar(m_up[u % 2], banks[2 + u % 2][:], m_bias[par][:, KC + q:KC + q + 1], ALPHA_LIMIT + 1.0,
                                      ALU.add, ALU.min).then_inc(s["up_read"], 1)
                    dve.wait_ge(*s.after("glu", g + 1))
                    dve.wait_ge(*s.after("up_read", g + 1))
                    behind(dve, s, "scaled", g - 1)
                    dve.scalar_tensor_tensor(m_hid[u % 2], m_up[u % 2], 1.0 - ALPHA_LIMIT, m_glu[u % 2], ALU.max, ALU.mult)\
                       .then_inc(s["product"], 1)
                    if u == 0 and not last:
                        split_lo(dve, s, e + 1, 1 - par)

            experts(dve, body)
            finish_dve(dve, s)

        def moe_pool(pool, s):
            norm_pool(pool, s)

            def body(e, par, last):
                pool.wait_ge(*s.after(f"wide_in{par}", 8 * (e - par) + 16))
                for u in range(UE):
                    g = UE * e + u
                    n = u // KC
                    pool.wait_ge(*s.after("product", g + 1))
                    behind(pool, s, "hid_hi", g - 1)
                    behind(pool, s, "hid_lo", g - 1)
                    pool.tensor_tensor(m_scaled[u % 2], m_hid[u % 2], score_wide[par][:, n * HALF:(n + 1) * HALF], ALU.mult)\
                        .then_inc(s["scaled"], 1)
                    pool.wait_ge(*s.after("hid_hi", g + 1))
                    behind(pool, s, "down", g - 1)
                    pool.tensor_tensor(hid[u % 2][1][:], m_scaled[u % 2], hid[u % 2][0][:].bitcast(F32), ALU.subtract)\
                        .then_inc(s["hid_lo"], 1)

            experts(pool, body)

        at[0] = 0
        qt = cut(GROUPS * T, GROUPS, T)
        kt = cut(GROUPS * T, GROUPS, T)
        qk_tok = [cut(2 * HEADS * STRIP, 2 * HEADS, STRIP) for _ in range(2)]
        v_tok = cut(TB * HEADS * STRIP, TB, HEADS, STRIP)
        shared = at[0]
        probs = [cut(GH * HALF, GH, HALF) for _ in range(2)]
        neg_max = cut(TB * P, TB, P)
        o_wide = cut(HALF)
        at[0] = shared
        qkv_raw = cut(KC * 3 * D, KC, 3 * D)
        wo_raw = cut(KC * D, KC, D)
        affine = [cut(HALF) for _ in range(2)]
        qk = cut(HALF)
        by_cos = cut(HALF)
        by_sin = cut(HALF)
        turned_qk = cut(HALF)
        centred = cut(HALF)
        squares = cut(HALF)
        w_qkv = [wr[0][k][:].rearrange("p (c n) -> p c n", c=KC) for k in range(2)]
        w_out = [wr[1][k][:, 0:KC * D].rearrange("p (c n) -> p c n", c=KC) for k in range(2)]
        MAX_UNITS = [(b, c, c * HALF, min(HALF, (b + 1) * P - c * HALF)) for b in range(TB) for c in range(b // 4 + 1)]
        EXP_UNITS = [(n, k, max(n * HALF, k * P), (n + 1) * HALF - max(n * HALF, k * P))
                     for n in range(NHALF) for k in range(4 * (n + 1))]
        NU = len(MAX_UNITS)
        assert NU == len(EXP_UNITS)
        ATTN1 = dict.fromkeys([*NORM, *("w_in w_hi w_lo zeroed table projected parts_free parts tok qk_turned qk_copied proj scores "
                                        "maxed negated neg_turned shifted e_scores exped weighted o_copied o_turned o_done "
                                        "x_done").split()])
        ATTN0 = dict.fromkeys([*ATTN1, *("var2 rstd2 var3 squared rstd3 scaled bias_added normed2 turned2 a_hi a_lo wo_done "
                                         "tb_in").split()])

        def attn_load(sp, s, kind, waits):
            for w in waits:
                sp.wait_ge(*w)
            k = kind
            loads = [(qkv_raw, a[k + "_wqkv"].rearrange("(c p) n -> p c n", p=P)),
                     (qkv_b[:], a[k + "_bqkv"].partition_broadcast(P)),
                     (cosine[:], a[k + "_cos"].rearrange("(b p) f -> p b f", p=P)),
                     (sine[:], a[k + "_sin"].rearrange("(b p) f -> p b f", p=P))]
            if kind == "attn0":
                loads += [(wo_raw, a["wo"].rearrange("(c p) n -> p c n", p=P)), (out_b[:], a["bo"].partition_broadcast(P)),
                          (head_g[:], a["head_g"].partition_broadcast(P)), (head_b[:], a["head_b"].partition_broadcast(P)),
                          (in_gb[:], a["in_gb"])]
            for dst, src in loads:
                sp.dma_start(dst, src).then_inc(s["w_in"], 16)

        def loaded(kind):
            return 16 * (9 if kind == "attn0" else 4)

        def attn_pool(pool, s, kind, waits):
            norm_pool(pool, s)
            for w in waits:
                pool.wait_ge(*w)
            for i in range(2):
                pool.memset(qk_tok[i][:, :, HD:STRIP], 0.0).then_inc(s["zeroed"], 1)
            pool.wait_ge(*s.after("zeroed", 2))
            for i in range(2):
                pool.memset(qk_tok[i][:, HEADS:2 * HEADS, HD:HD + 1], 1.0).then_inc(s["zeroed"], 1)
            pool.memset(v_tok[:, :, :, HD:STRIP], 0.0).then_inc(s["zeroed"], 1)
            pool.wait_ge(*s.after("zeroed", 5))
            pool.memset(v_tok[:, :, :, HD:HD + 1], 1.0).then_inc(s["zeroed"], 1)
            if kind == "attn0":
                pool.wait_ge(*s.after("var2", 1))
                link(pool, "pool", pool.tensor_tensor(rstd[:], vareps[:], half_neg[:, 0:TB], ALU.pow))
                pool.tensor_tensor(xnorm[:], xnorm[:], half_pos[:, 0:TB], ALU.pow).then_inc(s["rstd2"], 1)
                pool.wait_ge(*s.after("w_in", loaded(kind)))
                pool.wait_ge(*s.after("normed", TB))
                pool.tensor_tensor(x[:], x[:], bcast(out_b[:], 1, TB), ALU.add).then_inc(s["bias_added"], 1)
            for b in range(TB):
                pool.wait_ge(*s.after("table", 1))
                pool.wait_ge(*s.after("projected", b + 1))
                if kind == "attn0":
                    v = "p (h f two) -> p h f two"
                    shape = [P, 2 * HEADS, HD // 2, 2]
                    wide = lambda t: t[:, b, :].unsqueeze(1).unsqueeze(3).broadcast_to(shape)
                    kw = dict(f=HD // 2, two=2)
                else:
                    v = "p (h two f) -> p h two f"
                    shape = [P, 2 * HEADS, 2, HD // 2]
                    wide = lambda t: t[:, b, :].unsqueeze(1).unsqueeze(1).broadcast_to(shape)
                    kw = dict(f=HD // 2, two=2)
                if b >= 1:
                    pool.wait_ge(*s.after("parts_free", b))
                pool.tensor_tensor(by_cos.rearrange(v, **kw), qk.rearrange(v, **kw), wide(cosine), ALU.mult)
                pool.tensor_tensor(by_sin.rearrange(v, **kw), qk.rearrange(v, **kw), wide(sine), ALU.mult).then_inc(s["parts"], 1)
                if kind == "attn0":
                    pool.wait_ge(*s.after("var3", b + 1))
                    pool.tensor_tensor(head_rstd[:], head_var[:], half_neg[:], ALU.pow).then_inc(s["rstd3"], 1)
                    pool.wait_ge(*s.after("scaled", 2 * b + 1))
                    hv = squares.rearrange("p (h d) -> p h d", d=HD)
                    pool.tensor_tensor(hv, hv, bcast(head_g[:], 1, 2 * HEADS), ALU.mult).then_inc(s["scaled"], 1)

        def attn_act(act, s, kind):
            act.wait_ge(*s.after("w_in", loaded(kind)))
            act.activation(w_qkv[0], qkv_raw, ACT.Copy).then_inc(s["w_hi"], 1)
            if kind == "attn0":
                act.activation(w_out[0], wo_raw, ACT.Copy).then_inc(s["w_hi"], 1)
                for i in range(4):
                    n, c = i // KC, i % KC
                    act.wait_ge(*s.after("turned", i + 1))
                    for t in range(2):
                        if i >= 1:
                            act.wait_ge(*s.after("xt_lo", 2 * (i - 1) + t + 1))
                        link(act, "act", act.activation(affine[t], banks[i][:], ACT.Identity, scale=in_gb[:, 2 * t, c:c + 1],
                                                        bias=in_gb[:, 2 * t + 1, c:c + 1]))
                        if n == 1:
                            act.wait_ge(*s.after("proj", TB // 2))
                        act.activation(xt_hi[:, c, t * HALF:(t + 1) * HALF], affine[t], ACT.Copy).then_inc(s["xt_hi"], 1)
                    if i == 1:
                        for b in range(TB // 2 - 1):
                            square(act, s, b)
                            copy_qk(act, s, b)
                        square(act, s, TB // 2 - 1)
                for b in range(TB // 2 - 1, TB):
                    if b >= TB // 2:
                        square(act, s, b)
                    copy_qk(act, s, b)
            else:
                turn_act(act, s)
                for b in range(TB):
                    copy_qk(act, s, b)
            for g in range(GROUPS + 1):
                for u in range(NU):
                    if g >= 1:
                        n, k, q0, w = EXP_UNITS[u]
                        for j in range(GH):
                            job = ((g - 1) * NU + u) * GH + j
                            act.wait_ge(*s.after("e_scores", job + 1))
                            if j == 0 and (g - 1) * NU + u >= 2:
                                act.wait_ge(*s.after("weighted", (g - 1) * NU + u - 1))
                            act.activation(probs[u % 2][:, j, 0:w], banks[3 + job % 3][:, 0:w], ACT.Exp, scale=HD ** -0.5)\
                               .then_inc(s["exped"], 1)
                    for gd, n in ([(g - 1, 0)] if u == 4 and g >= 1 else []) + ([(g - 2, 1)] if u == 0 and g >= 2 else []):
                        o_copy(act, s, gd, n)
            o_copy(act, s, GROUPS - 1, 1)
            if kind == "attn0":
                for i in range(4):
                    n, c = i // KC, i % KC
                    act.wait_ge(*s.after("turned2", i + 1))
                    act.activation(xt_hi[:, c, n * HALF:(n + 1) * HALF], banks[i][:], ACT.Copy).then_inc(s["a_hi"], 1)

        def o_copy(act, s, g, n):
            act.wait_ge(*s.after("weighted", g * NU + (4 if n == 0 else NU)))
            if g or n:
                act.wait_ge(*s.after("o_turned", 2 * g + n))
            act.activation(o_wide, banks[6][:], ACT.Copy).then_inc(s["o_copied"], 1)

        def square(act, s, b):
            act.wait_ge(*s.after("tb_in", b + 1))
            act.activation(squares, centred, ACT.Square).then_inc(s["squared"], 1)

        def copy_qk(act, s, b):
            act.wait_ge(*s.after("qk_turned", b + 1))
            cols = slice(b * P, (b + 1) * P)
            act.activation(qt[:, :, cols], banks[0][:].rearrange("p (g t) -> p g t", g=GROUPS), ACT.Copy)
            act.activation(kt[:, :, cols], banks[1][:].rearrange("p (g t) -> p g t", g=GROUPS), ACT.Copy).then_inc(s["qk_copied"], 1)

        def attn_dve(dve, s, kind, waits):
            norm_dve(dve, s, x, xn, waits)
            if kind == "attn0":
                dve.wait_ge(*s.after("normed", TB))
                for b in range(TB):
                    ins = dve.bn_stats(stats[:, b, :], xn[:, b, :])
                link(dve, "dve", ins)
                for b in range(TB):
                    ins = dve.bn_aggr(meanvar[:, b, :], stats[:, b, :])
                link(dve, "dve", ins)
                link(dve, "dve", dve.tensor_tensor(xnorm[:], meanvar[:, :, 0], meanvar[:, :, 0], ALU.mult))
                link(dve, "dve", dve.tensor_tensor(xnorm[:], xnorm[:], meanvar[:, :, 1], ALU.add))
                dve.tensor_scalar(xnorm[:], xnorm[:], D * HD ** -0.5, None, ALU.mult)
                dve.tensor_scalar(vareps[:], meanvar[:, :, 1], EPS, None, ALU.add).then_inc(s["var2"], 1)
                dve.wait_ge(*s.after("rstd2", 1))
                for b in range(TB):
                    dve.tensor_scalar(xn[:, b, :], xn[:, b, :], meanvar[:, b, 0:1], rstd[:, b:b + 1],
                                      ALU.subtract, ALU.mult).then_inc(s["normed2"], 1)
                dve.wait_ge(*s.after("w_in", loaded(kind)))
                dve.tensor_tensor(cosine[:], cosine[:], bcast(xnorm[:], 2, HD // 2), ALU.mult)
                dve.tensor_tensor(sine[:], sine[:], bcast(xnorm[:], 2, HD // 2), ALU.mult).then_inc(s["table"], 1)
            else:
                dve.wait_ge(*s.after("w_in", loaded(kind)))
                dve.memset(xnorm[:], 1.0).then_inc(s["table"], 1)
            dve.wait_ge(*s.after("w_hi", 1))
            dve.tensor_tensor(w_qkv[1], qkv_raw, w_qkv[0].bitcast(F32), ALU.subtract).then_inc(s["w_lo"], 1)
            if kind == "attn0":
                dve.wait_ge(*s.after("w_hi", 2))
                dve.tensor_tensor(w_out[1], wo_raw, w_out[0].bitcast(F32), ALU.subtract).then_inc(s["w_lo"], 1)
                for i in range(4):
                    n, c = i // KC, i % KC
                    for t in range(2):
                        dve.wait_ge(*s.after("xt_hi", 2 * i + t + 1))
                        q = slice(t * HALF, (t + 1) * HALF)
                        dve.tensor_tensor(xt_lo[:, c, q], affine[t], xt_hi[:, c, q].bitcast(F32), ALU.subtract)\
                           .then_inc(s["xt_lo"], 1)
                    if i == 1:
                        for b in range(TB // 2):
                            tok_dve(dve, s, kind, b)
                for b in range(TB // 2, TB):
                    tok_dve(dve, s, kind, b)
            else:
                turn_dve(dve, s)
                for b in range(TB):
                    tok_dve(dve, s, kind, b)
            dve.wait_ge(*s.after("qk_copied", TB))
            link(dve, "dve", dve.memset(row_max[:, :, :, 1], SENTINEL))
            link(dve, "dve", dve.memset(neg_max, 0.0))
            for g in range(GROUPS + 1):
                for u in range(NU):
                    if g < GROUPS:
                        b, c, k0, w = MAX_UNITS[u]
                        for j in range(GH):
                            job = (g * NU + u) * GH + j
                            dve.wait_ge(*s.after("scores", job + 1))
                            dve.reduce_max(row_max[:, b, GH * g + j, c:c + 1], banks[job % 3][:, 0:w], axis=AX_X)\
                               .then_inc(s["maxed"], 1)
                    if u == 0 and g >= 1:
                        shift(dve, s, g - 1)
                    for gd, n in ([(g - 1, 0)] if u == 6 and g >= 1 else []) + ([(g - 2, 1)] if u == 2 and g >= 2 else []):
                        normalise(dve, s, gd, n)
                if g < GROUPS:
                    if g >= 1:
                        dve.wait_ge(*s.after("neg_turned", 2 * g))
                    dve.wait_ge(*s.after("maxed", (g + 1) * NU * GH))
                    hs = slice(GH * g, GH * (g + 1))
                    link(dve, "dve", dve.tensor_tensor(group_max[:], row_max[:, :, hs, 0], row_max[:, :, hs, 1], ALU.max))
                    dve.tensor_scalar(neg_max[:, :, HD::STRIP], group_max[:], -1.0, None, ALU.mult).then_inc(s["negated"], 1)
            normalise(dve, s, GROUPS - 1, 1)
            if kind == "attn0":
                for i in range(4):
                    n, c = i // KC, i % KC
                    dve.wait_ge(*s.after("a_hi", i + 1))
                    q = slice(n * HALF, (n + 1) * HALF)
                    dve.tensor_tensor(xt_lo[:, c, q], banks[i][:], xt_hi[:, c, q].bitcast(F32), ALU.subtract).then_inc(s["a_lo"], 1)
                dve.wait_ge(*s.after("bias_added", 1))
                for i in range(4):
                    dve.wait_ge(*s.after("wo_done", i + 1))
                    v = x[:, 2 * i:2 * i + 2, :].rearrange("p b d -> p (b d)")
                    dve.tensor_tensor(v, banks[4 + i][:], v, ALU.add).then_inc(s["x_done"], 1)
            else:
                dve.wait_ge(*s.after("o_done", 2 * GROUPS))
                for i in range(4):
                    v = slice(2 * i, 2 * i + 2)
                    dve.tensor_tensor(x[:, v, :], x[:, v, :], xn[:, v, :], ALU.add).then_inc(s["x_done"], 1)

        def shift(dve, s, g):
            for n in range(NHALF):
                dve.wait_ge(*s.after("neg_turned", 2 * g + n + 1))
                q = slice(n * HALF, (n + 1) * HALF)
                dve.tensor_tensor(qt[:, g, q], banks[7][:], qt[:, g, q], ALU.add).then_inc(s["shifted"], 1)

        def normalise(dve, s, g, n):
            dve.wait_ge(*s.after("o_turned", 2 * g + n + 1))
            o = banks[7][:].rearrange("p (b j d) -> p b j d", b=4, j=GH)
            link(dve, "dve", dve.reciprocal(inv_den[:], o[:, :, :, HD]))
            dst = xn[:, 4 * n:4 * n + 4, GH * HD * g:GH * HD * (g + 1)].rearrange("p b (j d) -> p b j d", j=GH)
            dve.tensor_tensor(dst, o[:, :, :, 0:HD], bcast(inv_den[:], 3, HD), ALU.mult).then_inc(s["o_done"], 1)

        def tok_dve(dve, s, kind, b):
            par = b % 2
            tok = qk_tok[par][:, :, 0:HD]
            dve.wait_ge(*s.after("proj", b + 1))
            if b >= 1:
                dve.wait_ge(*s.after("parts", b))
            bank_q, bank_kv = banks[4 + 2 * par], banks[5 + 2 * par]
            dve.tensor_tensor(qk[:, 0:D], bank_q[:, 0:D], qkv_b[:, 0:D], ALU.add)
            dve.tensor_tensor(qk[:, D:2 * D], bank_kv[:, 0:D], qkv_b[:, D:2 * D], ALU.add)
            hv = "p (h d) -> p h d"
            dve.tensor_tensor(v_tok[:, b, :, 0:HD], bank_kv[:, D:2 * D].rearrange(hv, d=HD), qkv_b[:, 2 * D:3 * D].rearrange(hv, d=HD),
                              ALU.add).then_inc(s["projected"], 1)
            dve.wait_ge(*s.after("parts", b + 1))
            dve.wait_ge(*s.after("zeroed", 6))
            if b >= 2:
                dve.wait_ge(*s.after("qk_turned", b - 1))
            if kind == "attn0":
                dst = turned_qk.rearrange("p (h f two) -> p h f two", f=HD // 2, two=2)
                c, sn = (t.rearrange("p (h f two) -> p h f two", f=HD // 2, two=2) for t in (by_cos, by_sin))
                first, second = (lambda t: t[:, :, :, 0]), (lambda t: t[:, :, :, 1])
            else:
                dst = tok.rearrange("p h (two f) -> p h two f", two=2)
                c, sn = (t.rearrange("p (h two f) -> p h two f", f=HD // 2, two=2) for t in (by_cos, by_sin))
                first, second = (lambda t: t[:, :, 0, :]), (lambda t: t[:, :, 1, :])
            last_to = "parts_free"
            dve.tensor_tensor(first(dst), first(c), second(sn), ALU.subtract).then_inc(chain_sem["dve"], 1)
            chained["dve"] += 1
            dve.tensor_tensor(second(dst), first(sn), second(c), ALU.add).then_inc(s[last_to], 1)
            if kind != "attn0":
                dve.wait_ge(*s.after("parts_free", b + 1))
                dve.wait_ge(chain_sem["dve"], chained["dve"])
                dve.memset(xnorm[:], 1.0).then_inc(s["tok"], 1)
                return
            dve.wait_ge(*s.after("parts_free", b + 1))
            dve.wait_ge(chain_sem["dve"], chained["dve"])
            r, cen, sq = (t.rearrange(hv, d=HD) for t in (turned_qk, centred, squares))
            link(dve, "dve", dve.reduce_sum(head_sum[:], r, axis=AX_X))
            dve.scalar_tensor_tensor(cen, bcast(head_sum[:], 2, HD), -1.0 / HD, r, ALU.mult, ALU.add).then_inc(s["tb_in"], 1)
            dve.wait_ge(*s.after("squared", b + 1))
            link(dve, "dve", dve.reduce_sum(head_var[:], sq, axis=AX_X))
            dve.tensor_scalar(head_var[:], head_var[:], 1.0 / HD, EPS, ALU.mult, ALU.add).then_inc(s["var3"], 1)
            dve.wait_ge(*s.after("rstd3", b + 1))
            dve.tensor_tensor(sq, cen, bcast(head_rstd[:], 2, HD), ALU.mult).then_inc(s["scaled"], 1)
            dve.wait_ge(*s.after("scaled", 2 * b + 2))
            dve.tensor_tensor(tok, sq, bcast(head_b[:], 1, 2 * HEADS), ALU.add).then_inc(s["tok"], 1)

        def attn_pe(pe, s, kind, waits):
            for w in waits:
                pe.wait_ge(*w)
            if kind == "attn0":
                for i in range(4):
                    n, c = i // KC, i % KC
                    pe.wait_ge(*s.after("normed2", 4 * (n + 1)))
                    for b in range(4):
                        ins = pe.transpose(banks[i][:, b * P:(b + 1) * P], xn[:, 4 * n + b, c * P:(c + 1) * P], ident[:])
                    ins.then_inc(s["turned"], 1)
            else:
                turn_pe(pe, s, xn)

            def project(b):
                par = b % 2
                if kind == "attn0":
                    pe.wait_ge(*s.after("xt_lo", 4 * (b // 4 + 1)))
                    q0, kv0 = (b % 4) * P, HALF + (b % 4) * P
                else:
                    pe.wait_ge(*s.after("xt_lo", 2 * (b // 4 + 1)))
                    q0 = kv0 = b * P
                pe.wait_ge(*s.after("w_lo", 1))
                if b >= 2:
                    pe.wait_ge(*s.after("projected", b - 1))
                three(pe, banks[4 + 2 * par][:, 0:D], [lambda k: xt_hi[:, k, q0:q0 + P], lambda k: xt_lo[:, k, q0:q0 + P]],
                      [lambda k: w_qkv[0][:, k, 0:D], lambda k: w_qkv[1][:, k, 0:D]], range(KC))
                three(pe, banks[5 + 2 * par][:], [lambda k: xt_hi[:, k, kv0:kv0 + P], lambda k: xt_lo[:, k, kv0:kv0 + P]],
                      [lambda k: w_qkv[0][:, k, D:3 * D], lambda k: w_qkv[1][:, k, D:3 * D]], range(KC)).then_inc(s["proj"], 1)

            def turn_qk(b):
                pe.wait_ge(*s.after("tok", b + 1))
                if b == 0:
                    pe.wait_ge(*s.after("xt_hi", 4))
                    pe.wait_ge(*s.after("xt_lo", 4))
                if b >= 1:
                    pe.wait_ge(*s.after("qk_copied", b))
                for side in range(2):
                    for g in range(GROUPS):
                        h = side * HEADS + g * GH
                        ins = pe.transpose(banks[side][:, g * P:(g + 1) * P],
                                           qk_tok[b % 2][:, h:h + GH, :].rearrange("p h d -> p (h d)"), ident[:])
                ins.then_inc(s["qk_turned"], 1)

            LAG = 1
            for b in range(TB + LAG):
                if b < TB:
                    project(b)
                if b >= LAG:
                    turn_qk(b - LAG)
            pe.wait_ge(*s.after("qk_copied", TB))

            def strip(t, j, g, cols):
                return t[j * STRIP:(j + 1) * STRIP, g, cols]

            def max_scores(g, u):
                b, c, k0, w = MAX_UNITS[u]
                for j in range(GH):
                    job = (g * NU + u) * GH + j
                    if job >= 3:
                        pe.wait_ge(*s.after("maxed", job - 2))
                    diagonal = k0 + w == (b + 1) * P
                    ins = pe.matmul(banks[job % 3][:, 0:w], strip(qt, j, g, slice(b * P, (b + 1) * P)), strip(kt, j, g, slice(k0, k0 + w)),
                                    start=True, stop=not diagonal, tile_position=(j * STRIP, 0))
                    if diagonal:
                        ins = pe.matmul(banks[job % 3][:, w - P:w], ident_b[:], mask_qk[:], start=False, stop=True)
                    ins.then_inc(s["scores"], 1)

            def exp_scores(g, u):
                n, k, q0, w = EXP_UNITS[u]
                for j in range(GH):
                    job = (g * NU + u) * GH + j
                    if job >= 3:
                        pe.wait_ge(*s.after("exped", job - 2))
                    diagonal = q0 == k * P
                    ins = pe.matmul(banks[3 + job % 3][:, 0:w], strip(kt, j, g, slice(k * P, (k + 1) * P)), strip(qt, j, g, slice(q0, q0 + w)),
                                    start=True, stop=not diagonal, tile_position=(j * STRIP, 0))
                    if diagonal:
                        ins = pe.matmul(banks[3 + job % 3][:, 0:P], ident_b[:], mask_kq[:], start=False, stop=True)
                    ins.then_inc(s["e_scores"], 1)

            def weigh(g, u):
                n, k, q0, w = EXP_UNITS[u]
                unit = g * NU + u
                if k == 0 and (g or n):
                    pe.wait_ge(*s.after("o_copied", 2 * g + n))
                for j in range(GH):
                    pe.wait_ge(*s.after("exped", unit * GH + j + 1))
                    ins = pe.matmul(banks[6][j * STRIP:(j + 1) * STRIP, q0 - n * HALF:HALF], v_tok[:, k, GH * g + j, :],
                                    probs[u % 2][:, j, 0:w], start=k == 0, stop=k == 4 * n + 3, tile_position=(0, j * STRIP),
                                    skip_group_check=True)
                ins.then_inc(s["weighted"], 1)

            def turn_max(g):
                pe.wait_ge(*s.after("negated", g + 1))
                for n in range(NHALF):
                    if n or g:
                        pe.wait_ge(*s.after("shifted", 2 * g + n))
                    if g >= 1 and n == 0:
                        pe.wait_ge(*s.after("o_done", 2 * g - 1))
                    for b in range(4):
                        ins = pe.transpose(banks[7][:, b * P:(b + 1) * P], neg_max[:, 4 * n + b, :], ident[:])
                    ins.then_inc(s["neg_turned"], 1)

            def turn_o(g, n):
                pe.wait_ge(*s.after("o_copied", 2 * g + n + 1))
                pe.wait_ge(*s.after("shifted", 2 * min(GROUPS, g + 1 + n)))
                if g or n:
                    pe.wait_ge(*s.after("o_done", 2 * g + n))
                for b in range(4):
                    ins = pe.transpose(banks[7][:, b * P:(b + 1) * P], o_wide[:, b * P:(b + 1) * P], ident[:])
                ins.then_inc(s["o_turned"], 1)

            for g in range(GROUPS + 1):
                for u in range(NU):
                    if g < GROUPS:
                        max_scores(g, u)
                    if g >= 1:
                        if u == 0:
                            turn_max(g - 1)
                            pe.wait_ge(*s.after("shifted", 2 * g))
                        exp_scores(g - 1, u)
                        if u >= 1:
                            weigh(g - 1, u - 1)
                        elif g >= 2:
                            weigh(g - 2, NU - 1)
                        if u == 6:
                            turn_o(g - 1, 0)
                        if u == 2 and g >= 2:
                            turn_o(g - 2, 1)
            weigh(GROUPS - 1, NU - 1)
            turn_o(GROUPS - 1, 1)
            if kind == "attn0":
                pe.wait_ge(*s.after("o_done", 2 * GROUPS))
                for i in range(4):
                    n, c = i // KC, i % KC
                    for b in range(4):
                        ins = pe.transpose(banks[i][:, b * P:(b + 1) * P], xn[:, 4 * n + b, c * P:(c + 1) * P], ident[:])
                    ins.then_inc(s["turned2"], 1)
                for b in range(TB):
                    pe.wait_ge(*s.after("a_lo", 2 * (b // 4 + 1)))
                    pe.wait_ge(*s.after("w_lo", 2))
                    q = slice(b * P, (b + 1) * P)
                    ins = three(pe, banks[4 + b // 2][:, (b % 2) * D:(b % 2 + 1) * D],
                                [lambda k: xt_hi[:, k, q], lambda k: xt_lo[:, k, q]],
                                [lambda k: w_out[0][:, k, :], lambda k: w_out[1][:, k, :]], range(KC))
                    if b % 2:
                        ins.then_inc(s["wo_done"], 1)

        totals = {"ffn": FFN, "moe": MOE, "attn0": ATTN0, "attn1": ATTN1}
        plan, run = [], {}
        for kind in stages:
            run[kind] = Sems(kind, totals[kind], run.get(kind))
            plan.append((kind, run[kind]))
        x_ready = [[(x_loaded, 16), (pool_consts, 4)]] + [[s.after("x_done", 4)] for _, s in plan]
        before = [[(w_lo, 9), (w_hi, 4)]] + x_ready[1:]
        stored = sem("stored")

        block = ctx.enter_context(nc.Block())

        @block.sync
        def _(sp):
            load_sync(sp)
            for i, (kind, s) in enumerate(plan):
                if kind == "moe":
                    moe_sync(sp, s, i % 2, before[i])
                if kind[:4] == "attn":
                    attn_load(sp, s, kind, before[i])
            for w in x_ready[-1]:
                sp.wait_ge(*w)
            sp.dma_start(out.rearrange("(b p) d -> p b d", p=P), x[:]).then_inc(stored, 16)
            sp.wait_ge(stored, 16)

        @block.scalar
        def _(act):
            load_act(act)
            prep_act(act)
            for i, (kind, s) in enumerate(plan):
                if kind == "ffn":
                    ffn_act(act, s)
                if kind == "moe":
                    moe_act(act, s)
                if kind[:4] == "attn":
                    attn_act(act, s, kind)

        @block.gpsimd
        def _(pool):
            prep_pool(pool)
            for i, (kind, s) in enumerate(plan):
                if kind == "ffn":
                    norm_pool(pool, s)
                if kind == "moe":
                    moe_pool(pool, s)
                if kind[:4] == "attn":
                    attn_pool(pool, s, kind, before[i])

        @block.vector
        def _(dve):
            prep_dve(dve)
            for i, (kind, s) in enumerate(plan):
                if kind == "ffn":
                    ffn_dve(dve, s, x_ready[i])
                if kind == "moe":
                    moe_dve(dve, s, x_ready[i])
                if kind[:4] == "attn":
                    attn_dve(dve, s, kind, x_ready[i])

        @block.tensor
        def _(pe):
            prep_pe(pe)
            for i, (kind, s) in enumerate(plan):
                if kind == "ffn":
                    ffn_pe(pe, s, before[i])
                if kind == "moe":
                    moe_pe(pe, s, before[i])
                if kind[:4] == "attn":
                    attn_pe(pe, s, kind, before[i])


def causal_masks():
    q = np.arange(P)
    m = np.where(q[None, :] > q[:, None], np.float32(MASKED), np.float32(0.0)).astype(np.float32)
    return m, np.ascontiguousarray(m.T)


def rotations(freqs):
    angle = np.arange(T, dtype=np.float32)[:, None] * freqs.astype(np.float32)[None, :]
    return np.cos(angle).astype(np.float32), np.sin(angle).astype(np.float32)


def expert_rows(i):
    g = i["L1_ffn_gate_up_proj"].reshape(E, KC, P, D, 2).transpose(0, 2, 1, 4, 3).reshape(E, P, EW)
    b = i["L1_ffn_gate_up_proj_bias"].reshape(E, KC, P, 2).transpose(0, 2, 3, 1).reshape(E, P, EB)
    d = i["L1_ffn_down_proj"].reshape(E, KC, P, D).transpose(0, 2, 1, 3).reshape(E, P, ED)
    return np.concatenate([g, b, d], axis=2)


def hadamard():
    h = np.ones((1, 1), np.float32)
    while h.shape[0] < P:
        h = np.block([[h, h], [h, -h]])
    return np.ascontiguousarray(h, dtype=np.float32)


STAGES = ('ffn', 'attn0', 'ffn', 'moe', 'attn1', 'moe')


def kernel(**inputs):
    import concourse.bacc as bacc
    from concourse.bass_utils import run_bass_kernel_spmd as run

    i = {k: np.asarray(v) for k, v in inputs.items()}
    mask_qk, mask_kq = causal_masks()
    steps = np.arange(0, HD, 2, dtype=np.float32) / np.float32(HD)
    cos0, sin0 = rotations(steps * np.log(np.float32(30000.0)))
    cos1, sin1 = rotations(np.float32(1.0) / np.float32(10000.0) ** steps)
    arrays = {
        "x": i["L0_attn_x"][0], "w1t": i["L0_ffn_W1"].T, "w3t": i["L0_ffn_W3"].T, "w2t": i["L0_ffn_W2"].T,
        "ident": np.eye(P, dtype=np.float32), "hadamard": hadamard(), "mask_qk": mask_qk, "mask_kq": mask_kq,
        "router_t": i["L1_ffn_router_weight"].T, "router_b": i["L1_ffn_router_bias"], "down_b": i["L1_ffn_down_proj_bias"],
        "moe_w": expert_rows(i),
        "attn0_wqkv": np.concatenate([i["L0_attn_Wq"], i["L0_attn_Wkv"]], axis=1),
        "attn0_bqkv": np.concatenate([i["L0_attn_bq"], i["L0_attn_bkv"]]),
        "attn1_wqkv": i["L1_attn_w_qkv"].reshape(HEADS, 3, HD, D).transpose(3, 1, 0, 2).reshape(D, 3 * D),
        "attn1_bqkv": i["L1_attn_b_qkv"].reshape(HEADS, 3, HD).transpose(1, 0, 2).reshape(3 * D),
        "wo": i["L0_attn_Wo"], "bo": i["L0_attn_bo"], "head_g": i["L0_attn_ln_g"], "head_b": i["L0_attn_ln_b"],
        "in_gb": np.stack([i["L0_attn_" + k].reshape(KC, P).T for k in ("qn_g", "qn_b", "kvn_g", "kvn_b")], axis=1),
        "attn0_cos": cos0, "attn0_sin": sin0, "attn1_cos": cos1, "attn1_sin": sin1,
    }
    arrays = {k: np.ascontiguousarray(v) for k, v in arrays.items()}
    nc = bacc.Bacc("TRN2", target_bir_lowering=False, num_devices=1)
    aps = {k: nc.dram_tensor("in_" + k, v.shape, F32, kind="ExternalInput").ap() for k, v in arrays.items()}
    out = nc.dram_tensor("out", (T, D), F32, kind="ExternalOutput").ap()
    build(nc, aps, out, STAGES)
    r = run(nc, [{"in_" + k: v for k, v in arrays.items()}], core_ids=[0])
    return r.results[0]["out"].reshape(1, T, D)
```

```python
import math
from contextlib import ExitStack

import numpy as np

import concourse.bass as bass
from concourse import mybir

F32 = mybir.dt.float32
F32R = mybir.dt.float32r
BF16 = mybir.dt.bfloat16
ALU = mybir.AluOpType
ACT = mybir.ActivationFunctionType
AX_X = mybir.AxisListType.X

P = 128
D = 256
KC = D // P
T = 1024
TB = T // P
HALF = 512
NHALF = T // HALF
FF = 1024
FB = FF // P
HEADS = 16
HD = D // HEADS
STRIP = 32
GH = P // STRIP
GROUPS = HEADS // GH
ARENA = 21 * 1024 + 416
PARTS = 6 * HD
SHIFT = 3
E = 16
TOPK = 4
EW = 2 * KC * 2 * P
ED = KC * D
EB = 2 * KC
ALPHA_LIMIT = 7.0
EPS = 1e-5
MASKED = -1.0e30
SENTINEL = -3.0e38
TAKEN = -3.3e38


def bcast(ap, axis, n):
    wide = ap.unsqueeze(axis)
    shape = list(wide.shape)
    shape[axis] = n
    return wide.broadcast_to(shape)


def build(nc, a, out, stages):
    ctx = ExitStack()
    with ctx:
        def sb(name, shape, dt=F32):
            return ctx.enter_context(nc.sbuf_tensor(name, shape, dt))

        def sem(name):
            return ctx.enter_context(nc.semaphore(name))

        all_banks = ctx.enter_context(nc.psum_tensor("all_banks", [P, 8, 512], F32))
        banks = [all_banks[:, i, :] for i in range(8)]
        pairs = [all_banks[:, 2 + 2 * i:4 + 2 * i, :] for i in range(2)]
        score_rows = nc.dram_tensor("score_rows", (2, E, T), F32, kind="Internal").ap()

        x = sb("x", [P, TB, D])
        xn = sb("xn", [P, TB, D])
        with ExitStack() as before_scores:
            xt_hi, xt_lo = (before_scores.enter_context(nc.sbuf_tensor(f"xt_{k}", [P, KC, T], F32R)) for k in ("hi", "lo"))
        stacked_xt = sb("stacked_xt", [P, 2 * GH * T], BF16)
        w1 = [sb(f"w1_{k}", [P, KC, FF], F32R) for k in ("hi", "lo")]
        w3 = [sb(f"w3_{k}", [P, KC, FF], F32R) for k in ("hi", "lo")]
        w2 = [sb(f"w2_{k}", [P, FB, D], F32R) for k in ("hi", "lo")]
        wr = [[sb(f"wr{i}_{k}", [P, EW + ED], F32R) for k in ("hi", "lo")] for i in range(2)]
        hid = [[sb(f"hid{i}_{k}", [P, HALF], F32R) for k in ("hi", "lo")] for i in range(2)]
        ident = sb("ident", [P, P])
        ident_b = sb("ident_b", [P, P], BF16)
        had_r = sb("had_r", [P, P], F32R)
        mask_qk = sb("mask_qk", [P, P], BF16)
        mask_kq = sb("mask_kq", [P, P], BF16)
        half_neg = sb("half_neg", [P, 32])
        half_pos = sb("half_pos", [P, 32])
        stats = sb("stats", [P, TB, 6])
        meanvar = sb("meanvar", [P, TB, 2])
        vareps = sb("vareps", [P, TB])
        rstd = sb("rstd", [P, TB])
        router_raw = sb("router_raw", [P, KC, E])
        router_w = [sb(f"router_{k}", [P, KC, E], F32R) for k in ("hi", "lo")]
        router_b = sb("router_b", [P, E])
        down_b = sb("down_b", [E, D])
        bias_one = sb("bias_one", [P, EB])
        qkv_b = sb("qkv_b", [P, 3 * D])
        out_b = sb("out_b", [P, D])
        head_g = sb("head_g", [P, HD])
        head_b = sb("head_b", [P, HD])
        in_gb = sb("in_gb", [P, 4, KC])
        cosine = sb("cosine", [P, TB, HD // 2])
        sine = sb("sine", [P, TB, HD // 2])
        row_max = sb("row_max", [P, TB, HEADS, 2])
        group_max = sb("group_max", [P, TB, GH])
        head_sum = sb("head_sum", [P, 2 * HEADS])
        head_var = sb("head_var", [P, 2 * HEADS])
        head_rstd = sb("head_rstd", [P, 2 * HEADS])
        inv_den = sb("inv_den", [P, 4, GH])
        xnorm = sb("xnorm", [P, TB])
        arena = sb("arena", [P, ARENA])
        at = [0]

        def cut(n, *shape):
            s = arena[:, at[0]:at[0] + n]
            at[0] += n
            assert at[0] <= ARENA
            if len(shape) == 2:
                return s.rearrange("p (a b) -> p a b", a=shape[0])
            if len(shape) == 3:
                return s.rearrange("p (a b c) -> p a b c", a=shape[0], b=shape[1])
            return s

        chain_sem = {k: sem(f"{k}_chain") for k in ("dve", "act", "pool")}
        chained = {k: 0 for k in chain_sem}

        def link(eng, k, ins):
            chained[k] += 1
            ins.then_inc(chain_sem[k], 1)
            eng.wait_ge(chain_sem[k], chained[k])

        at[0] = 0
        raw1 = cut(KC * FF, KC, FF)
        raw3 = cut(KC * FF, KC, FF)
        raw2 = cut(FB * D, FB, D)
        fly = [cut(FB * D, FB, D) for _ in range(2)]
        mask_raw = cut(3 * P, 3, P)
        c_loaded = sem("c_loaded")
        x_loaded = sem("x_loaded")
        w_loaded = [sem(f"w_loaded{i}") for i in range(3)]
        w_hi = sem("w_hi")
        w_lo = sem("w_lo")
        had_done = sem("had_done")
        had_copied = sem("had_copied")
        fly_done = sem("fly_done")
        pool_consts = sem("pool_consts")

        def load_sync(sp):
            sp.dma_start(x[:], a["x"].rearrange("(b p) d -> p b d", p=P)).then_inc(x_loaded, 16)
            sp.dma_start(raw2, a["w2t"].rearrange("(b p) d -> p b d", p=P)).then_inc(w_loaded[0], 16)
            sp.dma_start(raw1, a["w1t"].rearrange("(c p) h -> p c h", p=P)).then_inc(w_loaded[1], 16)
            sp.dma_start(raw3, a["w3t"].rearrange("(c p) h -> p c h", p=P)).then_inc(w_loaded[2], 16)

        def load_act(act):
            act.dma_start(ident[:], a["ident"]).then_inc(c_loaded, 16)
            act.dma_start(mask_raw[:, 0, :], a["hadamard"]).then_inc(c_loaded, 16)
            act.dma_start(mask_raw[:, 1, :], a["mask_qk"]).then_inc(c_loaded, 16)
            act.dma_start(mask_raw[:, 2, :], a["mask_kq"]).then_inc(c_loaded, 16)
            act.dma_start(router_raw[:], a["router_t"].rearrange("(c p) e -> p c e", p=P)).then_inc(c_loaded, 16)
            act.dma_start(router_b[:], a["router_b"].partition_broadcast(P)).then_inc(c_loaded, 16)
            act.dma_start(down_b[:], a["down_b"]).then_inc(c_loaded, 16)

        C_ALL = 7 * 16
        w2_raw = [xt_hi[:].rearrange("p c t -> p (c t)"), xt_lo[:].rearrange("p c t -> p (c t)")]
        flat2 = raw2.rearrange("p b d -> p (b d)")

        def prep_act(act):
            act.wait_ge(w_loaded[0], 16)
            act.activation(w2_raw[0], flat2, ACT.Copy).then_inc(w_hi, 1)
            act.wait_ge(w_loaded[1], 16)
            act.activation(w1[0][:], raw1, ACT.Copy).then_inc(w_hi, 1)
            act.wait_ge(w_loaded[2], 16)
            act.activation(w3[0][:], raw3, ACT.Copy).then_inc(w_hi, 1)
            for i in range(4):
                act.wait_ge(had_done, i + 1)
                act.activation(fly[0][:, 2 * i:2 * i + 2, :].rearrange("p b d -> p (b d)"), banks[i][:], ACT.Copy)\
                   .then_inc(had_copied, 1)
            act.wait_ge(fly_done, 1)
            act.activation(w2[0][:], fly[1], ACT.Copy, scale=1.0 / 64.0).then_inc(w_hi, 1)

        def prep_pool(pool):
            pool.memset(half_neg[:], -0.5).then_inc(pool_consts, 1)
            pool.memset(half_pos[:], 0.5).then_inc(pool_consts, 1)
            pool.memset(bias_one[:, 0:KC], 0.0).then_inc(pool_consts, 1)
            pool.memset(bias_one[:, KC:EB], 1.0).then_inc(pool_consts, 1)

        def prep_dve(dve):
            dve.wait_ge(c_loaded, C_ALL)
            dve.tensor_copy(had_r[:], mask_raw[:, 0, :]).then_inc(w_lo, 1)
            dve.tensor_copy(mask_qk[:], mask_raw[:, 1, :]).then_inc(w_lo, 1)
            dve.tensor_copy(mask_kq[:], mask_raw[:, 2, :]).then_inc(w_lo, 1)
            dve.tensor_copy(ident_b[:], ident[:]).then_inc(w_lo, 1)
            dve.wait_ge(w_hi, 1)
            dve.tensor_tensor(w2_raw[1], flat2, w2_raw[0].bitcast(F32), ALU.subtract).then_inc(w_lo, 1)
            dve.wait_ge(w_hi, 2)
            dve.tensor_tensor(w1[1][:], raw1, w1[0][:].bitcast(F32), ALU.subtract).then_inc(w_lo, 1)
            dve.wait_ge(w_hi, 3)
            dve.tensor_tensor(w3[1][:], raw3, w3[0][:].bitcast(F32), ALU.subtract).then_inc(w_lo, 1)
            link(dve, "dve", dve.tensor_copy(router_w[0][:], router_raw[:]))
            dve.tensor_tensor(router_w[1][:], router_raw[:], router_w[0][:].bitcast(F32), ALU.subtract).then_inc(w_lo, 1)
            dve.wait_ge(had_copied, 4)
            for k in range(3):
                s, d = fly[k % 2], fly[1 - k % 2]
                step = 1 << k
                sv = s.rearrange("p (a two b) d -> p a two (b d)", two=2, b=step)
                dv = d.rearrange("p (a two b) d -> p a two (b d)", two=2, b=step)
                link(dve, "dve", dve.tensor_tensor(dv[:, :, 0, :], sv[:, :, 0, :], sv[:, :, 1, :], ALU.add))
                ins = dve.tensor_tensor(dv[:, :, 1, :], sv[:, :, 0, :], sv[:, :, 1, :], ALU.subtract)
                if k < 2:
                    link(dve, "dve", ins)
                else:
                    ins.then_inc(fly_done, 1)
            dve.wait_ge(w_hi, 4)
            dve.scalar_tensor_tensor(w2[1][:].rearrange("p b d -> p (b d)"), fly[1].rearrange("p b d -> p (b d)"), 1.0 / 64.0,
                                     w2[0][:].rearrange("p b d -> p (b d)").bitcast(F32), ALU.mult, ALU.subtract).then_inc(w_lo, 1)

        def prep_pe(pe):
            pe.wait_ge(w_hi, 1)
            pe.wait_ge(w_lo, 5)
            for i in range(4):
                for k in range(2):
                    ins = pe.matmul(banks[i][:], had_r[:], w2_raw[k][:, 512 * i:512 * i + 512], start=k == 0, stop=k == 1)
                ins.then_inc(had_done, 1)

        class Sems:

            def __init__(self, stage, totals, before=None):
                self.sems = before.sems if before else {n: sem(f"{stage}_{n}") for n in totals}
                self.base = totals if before else dict.fromkeys(totals, 0)

            def __getitem__(self, n):
                return self.sems[n]

            def after(self, n, value):
                return self.sems[n], self.base[n] + value

        def norm_dve(dve, s, src, dst, waits):
            for w in waits:
                dve.wait_ge(*w)
            for b in range(TB):
                ins = dve.bn_stats(stats[:, b, :], src[:, b, :])
            link(dve, "dve", ins)
            for b in range(TB):
                ins = dve.bn_aggr(meanvar[:, b, :], stats[:, b, :])
            link(dve, "dve", ins)
            dve.tensor_scalar(vareps[:], meanvar[:, :, 1], EPS, None, ALU.add).then_inc(s["var"], 1)
            dve.wait_ge(*s.after("rstd", 1))
            for b in range(TB):
                dve.tensor_scalar(dst[:, b, :], src[:, b, :], meanvar[:, b, 0:1], rstd[:, b:b + 1],
                                  ALU.subtract, ALU.mult).then_inc(s["normed"], 1)

        def norm_pool(pool, s):
            pool.wait_ge(*s.after("var", 1))
            pool.tensor_tensor(rstd[:], vareps[:], half_neg[:, 0:TB], ALU.pow).then_inc(s["rstd"], 1)

        def turn_pe(pe, s, src):
            for i in range(NHALF * KC):
                n, c = i // KC, i % KC
                pe.wait_ge(*s.after("normed", TB // NHALF * (n + 1)))
                for b in range(4):
                    ins = pe.transpose(banks[i][:, b * P:(b + 1) * P], src[:, 4 * n + b, c * P:(c + 1) * P], ident[:])
                ins.then_inc(s["turned"], 1)

        def turn_act(act, s):
            for i in range(NHALF * KC):
                n, c = i // KC, i % KC
                act.wait_ge(*s.after("turned", i + 1))
                act.activation(xt_hi[:, c, n * HALF:(n + 1) * HALF], banks[i][:], ACT.Copy).then_inc(s["xt_hi"], 1)

        def turn_dve(dve, s):
            for i in range(NHALF * KC):
                n, c = i // KC, i % KC
                dve.wait_ge(*s.after("xt_hi", i + 1))
                q = slice(n * HALF, (n + 1) * HALF)
                dve.tensor_tensor(xt_lo[:, c, q], banks[i][:], xt_hi[:, c, q].bitcast(F32), ALU.subtract)\
                   .then_inc(s["xt_lo"], 1)

        NORM = dict(var=1, rstd=1, normed=TB, turned=4, xt_hi=4, xt_lo=4)

        def three(pe, dst, w, m, kcs, first=True, last=True):
            n = len(kcs) * 3
            for i, k in enumerate(kcs):
                for j, (hw, hm) in enumerate(((0, 0), (0, 1), (1, 0))):
                    ins = pe.matmul(dst, w[hw](k), m[hm](k), start=first and i + j == 0, stop=last and 3 * i + j == n - 1,
                                    skip_group_check=not (first and last))
            return ins

        def moving(n):
            q = slice(n * HALF, (n + 1) * HALF)
            return [lambda k: xt_hi[:, k, q], lambda k: xt_lo[:, k, q]]

        def finish_act(act, s, outT, scale, done):
            for n in range(NHALF):
                for c in range(KC):
                    act.wait_ge(*s.after("down", done(n)))
                    act.activation(outT[:, c, n * HALF:(n + 1) * HALF], banks[4 + 2 * n + c][:], ACT.Copy, scale=scale)\
                       .then_inc(s["out_copied"], 1)

        def finish_pe(pe, s, outT):
            for i in range(4):
                pe.wait_ge(*s.after("out_copied", KC * (i // 2 + 1)))
                for b in range(2):
                    for c in range(KC):
                        ins = pe.transpose(banks[i][:, b * D + c * P:b * D + (c + 1) * P],
                                           outT[:, c, (2 * i + b) * P:(2 * i + b + 1) * P], ident[:])
                ins.then_inc(s["out_turned"], 1)

        def finish_dve(dve, s):
            for i in range(4):
                dve.wait_ge(*s.after("out_turned", i + 1))
                v = x[:, 2 * i:2 * i + 2, :].rearrange("p b d -> p (b d)")
                dve.tensor_tensor(v, banks[i][:], v, ALU.add).then_inc(s["x_done"], 1)

        at[0] = 0
        f_silu = [cut(HALF) for _ in range(2)]
        f_hid = [cut(HALF) for _ in range(2)]
        at[0] = max(at[0], 16 * 1024)
        f_out = cut(KC * T, KC, T)
        UNITS = NHALF * FB
        FFN = NORM | dict.fromkeys("gate up silu hidden hid_hi hid_lo down".split(), UNITS) | dict.fromkeys(
            "out_copied out_turned x_done".split(), 4)

        def ffn_pe(pe, s, waits):
            def gate_up(i):
                n, h = i // FB, i % FB
                if i >= 2:
                    pe.wait_ge(*s.after("silu", i - 1))
                three(pe, banks[i % 2][:], [lambda k: w1[0][:, k, h * P:(h + 1) * P], lambda k: w1[1][:, k, h * P:(h + 1) * P]],
                      moving(n), range(KC)).then_inc(s["gate"], 1)
                if i >= 2:
                    pe.wait_ge(*s.after("hidden", i - 1))
                three(pe, banks[2 + i % 2][:], [lambda k: w3[0][:, k, h * P:(h + 1) * P], lambda k: w3[1][:, k, h * P:(h + 1) * P]],
                      moving(n), range(KC)).then_inc(s["up"], 1)

            turn_pe(pe, s, xn)
            pe.wait_ge(*s.after("xt_lo", 4))
            for w in waits:
                pe.wait_ge(*w)
            gate_up(0)
            gate_up(1)
            for i in range(UNITS):
                if i + 2 < UNITS:
                    gate_up(i + 2)
                n, h = i // FB, i % FB
                pe.wait_ge(*s.after("hid_lo", i + 1))
                for c in range(KC):
                    ins = three(pe, banks[4 + 2 * n + c][:],
                                [lambda k: w2[0][:, h, c * P:(c + 1) * P], lambda k: w2[1][:, h, c * P:(c + 1) * P]],
                                [lambda k: hid[i % 2][0][:], lambda k: hid[i % 2][1][:]], [0], first=h == 0, last=h == FB - 1)
                ins.then_inc(s["down"], 1)
            finish_pe(pe, s, f_out)

        def ffn_act(act, s):
            turn_act(act, s)
            for i in range(UNITS + 1):
                if i < UNITS:
                    act.wait_ge(*s.after("gate", i + 1))
                    if i >= 2:
                        act.wait_ge(*s.after("hidden", i - 1))
                    act.activation(f_silu[i % 2], banks[i % 2][:], ACT.Silu).then_inc(s["silu"], 1)
                if i >= 1:
                    j = i - 1
                    act.wait_ge(*s.after("hidden", j + 1))
                    if j >= 2:
                        act.wait_ge(*s.after("down", j - 1))
                    act.activation(hid[j % 2][0][:], f_hid[j % 2], ACT.Copy).then_inc(s["hid_hi"], 1)
            finish_act(act, s, f_out, 1.0, lambda n: FB * (n + 1))

        def ffn_dve(dve, s, waits):
            norm_dve(dve, s, x, xn, waits)
            turn_dve(dve, s)
            for i in range(UNITS + 1):
                if i < UNITS:
                    dve.wait_ge(*s.after("up", i + 1))
                    dve.wait_ge(*s.after("silu", i + 1))
                    if i >= 2:
                        dve.wait_ge(*s.after("hid_lo", i - 1))
                    dve.tensor_tensor(f_hid[i % 2], banks[2 + i % 2][:], f_silu[i % 2], ALU.mult).then_inc(s["hidden"], 1)
                if i >= 1:
                    j = i - 1
                    dve.wait_ge(*s.after("hid_hi", j + 1))
                    if j >= 2:
                        dve.wait_ge(*s.after("down", j - 1))
                    dve.tensor_tensor(hid[j % 2][1][:], f_hid[j % 2], hid[j % 2][0][:].bitcast(F32), ALU.subtract)\
                       .then_inc(s["hid_lo"], 1)
            finish_dve(dve, s)

        UE = NHALF * KC
        at[0] = 0
        raw = [cut(EW + EB + ED) for _ in range(2)]
        score_wide = [cut(T) for _ in range(2)]
        m_gate = [cut(HALF) for _ in range(2)]
        m_glu = [cut(HALF) for _ in range(2)]
        m_up = [cut(HALF) for _ in range(2)]
        m_hid = [cut(HALF) for _ in range(2)]
        m_scaled = [cut(HALF) for _ in range(2)]
        m_bias = [cut(EB) for _ in range(2)]
        m_scores_t = cut(T)
        m_logits = cut(TB * (E + TOPK), TB, E + TOPK)
        m_top = cut(TB * 8, TB, 8)
        m_taken = cut(TB * 8, TB, 8)
        m_marked = cut(TB * (E + TOPK), TB, E + TOPK)
        m_exp = cut(TB * E, TB, E)
        m_chosen = cut(TB * E, TB, E)
        m_sum = cut(TB)
        m_scores = cut(TB * E, TB, E)
        at[0] = max(at[0], 16 * 1024)
        m_out = cut(KC * T, KC, T)
        MOE = NORM | dict.fromkeys("gate up clipped up_read glu product scaled hid_hi hid_lo down".split(), UE * E)
        MOE |= dict.fromkeys("logits centred exped scored scores_turned".split(), 1)
        MOE |= dict.fromkeys("raw_in0 raw_in1 wide_in0 wide_in1".split(), 16 * E // 2)
        MOE |= dict(scores_copied=NHALF, scores_out=16, w_hi=E, w_lo=E, out_copied=4, out_turned=4, x_done=4)

        def router_pe(pe, s):
            for b in range(TB):
                q = slice(b * P, (b + 1) * P)
                ins = three(pe, banks[4][:, b * E:(b + 1) * E], [lambda k: xt_hi[:, k, q], lambda k: xt_lo[:, k, q]],
                            [lambda k: router_w[0][:, k, :], lambda k: router_w[1][:, k, :]], range(KC))
            ins.then_inc(s["logits"], 1)
            pe.wait_ge(*s.after("scored", 1))
            for b in range(TB):
                ins = pe.transpose(banks[5 + b // 4][0:E, (b % 4) * P:(b % 4 + 1) * P], m_scores[:, b, :], ident[:])
            ins.then_inc(s["scores_turned"], 1)

        def router_dve(dve, s):
            dve.memset(m_taken, SENTINEL)
            link(dve, "dve", dve.memset(m_logits[:, :, E:E + TOPK], SENTINEL))
            dve.wait_ge(*s.after("logits", 1))
            link(dve, "dve", dve.tensor_tensor(m_logits[:, :, 0:E], banks[4][:, 0:TB * E].rearrange("p (b e) -> p b e", b=TB),
                                               bcast(router_b[:], 1, TB), ALU.add))
            for b in range(TB):
                ins = dve.max(m_top[:, b, :], m_logits[:, b, 0:E])
            link(dve, "dve", ins)
            dve.tensor_tensor(m_exp, m_logits[:, :, 0:E], bcast(m_top[:, :, 0], 2, E), ALU.subtract).then_inc(s["centred"], 1)
            link(dve, "dve", dve.tensor_copy(m_taken[:, :, 0:TOPK], m_top[:, :, 0:TOPK]))
            for b in range(TB):
                ins = dve.match_replace(out=m_marked[:, b, :], in_to_replace=m_taken[:, b, :], in_values=m_logits[:, b, :],
                                        imm_value=TAKEN)
            link(dve, "dve", ins)
            link(dve, "dve", dve.tensor_tensor(m_chosen, m_marked[:, :, 0:E], m_logits[:, :, 0:E], ALU.not_equal))
            dve.wait_ge(*s.after("exped", 1))
            link(dve, "dve", dve.tensor_tensor(m_chosen, m_chosen, m_exp, ALU.mult))
            link(dve, "dve", dve.reduce_sum(m_sum, m_chosen, axis=AX_X))
            link(dve, "dve", dve.reciprocal(m_sum, m_sum))
            dve.tensor_tensor(m_scores, m_chosen, bcast(m_sum, 2, E), ALU.mult).then_inc(s["scored"], 1)

        def router_act(act, s):
            act.wait_ge(*s.after("centred", 1))
            act.activation(m_exp, m_exp, ACT.Exp).then_inc(s["exped"], 1)
            act.wait_ge(*s.after("scores_turned", 1))
            for n in range(NHALF):
                act.activation(m_scores_t[0:E, n * HALF:(n + 1) * HALF], banks[5 + n][0:E, :], ACT.Copy)\
                   .then_inc(s["scores_copied"], 1)

        def experts(eng, body):
            for e in (0, 1):
                body(e, e % 2, False)
            with eng.Fori(2, E - 2, 2) as e:
                body(e, 0, False)
                body(e + 1, 1, False)
            for e in (E - 2, E - 1):
                body(e, e % 2, e == E - 1)

        def behind(eng, s, name, value):
            if not isinstance(value, int) or value > 0:
                eng.wait_ge(*s.after(name, value))

        def moe_sync(sp, s, call, waits):
            for w in waits:
                sp.wait_ge(*w)

            weights = a["moe_w"].rearrange("(pair par) p w -> par pair p w", par=2)
            rows = score_rows[call].rearrange("(pair par) t -> par pair t", par=2)

            def load(pair, par):
                behind(sp, s, "w_lo", 2 * pair + par - 1)
                sp.dma_start(raw[par], weights[par][pair]).then_inc(s[f"raw_in{par}"], 16)

            def widen(pair, par):
                behind(sp, s, "scaled", UE * (2 * pair + par - 1))
                sp.dma_start(score_wide[par], rows[par][pair].partition_broadcast(P)).then_inc(s[f"wide_in{par}"], 16)

            load(0, 0)
            load(0, 1)
            sp.wait_ge(*s.after("scores_copied", NHALF))
            sp.dma_start(score_rows[call], m_scores_t[0:E, :]).then_inc(s["scores_out"], 16)
            sp.wait_ge(*s.after("scores_out", 16))
            widen(0, 0)
            widen(0, 1)
            with sp.Fori(1, E // 2) as pair:
                for par in range(2):
                    load(pair, par)
                    widen(pair, par)

        def moe_pe(pe, s, waits):
            turn_pe(pe, s, xn)
            pe.wait_ge(*s.after("xt_lo", 4))
            router_pe(pe, s)

            def gate_up(e, par, u):
                n, q = u // KC, u % KC
                if u == 0:
                    pe.wait_ge(*s.after("w_lo", e + 1))
                for part, ready, read in ((0, "gate", "clipped"), (1, "up", "up_read")):
                    behind(pe, s, read, UE * e + u - 1)
                    o = part * D + q * P
                    three(pe, banks[2 * part + u % 2][:],
                          [lambda k: wr[par][0][:, k * 2 * D + o:k * 2 * D + o + P],
                           lambda k: wr[par][1][:, k * 2 * D + o:k * 2 * D + o + P]],
                          moving(n), range(KC)).then_inc(s[ready], 1)

            def down(e, par, u, last):
                n, q = u // KC, u % KC
                pe.wait_ge(*s.after("hid_lo", UE * e + u + 1))
                for c in range(KC):
                    o = EW + q * D + c * P
                    ins = three(pe, banks[4 + 2 * n + c][:],
                                [lambda k: wr[par][0][:, o:o + P], lambda k: wr[par][1][:, o:o + P]],
                                [lambda k: hid[u % 2][0][:], lambda k: hid[u % 2][1][:]], [0],
                                first=False, last=last and q == KC - 1)
                ins.then_inc(s["down"], 1)

            pe.wait_ge(*s.after("scores_copied", NHALF))
            for n in range(NHALF):
                for c in range(KC):
                    pe.matmul(banks[4 + 2 * n + c][:], down_b[:, c * P:(c + 1) * P],
                              m_scores_t[0:E, n * HALF:(n + 1) * HALF], start=True, stop=False, skip_group_check=True)
            gate_up(0, 0, 0)
            gate_up(0, 0, 1)

            def body(e, par, last):
                for u in range(UE):
                    if u < 2:
                        gate_up(e, par, u + 2)
                    elif not last:
                        gate_up(e + 1, 1 - par, u - 2)
                    down(e, par, u, last)

            experts(pe, body)
            finish_pe(pe, s, m_out)

        def split_hi(act, s, e, par):
            act.wait_ge(*s.after(f"raw_in{par}", 8 * (e - par) + 16))
            behind(act, s, "down", UE * (e - 1))
            act.activation(wr[par][0][:, 0:EW], raw[par][:, 0:EW], ACT.Copy)
            act.activation(wr[par][0][:, EW:], raw[par][:, EW + EB:], ACT.Copy).then_inc(s["w_hi"], 1)

        def split_lo(dve, s, e, par):
            dve.wait_ge(*s.after("w_hi", e + 1))
            behind(dve, s, "clipped", UE * (e - 1))
            dve.tensor_tensor(m_bias[par], raw[par][:, EW:EW + EB], bias_one[:], ALU.add)
            dve.tensor_tensor(wr[par][1][:, 0:EW], raw[par][:, 0:EW], wr[par][0][:, 0:EW].bitcast(F32), ALU.subtract)
            dve.tensor_tensor(wr[par][1][:, EW:], raw[par][:, EW + EB:], wr[par][0][:, EW:].bitcast(F32), ALU.subtract)\
               .then_inc(s["w_lo"], 1)

        def moe_act(act, s):
            turn_act(act, s)
            router_act(act, s)
            split_hi(act, s, 0, 0)

            def body(e, par, last):
                for u in range(UE):
                    g = UE * e + u
                    act.wait_ge(*s.after("clipped", g + 1))
                    behind(act, s, "product", g - 1)
                    act.activation(m_glu[u % 2], m_gate[u % 2], ACT.Gelu_apprx_sigmoid).then_inc(s["glu"], 1)
                    act.wait_ge(*s.after("scaled", g + 1))
                    behind(act, s, "down", g - 1)
                    act.activation(hid[u % 2][0][:], m_scaled[u % 2], ACT.Copy).then_inc(s["hid_hi"], 1)
                    if u == 0 and not last:
                        split_hi(act, s, e + 1, 1 - par)

            experts(act, body)
            finish_act(act, s, m_out, 0.5, lambda n: UE * (E - 1) + KC * (n + 1))

        def moe_dve(dve, s, waits):
            norm_dve(dve, s, x, xn, waits)
            turn_dve(dve, s)
            router_dve(dve, s)
            split_lo(dve, s, 0, 0)

            def body(e, par, last):
                for u in range(UE):
                    g = UE * e + u
                    n, q = u // KC, u % KC
                    dve.wait_ge(*s.after("gate", g + 1))
                    behind(dve, s, "glu", g - 1)
                    dve.tensor_scalar(m_gate[u % 2], banks[u % 2][:], m_bias[par][:, q:q + 1], ALPHA_LIMIT, ALU.add, ALU.min)\
                       .then_inc(s["clipped"], 1)
                    dve.wait_ge(*s.after("up", g + 1))
                    dve.tensor_scalar(m_up[u % 2], banks[2 + u % 2][:], m_bias[par][:, KC + q:KC + q + 1], ALPHA_LIMIT + 1.0,
                                      ALU.add, ALU.min).then_inc(s["up_read"], 1)
                    dve.wait_ge(*s.after("glu", g + 1))
                    dve.wait_ge(*s.after("up_read", g + 1))
                    behind(dve, s, "scaled", g - 1)
                    dve.scalar_tensor_tensor(m_hid[u % 2], m_up[u % 2], 1.0 - ALPHA_LIMIT, m_glu[u % 2], ALU.max, ALU.mult)\
                       .then_inc(s["product"], 1)
                    if u == 0 and not last:
                        split_lo(dve, s, e + 1, 1 - par)

            experts(dve, body)
            finish_dve(dve, s)

        def moe_pool(pool, s):
            norm_pool(pool, s)

            def body(e, par, last):
                pool.wait_ge(*s.after(f"wide_in{par}", 8 * (e - par) + 16))
                for u in range(UE):
                    g = UE * e + u
                    n = u // KC
                    pool.wait_ge(*s.after("product", g + 1))
                    behind(pool, s, "hid_hi", g - 1)
                    behind(pool, s, "hid_lo", g - 1)
                    pool.tensor_tensor(m_scaled[u % 2], m_hid[u % 2], score_wide[par][:, n * HALF:(n + 1) * HALF], ALU.mult)\
                        .then_inc(s["scaled"], 1)
                    pool.wait_ge(*s.after("hid_hi", g + 1))
                    behind(pool, s, "down", g - 1)
                    pool.tensor_tensor(hid[u % 2][1][:], m_scaled[u % 2], hid[u % 2][0][:].bitcast(F32), ALU.subtract)\
                        .then_inc(s["hid_lo"], 1)

            experts(pool, body)

        at[0] = 0
        qk_tok = cut(2 * TB * D, 2, TB, D)
        v_tok = cut(TB * HEADS * (HD + 1), TB, HEADS, HD + 1)
        stack_at = at[0]
        stacked = [cut(2 * GH * T // 2).bitcast(BF16).rearrange("p (s j t) -> p s j t", s=2, j=GH) for _ in range(2)]
        stack_tok = [cut(4 * GH * P // 2).bitcast(BF16).rearrange("p (t c) -> p t c", c=P) for _ in range(2)]
        stacked.append(stacked_xt[:].rearrange("p (s j t) -> p s j t", s=2, j=GH))
        rest = cut(4 * GH * HD, 4, GH, HD)
        shared = at[0]
        probs = [cut(GH * HALF, GH, HALF) for _ in range(2)]
        neg_tok = cut(TB * GH * STRIP // 2).bitcast(BF16).rearrange("p (t j c) -> p t j c", t=TB, j=GH)
        neg_rest = cut(TB * GH, TB, GH)
        o_wide = cut(HALF)
        at[0] = shared
        qkv_raw = cut(KC * 3 * D, KC, 3 * D)
        wo_raw = cut(KC * D, KC, D)
        at[0] = stack_at + GH * T
        affine = [cut(HALF) for _ in range(2)]
        qk = cut(HALF)
        by_cos = cut(HALF)
        by_sin = cut(HALF)
        turned_qk = cut(HALF)
        centred = cut(HALF)
        squares = cut(HALF)
        w_qkv = [wr[0][k][:].rearrange("p (c n) -> p c n", c=KC) for k in range(2)]
        w_out = [wr[1][k][:, 0:KC * D].rearrange("p (c n) -> p c n", c=KC) for k in range(2)]
        MAX_UNITS = [(b, c, c * HALF, min(HALF, (b + 1) * P - c * HALF)) for b in range(TB) for c in range(b // 4 + 1)]
        EXP_UNITS = [(n, k, max(n * HALF, k * P), (n + 1) * HALF - max(n * HALF, k * P))
                     for n in range(NHALF) for k in range(4 * (n + 1))]
        NU = len(MAX_UNITS)
        assert NU == len(EXP_UNITS)
        ATTN1 = dict.fromkeys([*NORM, *("w_in w_hi w_lo zeroed table projected parts_free parts tok qk_turned qk_copied proj scores "
                                        "tok_half maxed negated neg_turned shifted e_scores exped weighted o_copied o_turned o_done "
                                        "x_done split stack_turned stack_copied").split()])
        ATTN0 = dict.fromkeys([*ATTN1, *("var2 rstd2 var3 squared rstd3 scaled bias_added normed2 turned2 a_hi a_lo wo_done "
                                         "tb_in").split()])

        def attn_load(sp, s, kind, waits):
            for w in waits:
                sp.wait_ge(*w)
            k = kind
            loads = [(qkv_raw, a[k + "_wqkv"].rearrange("(c p) n -> p c n", p=P)),
                     (qkv_b[:], a[k + "_bqkv"].partition_broadcast(P)),
                     (cosine[:], a[k + "_cos"].rearrange("(b p) f -> p b f", p=P)),
                     (sine[:], a[k + "_sin"].rearrange("(b p) f -> p b f", p=P))]
            if kind == "attn0":
                loads += [(wo_raw, a["wo"].rearrange("(c p) n -> p c n", p=P)), (out_b[:], a["bo"].partition_broadcast(P)),
                          (head_g[:], a["head_g"].partition_broadcast(P)), (head_b[:], a["head_b"].partition_broadcast(P)),
                          (in_gb[:], a["in_gb"])]
            for dst, src in loads:
                sp.dma_start(dst, src).then_inc(s["w_in"], 16)

        def loaded(kind):
            return 16 * (9 if kind == "attn0" else 4)

        def attn_pool(pool, s, kind, waits):
            norm_pool(pool, s)
            for w in waits:
                pool.wait_ge(*w)
            for i in range(2):
                pool.memset(stack_tok[i][:, :, PARTS:P], 0.0).then_inc(s["zeroed"], 1)
            pool.memset(v_tok[:, :, :, HD:HD + 1], 1.0).then_inc(s["zeroed"], 1)
            pool.wait_ge(*s.after("zeroed", 3))
            pool.memset(stack_tok[1][:, :, PARTS:PARTS + SHIFT], 1.0).then_inc(s["zeroed"], 1)
            if kind == "attn0":
                pool.wait_ge(*s.after("var2", 1))
                link(pool, "pool", pool.tensor_tensor(rstd[:], vareps[:], half_neg[:, 0:TB], ALU.pow))
                pool.tensor_tensor(xnorm[:], xnorm[:], half_pos[:, 0:TB], ALU.pow).then_inc(s["rstd2"], 1)
                pool.wait_ge(*s.after("w_in", loaded(kind)))
                pool.wait_ge(*s.after("normed", TB))
                pool.tensor_tensor(x[:], x[:], bcast(out_b[:], 1, TB), ALU.add).then_inc(s["bias_added"], 1)
            for b in range(TB):
                pool.wait_ge(*s.after("table", 1))
                pool.wait_ge(*s.after("projected", b + 1))
                if kind == "attn0":
                    v = "p (h f two) -> p h f two"
                    shape = [P, 2 * HEADS, HD // 2, 2]
                    wide = lambda t: t[:, b, :].unsqueeze(1).unsqueeze(3).broadcast_to(shape)
                    kw = dict(f=HD // 2, two=2)
                else:
                    v = "p (h two f) -> p h two f"
                    shape = [P, 2 * HEADS, 2, HD // 2]
                    wide = lambda t: t[:, b, :].unsqueeze(1).unsqueeze(1).broadcast_to(shape)
                    kw = dict(f=HD // 2, two=2)
                if b >= 1:
                    pool.wait_ge(*(s.after("parts_free", 2 * b) if kind == "attn0" else s.after("tok", b)))
                pool.tensor_tensor(by_cos.rearrange(v, **kw), qk.rearrange(v, **kw), wide(cosine), ALU.mult)
                pool.tensor_tensor(by_sin.rearrange(v, **kw), qk.rearrange(v, **kw), wide(sine), ALU.mult).then_inc(s["parts"], 1)
                if kind == "attn0":
                    pool.wait_ge(*s.after("var3", b + 1))
                    pool.tensor_tensor(head_rstd[:], head_var[:], half_neg[:], ALU.pow).then_inc(s["rstd3"], 1)
                    pool.wait_ge(*s.after("scaled", 2 * b + 1))
                    hv = squares.rearrange("p (h d) -> p h d", d=HD)
                    pool.tensor_tensor(hv, hv, bcast(head_g[:], 1, 2 * HEADS), ALU.mult).then_inc(s["scaled"], 1)
            for g in range(GROUPS):
                for step in range(4):
                    split(pool, s, g, step)

        def split(pool, s, g, step):
            n, side = step // 2, step % 2
            count = 4 * g + step
            tile = stack_tok[side]
            block = lambda k: tile[:, :, k * HD:(k + 1) * HD]
            v4 = "p (t j) d -> p t j d"
            src = qk_tok[:, side, 4 * n:4 * n + 4, GH * HD * g:GH * HD * (g + 1)].rearrange("p t (j d) -> p t j d", j=GH)
            mid, low = ((3, 5), (1, 2))[side]
            if g == 0:
                pool.wait_ge(*s.after("tok", 4 * (n + 1)))
                pool.wait_ge(*s.after("zeroed", 4))
            if count >= 2:
                pool.wait_ge(*s.after("stack_turned", 2 * (count - 1)))
            link(pool, "pool", pool.tensor_copy(block(0).rearrange(v4, j=GH), src))
            link(pool, "pool", pool.tensor_tensor(rest, src, block(0).rearrange(v4, j=GH), ALU.subtract))
            link(pool, "pool", pool.tensor_copy(block(mid).rearrange(v4, j=GH), rest))
            pool.tensor_tensor(block(low).rearrange(v4, j=GH), rest, block(mid).rearrange(v4, j=GH), ALU.subtract).then_inc(s["split"], 1)
            for to, of in (((1, 0), (2, 0), (4, 3)), ((3, 0), (5, 0), (4, 1)))[side]:
                ins = pool.tensor_copy(block(to), block(of))
                ins.then_inc(s["split"], 1)

        def attn_act(act, s, kind):
            act.wait_ge(*s.after("w_in", loaded(kind)))
            act.activation(w_qkv[0], qkv_raw, ACT.Copy).then_inc(s["w_hi"], 1)
            if kind == "attn0":
                act.activation(w_out[0], wo_raw, ACT.Copy).then_inc(s["w_hi"], 1)
                for i in range(4):
                    n, c = i // KC, i % KC
                    act.wait_ge(*s.after("turned", i + 1))
                    for t in range(2):
                        if i >= 1:
                            act.wait_ge(*s.after("xt_lo", 2 * (i - 1) + t + 1))
                        link(act, "act", act.activation(affine[t], banks[i][:], ACT.Identity, scale=in_gb[:, 2 * t, c:c + 1],
                                                        bias=in_gb[:, 2 * t + 1, c:c + 1]))
                        if n == 1:
                            act.wait_ge(*s.after("proj", TB // 2))
                        act.activation(xt_hi[:, c, t * HALF:(t + 1) * HALF], affine[t], ACT.Copy).then_inc(s["xt_hi"], 1)
                    if i == 1:
                        for b in range(TB // 2):
                            square(act, s, b)
                for b in range(TB // 2, TB):
                    square(act, s, b)
            else:
                turn_act(act, s)
            for k in range(4):
                stack_copy(act, s, 0, 2 * k)
            for g in range(GROUPS + 1):
                for u in range(NU):
                    if g >= 1:
                        n, k, q0, w = EXP_UNITS[u]
                        unit = (g - 1) * NU + u
                        for pair in range(2):
                            act.wait_ge(*s.after("e_scores", 2 * unit + pair + 1))
                            if pair == 0 and unit >= 2:
                                act.wait_ge(*s.after("weighted", unit - 1))
                            act.activation(probs[u % 2][:, 2 * pair:2 * pair + 2, 0:w], pairs[pair][:, :, 0:w], ACT.Exp, scale=HD ** -0.5)\
                               .then_inc(s["exped"], 1)
                    if g + 1 < GROUPS and u < 8 and u % 2 == 0:
                        stack_copy(act, s, g + 1, u)
                    if u == 4 and g >= 1:
                        o_copy(act, s, g - 1, 0)
                    if u == 0 and g >= 2:
                        o_copy(act, s, g - 2, 1)
            o_copy(act, s, GROUPS - 1, 1)
            if kind == "attn0":
                for i in range(4):
                    n, c = i // KC, i % KC
                    act.wait_ge(*s.after("turned2", i + 1))
                    act.activation(xt_hi[:, c, n * HALF:(n + 1) * HALF], banks[i][:], ACT.Copy).then_inc(s["a_hi"], 1)

        def o_copy(act, s, g, n):
            act.wait_ge(*s.after("weighted", g * NU + (4 if n == 0 else NU)))
            if g or n:
                act.wait_ge(*s.after("o_turned", 2 * g + n))
            act.activation(o_wide, banks[6][:], ACT.Copy).then_inc(s["o_copied"], 1)

        def square(act, s, b):
            act.wait_ge(*s.after("tb_in", b + 1))
            act.activation(squares, centred, ACT.Square).then_inc(s["squared"], 1)

        def stack_copy(eng, s, g, i):
            step, pair = i // 2, i % 2
            n, side = step // 2, step % 2
            q = slice(n * HALF + pair * 2 * P, n * HALF + (pair + 1) * 2 * P)
            dst = stacked[g % 3][:, side, :, q].rearrange("p j (t c) -> p t j c", c=P)
            src = banks[7][:].bitcast(BF16).rearrange("p (t j c) -> p t j c", t=2, j=GH)
            eng.wait_ge(*s.after("stack_turned", 8 * g + i + 1))
            for t in range(2):
                args = (dst[:, t, :, :], src[:, t, :, :])
                ins = eng.activation(*args, ACT.Copy) if i % 2 == 0 else eng.tensor_copy(*args)
            ins.then_inc(s["stack_copied"], 1)

        def attn_dve(dve, s, kind, waits):
            norm_dve(dve, s, x, xn, waits)
            if kind == "attn0":
                dve.wait_ge(*s.after("normed", TB))
                for b in range(TB):
                    ins = dve.bn_stats(stats[:, b, :], xn[:, b, :])
                link(dve, "dve", ins)
                for b in range(TB):
                    ins = dve.bn_aggr(meanvar[:, b, :], stats[:, b, :])
                link(dve, "dve", ins)
                link(dve, "dve", dve.tensor_tensor(xnorm[:], meanvar[:, :, 0], meanvar[:, :, 0], ALU.mult))
                link(dve, "dve", dve.tensor_tensor(xnorm[:], xnorm[:], meanvar[:, :, 1], ALU.add))
                dve.tensor_scalar(xnorm[:], xnorm[:], D * HD ** -0.5, None, ALU.mult)
                dve.tensor_scalar(vareps[:], meanvar[:, :, 1], EPS, None, ALU.add).then_inc(s["var2"], 1)
                dve.wait_ge(*s.after("rstd2", 1))
                for b in range(TB):
                    dve.tensor_scalar(xn[:, b, :], xn[:, b, :], meanvar[:, b, 0:1], rstd[:, b:b + 1],
                                      ALU.subtract, ALU.mult).then_inc(s["normed2"], 1)
                dve.wait_ge(*s.after("w_in", loaded(kind)))
                dve.tensor_tensor(cosine[:], cosine[:], bcast(xnorm[:], 2, HD // 2), ALU.mult)
                dve.tensor_tensor(sine[:], sine[:], bcast(xnorm[:], 2, HD // 2), ALU.mult).then_inc(s["table"], 1)
            else:
                dve.wait_ge(*s.after("w_in", loaded(kind)))
                dve.memset(xnorm[:], 1.0).then_inc(s["table"], 1)
            dve.wait_ge(*s.after("w_hi", 1))
            dve.tensor_tensor(w_qkv[1], qkv_raw, w_qkv[0].bitcast(F32), ALU.subtract).then_inc(s["w_lo"], 1)
            if kind == "attn0":
                dve.wait_ge(*s.after("w_hi", 2))
                dve.tensor_tensor(w_out[1], wo_raw, w_out[0].bitcast(F32), ALU.subtract).then_inc(s["w_lo"], 1)
                for i in range(4):
                    n, c = i // KC, i % KC
                    for t in range(2):
                        dve.wait_ge(*s.after("xt_hi", 2 * i + t + 1))
                        q = slice(t * HALF, (t + 1) * HALF)
                        dve.tensor_tensor(xt_lo[:, c, q], affine[t], xt_hi[:, c, q].bitcast(F32), ALU.subtract)\
                           .then_inc(s["xt_lo"], 1)
                    if i == 1:
                        for b in range(TB // 2):
                            tok_dve(dve, s, kind, b)
                for b in range(TB // 2, TB):
                    tok_dve(dve, s, kind, b)
            else:
                turn_dve(dve, s)
                for b in range(TB):
                    tok_dve(dve, s, kind, b)
            for k in range(4):
                stack_copy(dve, s, 0, 2 * k + 1)
            dve.memset(neg_tok[:, :, :, :], 0.0).then_inc(chain_sem["dve"], 1)
            chained["dve"] += 1
            dve.memset(banks[6], 0.0).then_inc(chain_sem["dve"], 1)
            chained["dve"] += 1
            link(dve, "dve", dve.memset(row_max[:, :, :, 1], SENTINEL))
            for g in range(GROUPS + 1):
                for u in range(NU):
                    if g < GROUPS:
                        b, c, k0, w = MAX_UNITS[u]
                        for j in range(GH):
                            job = (g * NU + u) * GH + j
                            dve.wait_ge(*s.after("scores", job + 1))
                            dve.reduce_max(row_max[:, b, GH * g + j, c:c + 1], banks[job % 2][:, 0:w], axis=AX_X)\
                               .then_inc(s["maxed"], 1)
                    if g + 1 < GROUPS and u < 8 and u % 2 == 1:
                        stack_copy(dve, s, g + 1, u)
                    if u == 0 and g >= 1:
                        shift(dve, s, g - 1)
                    if u == 9 and g >= 1:
                        normalise(dve, s, g - 1, 0)
                    if u == 2 and g >= 2:
                        normalise(dve, s, g - 2, 1)
                if g < GROUPS:
                    dve.wait_ge(*s.after("maxed", (g + 1) * NU * GH))
                    hs = slice(GH * g, GH * (g + 1))
                    link(dve, "dve", dve.tensor_tensor(group_max[:], row_max[:, :, hs, 0], row_max[:, :, hs, 1], ALU.max))
                    if g >= 1:
                        dve.wait_ge(*s.after("neg_turned", g))
                    part = lambda k: neg_tok[:, :, :, k]
                    link(dve, "dve", dve.tensor_scalar(part(0), group_max[:], -1.0, None, ALU.mult))
                    link(dve, "dve", dve.scalar_tensor_tensor(neg_rest, group_max[:], -1.0, part(0), ALU.mult, ALU.subtract))
                    link(dve, "dve", dve.tensor_copy(part(1), neg_rest))
                    dve.tensor_tensor(part(2), neg_rest, part(1), ALU.subtract).then_inc(s["negated"], 1)
            normalise(dve, s, GROUPS - 1, 1)
            if kind == "attn0":
                for i in range(4):
                    n, c = i // KC, i % KC
                    dve.wait_ge(*s.after("a_hi", i + 1))
                    q = slice(n * HALF, (n + 1) * HALF)
                    dve.tensor_tensor(xt_lo[:, c, q], banks[i][:], xt_hi[:, c, q].bitcast(F32), ALU.subtract).then_inc(s["a_lo"], 1)
                dve.wait_ge(*s.after("bias_added", 1))
                for i in range(4):
                    dve.wait_ge(*s.after("wo_done", i + 1))
                    v = x[:, 2 * i:2 * i + 2, :].rearrange("p b d -> p (b d)")
                    dve.tensor_tensor(v, banks[4 + i][:], v, ALU.add).then_inc(s["x_done"], 1)
            else:
                dve.wait_ge(*s.after("o_done", 2 * GROUPS))
                for i in range(4):
                    v = slice(2 * i, 2 * i + 2)
                    dve.tensor_tensor(x[:, v, :], x[:, v, :], xn[:, v, :], ALU.add).then_inc(s["x_done"], 1)

        def shift(dve, s, g):
            dve.wait_ge(*s.after("neg_turned", g + 1))
            for j in range(GH):
                dve.tensor_copy(stacked[g % 3][PARTS:P, 0, j, :], banks[7][j * STRIP:(j + 1) * STRIP, :].bitcast(BF16))\
                   .then_inc(s["shifted"], 1)

        def normalise(dve, s, g, n):
            dve.wait_ge(*s.after("o_turned", 2 * g + n + 1))
            o = banks[7][:].rearrange("p (b j d) -> p b j d", b=4, j=GH)
            link(dve, "dve", dve.reciprocal(inv_den[:], o[:, :, :, HD]))
            dst = xn[:, 4 * n:4 * n + 4, GH * HD * g:GH * HD * (g + 1)].rearrange("p b (j d) -> p b j d", j=GH)
            dve.tensor_tensor(dst, o[:, :, :, 0:HD], bcast(inv_den[:], 3, HD), ALU.mult).then_inc(s["o_done"], 1)

        def tok_dve(dve, s, kind, b):
            par = b % 2
            tok = qk_tok[:, :, b, :]
            dve.wait_ge(*s.after("proj", b + 1))
            if b >= 1:
                dve.wait_ge(*s.after("parts", b))
            bank_q, bank_kv = banks[4 + 2 * par], banks[5 + 2 * par]
            dve.tensor_tensor(qk[:, 0:D], bank_q[:, 0:D], qkv_b[:, 0:D], ALU.add)
            dve.tensor_tensor(qk[:, D:2 * D], bank_kv[:, 0:D], qkv_b[:, D:2 * D], ALU.add)
            hv = "p (h d) -> p h d"
            dve.tensor_tensor(v_tok[:, b, :, 0:HD], bank_kv[:, D:2 * D].rearrange(hv, d=HD), qkv_b[:, 2 * D:3 * D].rearrange(hv, d=HD),
                              ALU.add).then_inc(s["projected"], 1)
            dve.wait_ge(*s.after("parts", b + 1))
            dve.wait_ge(*s.after("zeroed", 4))
            if kind == "attn0":
                dst = turned_qk.rearrange("p (h f two) -> p h f two", f=HD // 2, two=2)
                c, sn = (t.rearrange("p (h f two) -> p h f two", f=HD // 2, two=2) for t in (by_cos, by_sin))
                first, second = (lambda t: t[:, :, :, 0]), (lambda t: t[:, :, :, 1])
            else:
                dst = tok.rearrange("p s (h two f) -> p s h two f", two=2, f=HD // 2)
                c, sn = (t.rearrange("p (h two f) -> p h two f", f=HD // 2, two=2) for t in (by_cos, by_sin))
                c, sn = (t.rearrange("p (s h) two f -> p s h two f", s=2) for t in (c, sn))
                first, second = (lambda t: t[..., 0, :]), (lambda t: t[..., 1, :])
                dve.tensor_tensor(first(dst), first(c), second(sn), ALU.subtract).then_inc(s["tok_half"], 1)
                dve.tensor_tensor(second(dst), first(sn), second(c), ALU.add).then_inc(s["tok"], 1)
                return
            dve.tensor_tensor(first(dst), first(c), second(sn), ALU.subtract).then_inc(s["parts_free"], 1)
            dve.tensor_tensor(second(dst), first(sn), second(c), ALU.add).then_inc(s["parts_free"], 1)
            dve.wait_ge(*s.after("parts_free", 2 * b + 2))
            r, cen, sq = (t.rearrange(hv, d=HD) for t in (turned_qk, centred, squares))
            link(dve, "dve", dve.reduce_sum(head_sum[:], r, axis=AX_X))
            dve.scalar_tensor_tensor(cen, bcast(head_sum[:], 2, HD), -1.0 / HD, r, ALU.mult, ALU.add).then_inc(s["tb_in"], 1)
            dve.wait_ge(*s.after("squared", b + 1))
            link(dve, "dve", dve.reduce_sum(head_var[:], sq, axis=AX_X))
            dve.tensor_scalar(head_var[:], head_var[:], 1.0 / HD, EPS, ALU.mult, ALU.add).then_inc(s["var3"], 1)
            dve.wait_ge(*s.after("rstd3", b + 1))
            dve.tensor_tensor(sq, cen, bcast(head_rstd[:], 2, HD), ALU.mult).then_inc(s["scaled"], 1)
            dve.wait_ge(*s.after("scaled", 2 * b + 2))
            dve.tensor_tensor(tok.rearrange("p s (h d) -> p s h d", d=HD), sq.rearrange("p (s h) d -> p s h d", s=2),
                              head_b[:].unsqueeze(1).unsqueeze(1).broadcast_to([P, 2, HEADS, HD]), ALU.add).then_inc(s["tok"], 1)

        def attn_pe(pe, s, kind, waits):
            for w in waits:
                pe.wait_ge(*w)
            if kind == "attn0":
                for i in range(4):
                    n, c = i // KC, i % KC
                    pe.wait_ge(*s.after("normed2", 4 * (n + 1)))
                    for b in range(4):
                        ins = pe.transpose(banks[i][:, b * P:(b + 1) * P], xn[:, 4 * n + b, c * P:(c + 1) * P], ident[:])
                    ins.then_inc(s["turned"], 1)
            else:
                turn_pe(pe, s, xn)

            def project(b):
                par = b % 2
                if kind == "attn0":
                    pe.wait_ge(*s.after("xt_lo", 4 * (b // 4 + 1)))
                    q0, kv0 = (b % 4) * P, HALF + (b % 4) * P
                else:
                    pe.wait_ge(*s.after("xt_lo", 2 * (b // 4 + 1)))
                    q0 = kv0 = b * P
                pe.wait_ge(*s.after("w_lo", 1))
                if b >= 2:
                    pe.wait_ge(*s.after("projected", b - 1))
                three(pe, banks[4 + 2 * par][:, 0:D], [lambda k: xt_hi[:, k, q0:q0 + P], lambda k: xt_lo[:, k, q0:q0 + P]],
                      [lambda k: w_qkv[0][:, k, 0:D], lambda k: w_qkv[1][:, k, 0:D]], range(KC))
                three(pe, banks[5 + 2 * par][:], [lambda k: xt_hi[:, k, kv0:kv0 + P], lambda k: xt_lo[:, k, kv0:kv0 + P]],
                      [lambda k: w_qkv[0][:, k, D:3 * D], lambda k: w_qkv[1][:, k, D:3 * D]], range(KC)).then_inc(s["proj"], 1)

            def turn_stack(g, i):
                step, pair = i // 2, i % 2
                side = step % 2
                count = 4 * g + step
                pe.wait_ge(*s.after("split", 4 * (count + 1)))
                if g >= 3 and i == 3:
                    pe.wait_ge(*s.after("o_done", 2 * (g - 2)))
                if 8 * g + i:
                    pe.wait_ge(*s.after("stack_copied", 8 * g + i))
                dst = banks[7][:].bitcast(BF16)
                for t in range(2 * GH):
                    ins = pe.transpose(dst[:, t * P:(t + 1) * P], stack_tok[side][:, 2 * GH * pair + t, :], ident_b[:])
                ins.then_inc(s["stack_turned"], 1)

            for b in range(TB):
                project(b)
            pe.wait_ge(*s.after("projected", TB))
            for i in range(8):
                turn_stack(0, i)
            pe.wait_ge(*s.after("stack_copied", 8))

            def max_scores(g, u):
                b, c, k0, w = MAX_UNITS[u]
                if u == 0:
                    pe.wait_ge(*s.after("stack_copied", 8 * (g + 1)))
                for j in range(GH):
                    job = (g * NU + u) * GH + j
                    if job >= 2:
                        pe.wait_ge(*s.after("maxed", job - 1))
                    diagonal = k0 + w == (b + 1) * P
                    ins = pe.matmul(banks[job % 2][:, 0:w], stacked[g % 3][0:PARTS, 0, j, b * P:(b + 1) * P],
                                    stacked[g % 3][0:PARTS, 1, j, k0:k0 + w], start=True, stop=not diagonal)
                    if diagonal:
                        ins = pe.matmul(banks[job % 2][:, w - P:w], ident_b[:], mask_qk[:], start=False, stop=True)
                    ins.then_inc(s["scores"], 1)

            def exp_scores(g, u, pair):
                n, k, q0, w = EXP_UNITS[u]
                unit = g * NU + u
                if unit >= 1:
                    pe.wait_ge(*s.after("exped", 2 * unit + pair - 1))
                diagonal = q0 == k * P
                for i in range(2):
                    j = 2 * pair + i
                    dst = pairs[pair][:, i, :]
                    ins = pe.matmul(dst[:, 0:w], stacked[g % 3][0:PARTS + SHIFT, 1, j, k * P:(k + 1) * P],
                                    stacked[g % 3][0:PARTS + SHIFT, 0, j, q0:q0 + w], start=True, stop=not diagonal)
                    if diagonal:
                        ins = pe.matmul(dst[:, 0:P], ident_b[:], mask_kq[:], start=False, stop=True)
                ins.then_inc(s["e_scores"], 1)

            def weigh(g, u):
                n, k, q0, w = EXP_UNITS[u]
                unit = g * NU + u
                if k == 0 and (g or n):
                    pe.wait_ge(*s.after("o_copied", 2 * g + n))
                pe.wait_ge(*s.after("exped", 2 * (unit + 1)))
                for j in range(GH):
                    ins = pe.matmul(banks[6][j * STRIP:j * STRIP + HD + 1, q0 - n * HALF:HALF], v_tok[:, k, GH * g + j, :],
                                    probs[u % 2][:, j, 0:w], start=k == 0, stop=k == 4 * n + 3, tile_position=(0, j * STRIP),
                                    skip_group_check=True)
                ins.then_inc(s["weighted"], 1)

            def turn_max(g):
                pe.wait_ge(*s.after("negated", g + 1))
                if g + 1 < GROUPS:
                    pe.wait_ge(*s.after("stack_copied", 8 * (g + 2)))
                if g >= 1:
                    pe.wait_ge(*s.after("o_done", 2 * g - 1))
                dst = banks[7][:].bitcast(BF16)
                for b in range(TB):
                    ins = pe.transpose(dst[:, b * P:(b + 1) * P], neg_tok[:, b, :, :].rearrange("p j c -> p (j c)"), ident_b[:])
                ins.then_inc(s["neg_turned"], 1)

            def turn_o(g, n):
                pe.wait_ge(*s.after("o_copied", 2 * g + n + 1))
                pe.wait_ge(*s.after("shifted", GH * min(GROUPS, g + 1 + n)))
                pe.wait_ge(*s.after("stack_copied", min(8 * GROUPS, 8 * (g + 3) + 3 * n)))
                if g or n:
                    pe.wait_ge(*s.after("o_done", 2 * g + n))
                for b in range(4):
                    ins = pe.transpose(banks[7][:, b * P:(b + 1) * P], o_wide[:, b * P:(b + 1) * P], ident[:])
                ins.then_inc(s["o_turned"], 1)

            for g in range(GROUPS + 1):
                for u in range(NU):
                    if g < GROUPS:
                        max_scores(g, u)
                    if g >= 1:
                        if u == 0:
                            turn_max(g - 1)
                            pe.wait_ge(*s.after("shifted", GH * g))
                        exp_scores(g - 1, u, 0)
                        exp_scores(g - 1, u, 1)
                    if g + 1 < GROUPS and u < 8:
                        turn_stack(g + 1, u)
                    if g >= 1:
                        if u >= 1:
                            weigh(g - 1, u - 1)
                        elif g >= 2:
                            weigh(g - 2, NU - 1)
                        if u == 2 and g >= 2:
                            turn_o(g - 2, 1)
                        if u == 9:
                            turn_o(g - 1, 0)
            weigh(GROUPS - 1, NU - 1)
            turn_o(GROUPS - 1, 1)
            if kind == "attn0":
                pe.wait_ge(*s.after("o_done", 2 * GROUPS))
                for i in range(4):
                    n, c = i // KC, i % KC
                    for b in range(4):
                        ins = pe.transpose(banks[i][:, b * P:(b + 1) * P], xn[:, 4 * n + b, c * P:(c + 1) * P], ident[:])
                    ins.then_inc(s["turned2"], 1)
                for b in range(TB):
                    pe.wait_ge(*s.after("a_lo", 2 * (b // 4 + 1)))
                    pe.wait_ge(*s.after("w_lo", 2))
                    q = slice(b * P, (b + 1) * P)
                    ins = three(pe, banks[4 + b // 2][:, (b % 2) * D:(b % 2 + 1) * D],
                                [lambda k: xt_hi[:, k, q], lambda k: xt_lo[:, k, q]],
                                [lambda k: w_out[0][:, k, :], lambda k: w_out[1][:, k, :]], range(KC))
                    if b % 2:
                        ins.then_inc(s["wo_done"], 1)

        totals = {"ffn": FFN, "moe": MOE, "attn0": ATTN0, "attn1": ATTN1}
        plan, run = [], {}
        for kind in stages:
            run[kind] = Sems(kind, totals[kind], run.get(kind))
            plan.append((kind, run[kind]))
        x_ready = [[(x_loaded, 16), (pool_consts, 4)]] + [[s.after("x_done", 4)] for _, s in plan]
        before = [[(w_lo, 9), (w_hi, 4)]] + x_ready[1:]
        stored = sem("stored")

        block = ctx.enter_context(nc.Block())

        @block.sync
        def _(sp):
            load_sync(sp)
            for i, (kind, s) in enumerate(plan):
                if kind == "moe":
                    moe_sync(sp, s, i % 2, before[i])
                if kind[:4] == "attn":
                    attn_load(sp, s, kind, before[i])
            for w in x_ready[-1]:
                sp.wait_ge(*w)
            sp.dma_start(out.rearrange("(b p) d -> p b d", p=P), x[:]).then_inc(stored, 16)
            sp.wait_ge(stored, 16)

        @block.scalar
        def _(act):
            load_act(act)
            prep_act(act)
            for i, (kind, s) in enumerate(plan):
                if kind == "ffn":
                    ffn_act(act, s)
                if kind == "moe":
                    moe_act(act, s)
                if kind[:4] == "attn":
                    attn_act(act, s, kind)

        @block.gpsimd
        def _(pool):
            prep_pool(pool)
            for i, (kind, s) in enumerate(plan):
                if kind == "ffn":
                    norm_pool(pool, s)
                if kind == "moe":
                    moe_pool(pool, s)
                if kind[:4] == "attn":
                    attn_pool(pool, s, kind, before[i])

        @block.vector
        def _(dve):
            prep_dve(dve)
            for i, (kind, s) in enumerate(plan):
                if kind == "ffn":
                    ffn_dve(dve, s, x_ready[i])
                if kind == "moe":
                    moe_dve(dve, s, x_ready[i])
                if kind[:4] == "attn":
                    attn_dve(dve, s, kind, x_ready[i])

        @block.tensor
        def _(pe):
            prep_pe(pe)
            for i, (kind, s) in enumerate(plan):
                if kind == "ffn":
                    ffn_pe(pe, s, before[i])
                if kind == "moe":
                    moe_pe(pe, s, before[i])
                if kind[:4] == "attn":
                    attn_pe(pe, s, kind, before[i])


def causal_masks():
    q = np.arange(P)
    m = np.where(q[None, :] > q[:, None], np.float32(MASKED), np.float32(0.0)).astype(np.float32)
    return m, np.ascontiguousarray(m.T)


def rotations(freqs):
    angle = np.arange(T, dtype=np.float32)[:, None] * freqs.astype(np.float32)[None, :]
    return np.cos(angle).astype(np.float32), np.sin(angle).astype(np.float32)


def expert_rows(i):
    g = i["L1_ffn_gate_up_proj"].reshape(E, KC, P, D, 2).transpose(0, 2, 1, 4, 3).reshape(E, P, EW)
    b = i["L1_ffn_gate_up_proj_bias"].reshape(E, KC, P, 2).transpose(0, 2, 3, 1).reshape(E, P, EB)
    d = i["L1_ffn_down_proj"].reshape(E, KC, P, D).transpose(0, 2, 1, 3).reshape(E, P, ED)
    return np.concatenate([g, b, d], axis=2)


def hadamard():
    h = np.ones((1, 1), np.float32)
    while h.shape[0] < P:
        h = np.block([[h, h], [h, -h]])
    return np.ascontiguousarray(h, dtype=np.float32)


STAGES = ('ffn', 'attn0', 'ffn', 'moe', 'attn1', 'moe')


def kernel(**inputs):
    import concourse.bacc as bacc
    from concourse.bass_utils import run_bass_kernel_spmd as run

    i = {k: np.asarray(v) for k, v in inputs.items()}
    mask_qk, mask_kq = causal_masks()
    steps = np.arange(0, HD, 2, dtype=np.float32) / np.float32(HD)
    cos0, sin0 = rotations(steps * np.log(np.float32(30000.0)))
    cos1, sin1 = rotations(np.float32(1.0) / np.float32(10000.0) ** steps)
    arrays = {
        "x": i["L0_attn_x"][0], "w1t": i["L0_ffn_W1"].T, "w3t": i["L0_ffn_W3"].T, "w2t": i["L0_ffn_W2"].T,
        "ident": np.eye(P, dtype=np.float32), "hadamard": hadamard(), "mask_qk": mask_qk, "mask_kq": mask_kq,
        "router_t": i["L1_ffn_router_weight"].T, "router_b": i["L1_ffn_router_bias"], "down_b": i["L1_ffn_down_proj_bias"],
        "moe_w": expert_rows(i),
        "attn0_wqkv": np.concatenate([i["L0_attn_Wq"], i["L0_attn_Wkv"]], axis=1),
        "attn0_bqkv": np.concatenate([i["L0_attn_bq"], i["L0_attn_bkv"]]),
        "attn1_wqkv": i["L1_attn_w_qkv"].reshape(HEADS, 3, HD, D).transpose(3, 1, 0, 2).reshape(D, 3 * D),
        "attn1_bqkv": i["L1_attn_b_qkv"].reshape(HEADS, 3, HD).transpose(1, 0, 2).reshape(3 * D),
        "wo": i["L0_attn_Wo"], "bo": i["L0_attn_bo"], "head_g": i["L0_attn_ln_g"], "head_b": i["L0_attn_ln_b"],
        "in_gb": np.stack([i["L0_attn_" + k].reshape(KC, P).T for k in ("qn_g", "qn_b", "kvn_g", "kvn_b")], axis=1),
        "attn0_cos": cos0, "attn0_sin": sin0, "attn1_cos": cos1, "attn1_sin": sin1,
    }
    arrays = {k: np.ascontiguousarray(v) for k, v in arrays.items()}
    nc = bacc.Bacc("TRN2", target_bir_lowering=False, num_devices=1)
    aps = {k: nc.dram_tensor("in_" + k, v.shape, F32, kind="ExternalInput").ap() for k, v in arrays.items()}
    out = nc.dram_tensor("out", (T, D), F32, kind="ExternalOutput").ap()
    build(nc, aps, out, STAGES)
    r = run(nc, [{"in_" + k: v for k, v in arrays.items()}], core_ids=[0])
    return r.results[0]["out"].reshape(1, T, D)
```

```python
from contextlib import ExitStack

import numpy as np

from concourse import mybir

F32 = mybir.dt.float32
F32R = mybir.dt.float32r
BF16 = mybir.dt.bfloat16
ALU = mybir.AluOpType
ACT = mybir.ActivationFunctionType
AX_X = mybir.AxisListType.X

P = 128
D = 256
KC = D // P
T = 1024
TB = T // P
HALF = 512
NHALF = T // HALF
FF = 1024
FB = FF // P
HEADS = 16
HD = D // HEADS
STRIP = 32
GH = P // STRIP
GROUPS = HEADS // GH
ARENA = 21 * 1024 + 416
BATCH = 2
PARTS = 6 * HD
SHIFT = 3
E = 16
TOPK = 4
EW = 2 * KC * 2 * P
ED = KC * D
EB = 2 * KC
ALPHA_LIMIT = 7.0
EPS = 1e-5
MASKED = -1.0e30
SENTINEL = -3.0e38
TAKEN = -3.3e38


def bcast(ap, axis, n):
    wide = ap.unsqueeze(axis)
    shape = list(wide.shape)
    shape[axis] = n
    return wide.broadcast_to(shape)


def build(nc, a, out, stages):
    ctx = ExitStack()
    with ctx:
        def sb(name, shape, dt=F32):
            return ctx.enter_context(nc.sbuf_tensor(name, shape, dt))

        def sem(name):
            return ctx.enter_context(nc.semaphore(name))

        all_banks = ctx.enter_context(nc.psum_tensor("all_banks", [P, 8, 512], F32))
        banks = [all_banks[:, i, :] for i in range(8)]
        pairs = [all_banks[:, 2 + 2 * i:4 + 2 * i, :] for i in range(2)]
        score_rows = nc.dram_tensor("score_rows", (E, T), F32, kind="Internal").ap()

        x = sb("x", [P, TB, D])
        xn = sb("xn", [P, TB, D])
        with ExitStack() as before_scores:
            xt_hi, xt_lo = (before_scores.enter_context(nc.sbuf_tensor(f"xt_{k}", [P, KC, T], F32R)) for k in ("hi", "lo"))
        stacked_xt = sb("stacked_xt", [P, 2 * GH * T], BF16)
        w1 = [sb(f"w1_{k}", [P, KC, FF], F32R) for k in ("hi", "lo")]
        w3 = [sb(f"w3_{k}", [P, KC, FF], F32R) for k in ("hi", "lo")]
        w2 = [sb(f"w2_{k}", [P, FB, D], F32R) for k in ("hi", "lo")]
        wr = [[sb(f"wr{i}_{k}", [P, EW + ED], F32R) for k in ("hi", "lo")] for i in range(2)]
        hid = [[sb(f"hid{i}_{k}", [P, HALF], F32R) for k in ("hi", "lo")] for i in range(2)]
        ident = sb("ident", [P, P])
        ident_b = sb("ident_b", [P, P], BF16)
        had_r = sb("had_r", [P, P], F32R)
        mask_qk = sb("mask_qk", [P, P], BF16)
        mask_kq = sb("mask_kq", [P, P], BF16)
        half_neg = sb("half_neg", [P, 32])
        half_pos = sb("half_pos", [P, 32])
        stats = sb("stats", [P, TB, 6])
        meanvar = sb("meanvar", [P, TB, 2])
        vareps = sb("vareps", [P, TB])
        rstd = sb("rstd", [P, TB])
        router_raw = sb("router_raw", [P, KC, E])
        router_w = [sb(f"router_{k}", [P, KC, E], F32R) for k in ("hi", "lo")]
        router_b = sb("router_b", [P, E])
        down_b = sb("down_b", [E, D])
        bias_one = sb("bias_one", [P, EB])
        qkv_b = sb("qkv_b", [P, 3 * D])
        out_b = sb("out_b", [P, D])
        head_g = sb("head_g", [P, HD])
        head_b = sb("head_b", [P, HD])
        in_gb = sb("in_gb", [P, 4, KC])
        cosine = sb("cosine", [P, TB, HD // 2])
        sine = sb("sine", [P, TB, HD // 2])
        row_max = sb("row_max", [P, TB, HEADS, 2])
        group_max = sb("group_max", [P, TB, GH])
        inv_den = sb("inv_den", [P, 4, GH])
        xnorm = sb("xnorm", [P, TB])
        arena = sb("arena", [P, ARENA])
        at = [0]

        def cut(n, *shape):
            s = arena[:, at[0]:at[0] + n]
            at[0] += n
            assert at[0] <= ARENA
            if len(shape) == 2:
                return s.rearrange("p (a b) -> p a b", a=shape[0])
            if len(shape) == 3:
                return s.rearrange("p (a b c) -> p a b c", a=shape[0], b=shape[1])
            return s

        chain_sem = {k: sem(f"{k}_chain") for k in ("dve", "act", "pool")}
        chained = {k: 0 for k in chain_sem}

        def link(eng, k, ins):
            chained[k] += 1
            ins.then_inc(chain_sem[k], 1)
            eng.wait_ge(chain_sem[k], chained[k])

        at[0] = 0
        raw1 = cut(KC * FF, KC, FF)
        raw3 = cut(KC * FF, KC, FF)
        raw2 = cut(FB * D, FB, D)
        fly = [cut(FB * D, FB, D) for _ in range(2)]
        at[0] = 65 * 256
        mask_raw = cut(3 * P, 3, P)
        w2_raw = [[wr[k][j][:, 0:2 * HALF] for j in range(2)] for k in range(2)]
        had_neg = wr[0][0][:, 2 * HALF:2 * HALF + P]
        ident_loaded = sem("ident_loaded")
        c_loaded = sem("c_loaded")
        x_loaded = sem("x_loaded")
        w_loaded = [sem(f"w_loaded{i}") for i in range(3)]
        w_hi = sem("w_hi")
        w1_lo = sem("w1_lo")
        w3_lo = sem("w3_lo")
        w2_raw_lo = sem("w2_raw_lo")
        w2_lo = sem("w2_lo")
        consts = sem("consts")
        had_done = sem("had_done")
        had_copied = sem("had_copied")
        fly_done = sem("fly_done")
        pool_consts = sem("pool_consts")

        def load_sync(sp):
            sp.dma_start(x[:], a["x"].rearrange("(b p) d -> p b d", p=P)).then_inc(x_loaded, 16)
            sp.dma_start(raw1, a["w1t"].rearrange("(c p) h -> p c h", p=P)).then_inc(w_loaded[0], 16)
            sp.dma_start(raw3, a["w3t"].rearrange("(c p) h -> p c h", p=P)).then_inc(w_loaded[1], 16)
            sp.dma_start(raw2, a["w2t"].rearrange("(b p) d -> p b d", p=P)).then_inc(w_loaded[2], 16)

        def load_act(act):
            act.dma_start(ident[:], a["ident"]).then_inc(ident_loaded, 16)
            act.dma_start(mask_raw[:, 0, :], a["hadamard"]).then_inc(c_loaded, 16)
            act.dma_start(mask_raw[:, 1, :], a["mask_qk"]).then_inc(c_loaded, 16)
            act.dma_start(mask_raw[:, 2, :], a["mask_kq"]).then_inc(c_loaded, 16)
            act.dma_start(router_raw[:], a["router_t"].rearrange("(c p) e -> p c e", p=P)).then_inc(c_loaded, 16)
            act.dma_start(router_b[:], a["router_b"].partition_broadcast(P)).then_inc(c_loaded, 16)
            act.dma_start(down_b[:], a["down_b"]).then_inc(c_loaded, 16)

        C_ALL = 6 * 16
        flat2 = raw2.rearrange("p b d -> p (b d)")

        def prep_act(act):
            act.wait_ge(w_loaded[0], 16)
            act.activation(w1[0][:], raw1, ACT.Copy).then_inc(w_hi, 1)
            act.wait_ge(w_loaded[1], 16)
            act.activation(w3[0][:], raw3, ACT.Copy).then_inc(w_hi, 1)

        def prep_late_act(act):
            act.wait_ge(w_loaded[2], 16)
            for j in range(2):
                ins = act.activation(w2_raw[0][j], flat2[:, 2 * HALF * j:2 * HALF * (j + 1)], ACT.Copy)
            ins.then_inc(w_hi, 1)
            for i in range(5):
                if i < 4:
                    act.wait_ge(had_done, i + 1)
                    act.activation(fly[0][:, 2 * i:2 * i + 2, :].rearrange("p b d -> p (b d)"), banks[4 + i][:], ACT.Copy)\
                       .then_inc(had_copied, 1)
                if i >= 1:
                    act.wait_ge(fly_done, 2 * i)
                    act.activation(w2[0][:, 2 * i - 2:2 * i, :], fly[1][:, 2 * i - 2:2 * i, :], ACT.Copy, scale=1.0 / 64.0)\
                       .then_inc(w_hi, 1)

        def prep_pool(pool):
            pool.memset(half_neg[:], -0.5).then_inc(pool_consts, 1)
            pool.memset(half_pos[:], 0.5).then_inc(pool_consts, 1)
            pool.memset(bias_one[:, 0:KC], 0.0).then_inc(pool_consts, 1)
            pool.memset(bias_one[:, KC:EB], 1.0).then_inc(pool_consts, 1)

        def prep_late_pool(pool):
            pool.wait_ge(w_hi, 1)
            pool.tensor_tensor(w1[1][:], raw1, w1[0][:].bitcast(F32), ALU.subtract).then_inc(w1_lo, 1)

        def prep_w3_dve(dve):
            dve.wait_ge(w_hi, 2)
            dve.tensor_tensor(w3[1][:], raw3, w3[0][:].bitcast(F32), ALU.subtract).then_inc(w3_lo, 1)

        def prep_late_dve(dve):
            dve.wait_ge(c_loaded, C_ALL)
            dve.tensor_copy(had_r[:], mask_raw[:, 0, :]).then_inc(consts, 1)
            dve.tensor_scalar(had_neg, mask_raw[:, 0, :], -1.0, None, ALU.mult).then_inc(consts, 1)
            dve.wait_ge(w_hi, 3)
            for j in range(2):
                ins = dve.tensor_tensor(w2_raw[1][j], flat2[:, 2 * HALF * j:2 * HALF * (j + 1)], w2_raw[0][j].bitcast(F32),
                                        ALU.subtract)
            ins.then_inc(w2_raw_lo, 1)
            dve.tensor_copy(mask_qk[:], mask_raw[:, 1, :]).then_inc(consts, 1)
            dve.tensor_copy(mask_kq[:], mask_raw[:, 2, :]).then_inc(consts, 1)
            dve.wait_ge(ident_loaded, 16)
            dve.tensor_copy(ident_b[:], ident[:]).then_inc(consts, 1)
            link(dve, "dve", dve.tensor_copy(router_w[0][:], router_raw[:]))
            dve.tensor_tensor(router_w[1][:], router_raw[:], router_w[0][:].bitcast(F32), ALU.subtract).then_inc(consts, 1)
            for i in range(5):
                if i < 4:
                    dve.wait_ge(had_copied, i + 1)
                    even, odd = (fly[0][:, 2 * i + r, :] for r in range(2))
                    dve.tensor_tensor(fly[1][:, 2 * i, :], even, odd, ALU.add).then_inc(fly_done, 1)
                    dve.tensor_tensor(fly[1][:, 2 * i + 1, :], even, odd, ALU.subtract).then_inc(fly_done, 1)
                if i >= 1:
                    dve.wait_ge(w_hi, 3 + i)
                    b = slice(2 * i - 2, 2 * i)
                    dve.scalar_tensor_tensor(w2[1][:, b, :], fly[1][:, b, :], 1.0 / 64.0, w2[0][:, b, :].bitcast(F32),
                                             ALU.mult, ALU.subtract).then_inc(w2_lo, 1)

        def prep_late_pe(pe):
            pe.wait_ge(consts, 2)
            pe.wait_ge(w2_raw_lo, 1)
            for i in range(4):
                for j in range(4):
                    for k in range(2):
                        h = had_neg if bin(i & j).count("1") % 2 else had_r[:]
                        ins = pe.matmul(banks[4 + i][:], h, w2_raw[k][j // 2][:, HALF * (j % 2):HALF * (j % 2 + 1)], start=j + k == 0,
                                        stop=j + k == 4)
                ins.then_inc(had_done, 1)

        class Sems:

            def __init__(self, stage, totals, before=None):
                self.sems = before.sems if before else {n: sem(f"{stage}_{n}") for n in totals}
                self.base = totals if before else dict.fromkeys(totals, 0)

            def __getitem__(self, n):
                return self.sems[n]

            def after(self, n, value):
                return self.sems[n], self.base[n] + value

        def head_stats(dve, s, n, ready):
            for w in ready:
                dve.wait_ge(*w)
            mine = slice(4 * n, 4 * n + 4)
            for b in range(4 * n, 4 * n + 4):
                ins = dve.bn_stats(stats[:, b, :], x[:, b, :])
            link(dve, "dve", ins)
            for b in range(4 * n, 4 * n + 4):
                ins = dve.bn_aggr(meanvar[:, b, :], stats[:, b, :])
            link(dve, "dve", ins)
            dve.tensor_scalar(vareps[:, mine], meanvar[:, mine, 1], EPS, None, ALU.add).then_inc(s["var"], 1)

        def head_norm(dve, s, kind, n):
            dve.wait_ge(*s.after("rstd", n + 1))
            for b in range(4 * n, 4 * n + 4):
                dve.tensor_scalar(xn[:, b, :], x[:, b, :], meanvar[:, b, 0:1], rstd[:, b:b + 1],
                                  ALU.subtract, ALU.mult).then_inc(s["normed"], 1)
            if kind == "attn0":
                norm_again(dve, s, n)

        def head_pool(pool, s, kind, n):
            mine = slice(4 * n, 4 * n + 4)
            pool.wait_ge(*s.after("var", n + 1))
            pool.tensor_tensor(rstd[:, mine], vareps[:, mine], half_neg[:, 0:4], ALU.pow).then_inc(s["rstd"], 1)
            if kind == "attn0":
                pool.wait_ge(*s.after("var2", n + 1))
                pool.tensor_tensor(rstd[:, mine], vareps[:, mine], half_neg[:, 0:4], ALU.pow).then_inc(s["rstd2"], 1)

        def head_turn_pe(pe, s, kind, n):
            pe.wait_ge(*s.after("normed2" if kind == "attn0" else "normed", 4 * (n + 1)))
            for c in range(KC):
                for b in range(4):
                    ins = pe.transpose(banks[4 + 2 * n + c][:, b * P:(b + 1) * P], xn[:, 4 * n + b, c * P:(c + 1) * P], ident[:])
                ins.then_inc(s["turned"], 1)

        def head_turn_act(act, s, kind, n):
            if kind == "attn0":
                affine_act(act, s, n)
                return
            for c in range(KC):
                act.wait_ge(*s.after("turned", KC * n + c + 1))
                act.activation(xt_hi[:, c, n * HALF:(n + 1) * HALF], banks[4 + 2 * n + c][:], ACT.Copy).then_inc(s["xt_hi"], 1)

        def head_turn_dve(dve, s, kind, n):
            if kind == "attn0":
                if n == 0:
                    affine_lo(dve, s, n)
                return
            for c in range(KC):
                dve.wait_ge(*s.after("xt_hi", KC * n + c + 1))
                q = slice(n * HALF, (n + 1) * HALF)
                dve.tensor_tensor(xt_lo[:, c, q], banks[4 + 2 * n + c][:], xt_hi[:, c, q].bitcast(F32), ALU.subtract)\
                   .then_inc(s["xt_lo"], 1)

        def head_weights_act(act, s, kind):
            if kind == "moe":
                split_hi(act, s, 0, 0)
            if kind[:4] == "attn":
                act.wait_ge(*s.after("w_in", loaded(kind)))
                act.activation(w_qkv[0], qkv_raw, ACT.Copy).then_inc(s["w_hi"], 1)
                if kind == "attn0":
                    act.activation(w_out[0], wo_raw, ACT.Copy).then_inc(s["w_hi"], 1)

        def head_weights_pool(pool, s, kind):
            if kind == "moe":
                split_lo(pool, s, 0, 0)
                split_down_lo(pool, s, 0, 0)
            if kind[:4] == "attn":
                pool.wait_ge(*s.after("w_hi", 1))
                pool.tensor_tensor(w_qkv[1], qkv_raw, w_qkv[0].bitcast(F32), ALU.subtract).then_inc(s["w_lo"], 1)
                if kind == "attn0":
                    pool.wait_ge(*s.after("w_hi", 2))
                    pool.tensor_tensor(w_out[1], wo_raw, w_out[0].bitcast(F32), ALU.subtract).then_inc(s["w_lo"], 1)

        def end_pe(pe, nxt, finish):
            finish(0)
            finish(1)
            if nxt:
                head_turn_pe(pe, nxt[1], nxt[0], 0)

        def end_act(act, nxt, finish):
            finish(0)
            finish(1)
            if nxt:
                head_weights_act(act, nxt[1], nxt[0])
                for n in range(NHALF):
                    head_turn_act(act, nxt[1], nxt[0], n)

        def end_pool(pool, nxt):
            if nxt:
                head_pool(pool, nxt[1], nxt[0], 0)
                head_weights_pool(pool, nxt[1], nxt[0])
                head_pool(pool, nxt[1], nxt[0], 1)

        def end_dve(dve, s, nxt, finish):
            finish(0)
            if nxt:
                head_stats(dve, nxt[1], 0, [s.after("x_done", 2)])
            finish(1)
            if nxt:
                head_norm(dve, nxt[1], nxt[0], 0)
                head_stats(dve, nxt[1], 1, [s.after("x_done", 4)])
                head_turn_dve(dve, nxt[1], nxt[0], 0)
                head_norm(dve, nxt[1], nxt[0], 1)
                head_turn_dve(dve, nxt[1], nxt[0], 1)

        NORM = dict(var=NHALF, rstd=NHALF, normed=TB, turned=4, xt_hi=4, xt_lo=4)

        def three(pe, dst, w, m, kcs, first=True, last=True):
            n = len(kcs) * 3
            for i, k in enumerate(kcs):
                for j, (hw, hm) in enumerate(((0, 0), (0, 1), (1, 0))):
                    ins = pe.matmul(dst, w[hw](k), m[hm](k), start=first and i + j == 0, stop=last and 3 * i + j == n - 1,
                                    skip_group_check=not (first and last))
            return ins

        def moving(n):
            q = slice(n * HALF, (n + 1) * HALF)
            return [lambda k: xt_hi[:, k, q], lambda k: xt_lo[:, k, q]]

        OUT_AT = 49 * 256

        def finish_act(act, s, outT, scale, n, done):
            for c in range(KC):
                act.wait_ge(*s.after("down", done))
                act.activation(outT[:, c, n * HALF:(n + 1) * HALF], banks[4 + 2 * n + c][:], ACT.Copy, scale=scale)\
                   .then_inc(s["out_copied"], 1)

        def finish_pe(pe, s, outT, n):
            pe.wait_ge(*s.after("out_copied", KC * (n + 1)))
            for i in (2 * n, 2 * n + 1):
                for b in range(2):
                    for c in range(KC):
                        ins = pe.transpose(banks[4 + i][:, b * D + c * P:b * D + (c + 1) * P],
                                           outT[:, c, (2 * i + b) * P:(2 * i + b + 1) * P], ident[:])
                ins.then_inc(s["out_turned"], 1)

        def finish_dve(dve, s, n):
            for i in (2 * n, 2 * n + 1):
                dve.wait_ge(*s.after("out_turned", i + 1))
                v = x[:, 2 * i:2 * i + 2, :].rearrange("p b d -> p (b d)")
                dve.tensor_tensor(v, banks[4 + i][:], v, ALU.add).then_inc(s["x_done"], 1)

        at[0] = OUT_AT
        f_out = cut(KC * T, KC, T)
        f_silu = [cut(HALF) for _ in range(2)]
        f_hid = [cut(HALF) for _ in range(2)]
        UNITS = NHALF * FB
        FFN = NORM | dict.fromkeys("gate up silu hidden hid_hi hid_lo down".split(), UNITS) | dict.fromkeys(
            "out_copied out_turned x_done".split(), 4)

        assert FB == 8

        def early(nxt):
            return nxt and nxt[0] != "attn0"

        def ffn_pe(pe, s, nxt, late):
            def gate_up(i):
                n, h = i // FB, i % FB
                if h == 0:
                    pe.wait_ge(*s.after("xt_lo", KC * (n + 1)))
                if i >= 2:
                    pe.wait_ge(*s.after("silu", i - 1))
                three(pe, banks[i % 2][:], [lambda k: w1[0][:, k, h * P:(h + 1) * P], lambda k: w1[1][:, k, h * P:(h + 1) * P]],
                      moving(n), range(KC)).then_inc(s["gate"], 1)
                if i >= 2:
                    pe.wait_ge(*s.after("hidden", i - 1))
                three(pe, banks[2 + i % 2][:], [lambda k: w3[0][:, k, h * P:(h + 1) * P], lambda k: w3[1][:, k, h * P:(h + 1) * P]],
                      moving(n), range(KC)).then_inc(s["up"], 1)

            if late:
                pe.wait_ge(w1_lo, 1)
                pe.wait_ge(w3_lo, 1)
            gate_up(0)
            gate_up(1)
            if not late:
                head_turn_pe(pe, s, "ffn", 1)
            else:
                pe.wait_ge(*s.after("xt_lo", 4))
                prep_late_pe(pe)
            for i in range(UNITS):
                if i + 2 < UNITS:
                    gate_up(i + 2)
                n, h = i // FB, i % FB
                pe.wait_ge(*s.after("hid_lo", i + 1))
                if late and n == 0:
                    pe.wait_ge(w2_lo, h // 2 + 1)
                for c in range(KC):
                    ins = three(pe, banks[4 + 2 * n + c][:],
                                [lambda k: w2[0][:, h, c * P:(c + 1) * P], lambda k: w2[1][:, h, c * P:(c + 1) * P]],
                                [lambda k: hid[i % 2][0][:], lambda k: hid[i % 2][1][:]], [0], first=h == 0, last=h == FB - 1)
                ins.then_inc(s["down"], 1)
                if i == FB:
                    finish_pe(pe, s, f_out, 0)
                if i == FB + 6 and nxt:
                    head_turn_pe(pe, nxt[1], nxt[0], 0)
            finish_pe(pe, s, f_out, 1)

        def ffn_act(act, s, nxt, late):
            for i in range(UNITS + 1):
                if i < UNITS:
                    act.wait_ge(*s.after("gate", i + 1))
                    if i >= 2:
                        act.wait_ge(*s.after("hidden", i - 1))
                    act.activation(f_silu[i % 2], banks[i % 2][:], ACT.Silu).then_inc(s["silu"], 1)
                if i == 0 and late:
                    prep_late_act(act)
                if i >= 1:
                    j = i - 1
                    act.wait_ge(*s.after("hidden", j + 1))
                    if j >= 2:
                        act.wait_ge(*s.after("down", j - 1))
                    act.activation(hid[j % 2][0][:], f_hid[j % 2], ACT.Copy).then_inc(s["hid_hi"], 1)
                if i == FB + 1:
                    finish_act(act, s, f_out, 1.0, 0, FB)
                if i == FB + 3 and nxt:
                    head_weights_act(act, nxt[1], nxt[0])
                if i == FB + 8 and early(nxt):
                    head_turn_act(act, nxt[1], nxt[0], 0)
            finish_act(act, s, f_out, 1.0, 1, UNITS)
            if nxt:
                if not early(nxt):
                    head_turn_act(act, nxt[1], nxt[0], 0)
                head_turn_act(act, nxt[1], nxt[0], 1)

        def ffn_pool(pool, s, nxt):
            if nxt:
                head_weights_pool(pool, nxt[1], nxt[0])
                for n in range(NHALF):
                    head_pool(pool, nxt[1], nxt[0], n)

        def ffn_dve(dve, s, nxt, late):
            if late:
                prep_late_dve(dve)
            for i in range(UNITS + 1):
                if i < UNITS:
                    dve.wait_ge(*s.after("up", i + 1))
                    dve.wait_ge(*s.after("silu", i + 1))
                    if i >= 2:
                        dve.wait_ge(*s.after("hid_lo", i - 1))
                    dve.tensor_tensor(f_hid[i % 2], banks[2 + i % 2][:], f_silu[i % 2], ALU.mult).then_inc(s["hidden"], 1)
                if i >= 1:
                    j = i - 1
                    dve.wait_ge(*s.after("hid_hi", j + 1))
                    if j >= 2:
                        dve.wait_ge(*s.after("down", j - 1))
                    dve.tensor_tensor(hid[j % 2][1][:], f_hid[j % 2], hid[j % 2][0][:].bitcast(F32), ALU.subtract)\
                       .then_inc(s["hid_lo"], 1)
                if i == FB + 2:
                    finish_dve(dve, s, 0)
                if i == FB + 3 and nxt:
                    head_stats(dve, nxt[1], 0, [s.after("x_done", 2)])
                if i == FB + 5 and nxt:
                    head_norm(dve, nxt[1], nxt[0], 0)
                if i == FB + 8 and early(nxt):
                    head_turn_dve(dve, nxt[1], nxt[0], 0)
            finish_dve(dve, s, 1)
            if nxt:
                head_stats(dve, nxt[1], 1, [s.after("x_done", 4)])
                if not early(nxt):
                    head_turn_dve(dve, nxt[1], nxt[0], 0)
                head_norm(dve, nxt[1], nxt[0], 1)
                head_turn_dve(dve, nxt[1], nxt[0], 1)

        UE = NHALF * KC
        at[0] = 0
        raw = [cut(EW + EB + ED) for _ in range(2)]
        m_bias = [cut(EB) for _ in range(2)]
        assert at[0] <= TB * 2 * D
        score_wide = [cut(T) for _ in range(2)]
        m_gate = [cut(HALF) for _ in range(2)]
        m_glu = [cut(HALF) for _ in range(2)]
        m_up = [cut(HALF) for _ in range(2)]
        m_hid = [cut(HALF) for _ in range(2)]
        m_scaled = [cut(HALF) for _ in range(2)]
        m_scores_t = cut(T)
        m_logits = cut(TB * (E + TOPK), TB, E + TOPK)
        m_top = cut(TB * 8, TB, 8)
        m_taken = cut(TB * 8, TB, 8)
        m_marked = cut(TB * (E + TOPK), TB, E + TOPK)
        m_exp = cut(TB * E, TB, E)
        m_chosen = cut(TB * E, TB, E)
        m_sum = cut(TB)
        m_scores = cut(TB * E, TB, E)
        assert at[0] <= OUT_AT
        at[0] = OUT_AT
        m_out = cut(KC * T, KC, T)
        MOE = NORM | dict.fromkeys("gate up clipped up_read glu product scaled hid_hi hid_lo down".split(), UE * E)
        MOE |= dict.fromkeys("logits centred exped scored scores_turned".split(), 1)
        MOE |= dict.fromkeys("raw_in0 raw_in1 wide_in0 wide_in1".split(), 16 * E // 2)
        MOE |= dict(logits_t=NHALF, logits_copied=NHALF, scores_copied=NHALF, scores_out=16)
        MOE |= dict(w_hi=E, w_lo=E, down_lo=E, out_copied=4, out_turned=4, x_done=4)

        def router_pe(pe, s):
            for n in range(NHALF):
                ins = three(pe, banks[4 + n][0:E, :], [lambda k: router_w[0][:, k, :], lambda k: router_w[1][:, k, :]],
                            moving(n), range(KC))
                ins.then_inc(s["logits_t"], 1)
            for b in range(TB):
                pe.wait_ge(*s.after("logits_copied", b // 4 + 1))
                ins = pe.transpose(banks[6][:, b * E:(b + 1) * E], m_scores_t[0:E, b * P:(b + 1) * P], ident[0:E, 0:E])
            ins.then_inc(s["logits"], 1)

        def scores_pe(pe, s):
            pe.wait_ge(*s.after("scored", 1))
            for b in range(TB):
                ins = pe.transpose(banks[4 + b // 4][0:E, (b % 4) * P:(b % 4 + 1) * P], m_scores[:, b, :], ident[:])
            ins.then_inc(s["scores_turned"], 1)

        def router_dve(dve, s):
            dve.memset(m_taken, SENTINEL)
            link(dve, "dve", dve.memset(m_logits[:, :, E:E + TOPK], SENTINEL))
            dve.wait_ge(*s.after("logits", 1))
            link(dve, "dve", dve.tensor_tensor(m_logits[:, :, 0:E], banks[6][:, 0:TB * E].rearrange("p (b e) -> p b e", b=TB),
                                               bcast(router_b[:], 1, TB), ALU.add))
            for b in range(TB):
                ins = dve.max(m_top[:, b, :], m_logits[:, b, 0:E])
            link(dve, "dve", ins)
            dve.tensor_tensor(m_exp, m_logits[:, :, 0:E], bcast(m_top[:, :, 0], 2, E), ALU.subtract).then_inc(s["centred"], 1)
            link(dve, "dve", dve.tensor_copy(m_taken[:, :, 0:TOPK], m_top[:, :, 0:TOPK]))
            for b in range(TB):
                ins = dve.match_replace(out=m_marked[:, b, :], in_to_replace=m_taken[:, b, :], in_values=m_logits[:, b, :],
                                        imm_value=TAKEN)
            link(dve, "dve", ins)
            link(dve, "dve", dve.tensor_tensor(m_chosen, m_marked[:, :, 0:E], m_logits[:, :, 0:E], ALU.not_equal))
            dve.wait_ge(*s.after("exped", 1))
            link(dve, "dve", dve.tensor_tensor(m_chosen, m_chosen, m_exp, ALU.mult))
            link(dve, "dve", dve.reduce_sum(m_sum, m_chosen, axis=AX_X))
            link(dve, "dve", dve.reciprocal(m_sum, m_sum))
            dve.tensor_tensor(m_scores, m_chosen, bcast(m_sum, 2, E), ALU.mult).then_inc(s["scored"], 1)

        def router_act(act, s):
            for n in range(NHALF):
                act.wait_ge(*s.after("logits_t", n + 1))
                act.activation(m_scores_t[0:E, n * HALF:(n + 1) * HALF], banks[4 + n][0:E, :], ACT.Copy)\
                   .then_inc(s["logits_copied"], 1)
            act.wait_ge(*s.after("centred", 1))
            act.activation(m_exp, m_exp, ACT.Exp).then_inc(s["exped"], 1)
            act.wait_ge(*s.after("scores_turned", 1))
            for n in range(NHALF):
                act.activation(m_scores_t[0:E, n * HALF:(n + 1) * HALF], banks[4 + n][0:E, :], ACT.Copy)\
                   .then_inc(s["scores_copied"], 1)

        def experts(eng, body):
            for e in (0, 1):
                body(e, e % 2, False)
            with eng.Fori(2, E - 2, 2) as e:
                body(e, 0, False)
                body(e + 1, 1, False)
            for e in (E - 2, E - 1):
                body(e, e % 2, e == E - 1)

        def behind(eng, s, name, value):
            if not isinstance(value, int) or value > 0:
                eng.wait_ge(*s.after(name, value))

        def moe_sync(sp, s, waits):
            for w in waits:
                sp.wait_ge(*w)

            weights = a["moe_w"].rearrange("(pair par) p w -> par pair p w", par=2)
            rows = score_rows.rearrange("(pair par) t -> par pair t", par=2)

            def load(pair, par):
                behind(sp, s, "down_lo", 2 * pair + par - 1)
                sp.dma_start(raw[par], weights[par][pair]).then_inc(s[f"raw_in{par}"], 16)

            def widen(pair, par):
                behind(sp, s, "scaled", UE * (2 * pair + par - 1))
                sp.dma_start(score_wide[par], rows[par][pair].partition_broadcast(P)).then_inc(s[f"wide_in{par}"], 16)

            load(0, 0)
            load(0, 1)
            sp.wait_ge(*s.after("scores_copied", NHALF))
            sp.dma_start(score_rows, m_scores_t[0:E, :]).then_inc(s["scores_out"], 16)
            sp.wait_ge(*s.after("scores_out", 16))
            widen(0, 0)
            widen(0, 1)
            with sp.Fori(1, E // 2) as pair:
                for par in range(2):
                    load(pair, par)
                    widen(pair, par)

        def moe_pe(pe, s, nxt):
            def gate_up(e, par, u):
                n, q = u // KC, u % KC
                if u == 0:
                    pe.wait_ge(*s.after("w_lo", e + 1))
                for part, ready, read in ((0, "gate", "clipped"), (1, "up", "up_read")):
                    behind(pe, s, read, UE * e + u - 1)
                    o = part * D + q * P
                    three(pe, banks[2 * part + u % 2][:],
                          [lambda k: wr[par][0][:, k * 2 * D + o:k * 2 * D + o + P],
                           lambda k: wr[par][1][:, k * 2 * D + o:k * 2 * D + o + P]],
                          moving(n), range(KC)).then_inc(s[ready], 1)

            def down(e, par, u, last):
                n, q = u // KC, u % KC
                if u == 0:
                    pe.wait_ge(*s.after("down_lo", e + 1))
                pe.wait_ge(*s.after("hid_lo", UE * e + u + 1))
                for c in range(KC):
                    o = EW + q * D + c * P
                    ins = three(pe, banks[4 + 2 * n + c][:],
                                [lambda k: wr[par][0][:, o:o + P], lambda k: wr[par][1][:, o:o + P]],
                                [lambda k: hid[u % 2][0][:], lambda k: hid[u % 2][1][:]], [0],
                                first=False, last=last and q == KC - 1)
                ins.then_inc(s["down"], 1)

            pe.wait_ge(*s.after("xt_lo", KC))
            gate_up(0, 0, 0)
            gate_up(0, 0, 1)
            head_turn_pe(pe, s, "moe", 1)
            pe.wait_ge(*s.after("xt_lo", 2 * KC))
            router_pe(pe, s)
            scores_pe(pe, s)
            pe.wait_ge(*s.after("scores_copied", NHALF))
            for n in range(NHALF):
                for c in range(KC):
                    pe.matmul(banks[4 + 2 * n + c][:], down_b[:, c * P:(c + 1) * P],
                              m_scores_t[0:E, n * HALF:(n + 1) * HALF], start=True, stop=False, skip_group_check=True)

            def body(e, par, last):
                for u in range(UE):
                    if u < 2:
                        gate_up(e, par, u + 2)
                    elif not last:
                        gate_up(e + 1, 1 - par, u - 2)
                    down(e, par, u, last)

            experts(pe, body)
            end_pe(pe, nxt, lambda n: finish_pe(pe, s, m_out, n))

        def split_hi(act, s, e, par):
            act.wait_ge(*s.after(f"raw_in{par}", 8 * (e - par) + 16))
            behind(act, s, "down", UE * (e - 1))
            act.activation(wr[par][0][:, 0:EW], raw[par][:, 0:EW], ACT.Copy)
            act.activation(wr[par][0][:, EW:], raw[par][:, EW + EB:], ACT.Copy).then_inc(s["w_hi"], 1)

        def split_lo(pool, s, e, par):
            pool.wait_ge(*s.after("w_hi", e + 1))
            behind(pool, s, "up_read", UE * (e - 1))
            pool.tensor_tensor(m_bias[par], raw[par][:, EW:EW + EB], bias_one[:], ALU.add)
            pool.tensor_tensor(wr[par][1][:, 0:EW], raw[par][:, 0:EW], wr[par][0][:, 0:EW].bitcast(F32), ALU.subtract)\
               .then_inc(s["w_lo"], 1)

        def split_down_lo(pool, s, e, par):
            pool.tensor_tensor(wr[par][1][:, EW:], raw[par][:, EW + EB:], wr[par][0][:, EW:].bitcast(F32), ALU.subtract)\
               .then_inc(s["down_lo"], 1)

        def low_part(dve, s, e, u):
            g = UE * e + u
            dve.wait_ge(*s.after("hid_hi", g + 1))
            behind(dve, s, "down", g - 1)
            dve.tensor_tensor(hid[u % 2][1][:], m_scaled[u % 2], hid[u % 2][0][:].bitcast(F32), ALU.subtract)\
               .then_inc(s["hid_lo"], 1)

        def moe_act(act, s, nxt):
            router_act(act, s)

            def body(e, par, last):
                for u in range(UE):
                    g = UE * e + u
                    act.wait_ge(*s.after("clipped", g + 1))
                    behind(act, s, "product", g - 1)
                    act.activation(m_glu[u % 2], m_gate[u % 2], ACT.Gelu_apprx_sigmoid).then_inc(s["glu"], 1)
                    if u == 1 and not last:
                        split_hi(act, s, e + 1, 1 - par)
                    act.wait_ge(*s.after("scaled", g + 1))
                    behind(act, s, "down", g - 1)
                    act.activation(hid[u % 2][0][:], m_scaled[u % 2], ACT.Copy).then_inc(s["hid_hi"], 1)

            experts(act, body)
            end_act(act, nxt, lambda n: finish_act(act, s, m_out, 0.5, n, UE * (E - 1) + KC * (n + 1)))

        def moe_dve(dve, s, nxt):
            router_dve(dve, s)

            def body(e, par, last):
                for u in range(UE):
                    g = UE * e + u
                    n, q = u // KC, u % KC
                    if u == 0:
                        dve.wait_ge(*s.after("w_lo", e + 1))
                    dve.wait_ge(*s.after("gate", g + 1))
                    behind(dve, s, "glu", g - 1)
                    dve.tensor_scalar(m_gate[u % 2], banks[u % 2][:], m_bias[par][:, q:q + 1], ALPHA_LIMIT, ALU.add, ALU.min)\
                       .then_inc(s["clipped"], 1)
                    dve.wait_ge(*s.after("up", g + 1))
                    dve.tensor_scalar(m_up[u % 2], banks[2 + u % 2][:], m_bias[par][:, KC + q:KC + q + 1], ALPHA_LIMIT + 1.0,
                                      ALU.add, ALU.min).then_inc(s["up_read"], 1)
                    if u >= 1:
                        low_part(dve, s, e, u - 1)
                    dve.wait_ge(*s.after("glu", g + 1))
                    dve.wait_ge(*s.after("up_read", g + 1))
                    behind(dve, s, "scaled", g - 1)
                    dve.scalar_tensor_tensor(m_hid[u % 2], m_up[u % 2], 1.0 - ALPHA_LIMIT, m_glu[u % 2], ALU.max, ALU.mult)\
                       .then_inc(s["product"], 1)
                low_part(dve, s, e, UE - 1)

            experts(dve, body)
            end_dve(dve, s, nxt, lambda n: finish_dve(dve, s, n))

        def moe_pool(pool, s, nxt):
            def body(e, par, last):
                pool.wait_ge(*s.after(f"wide_in{par}", 8 * (e - par) + 16))
                for u in range(UE):
                    g = UE * e + u
                    n = u // KC
                    pool.wait_ge(*s.after("product", g + 1))
                    behind(pool, s, "hid_hi", g - 1)
                    behind(pool, s, "hid_lo", g - 1)
                    pool.tensor_tensor(m_scaled[u % 2], m_hid[u % 2], score_wide[par][:, n * HALF:(n + 1) * HALF], ALU.mult)\
                        .then_inc(s["scaled"], 1)
                    if u == 1 and not last:
                        split_lo(pool, s, e + 1, 1 - par)
                    if u == 2 and not last:
                        split_down_lo(pool, s, e + 1, 1 - par)

            experts(pool, body)
            end_pool(pool, nxt)

        at[0] = 0
        qk_tok = cut(TB * 2 * D, TB, 2 * D)
        v_tok = cut(TB * HEADS * (HD + 1), TB, HEADS, HD + 1)
        stack_at = at[0]
        stacked = [cut(2 * GH * T // 2).bitcast(BF16).rearrange("p (s j t) -> p s j t", s=2, j=GH) for _ in range(2)]
        stack_tok = [cut(4 * GH * P // 2).bitcast(BF16).rearrange("p (t c) -> p t c", c=P) for _ in range(2)]
        stacked.append(stacked_xt[:].rearrange("p (s j t) -> p s j t", s=2, j=GH))
        rest = cut(4 * GH * HD, 4, GH, HD)
        shared = at[0]
        probs = [cut(GH * HALF, GH, HALF) for _ in range(2)]
        neg_tok = cut(TB * GH * STRIP // 2).bitcast(BF16).rearrange("p (t j c) -> p t j c", t=TB, j=GH)
        neg_rest = cut(TB * GH, TB, GH)
        o_wide = cut(HALF)
        at[0] = shared
        qkv_raw = cut(KC * 3 * D, KC, 3 * D)
        wo_raw = cut(KC * D, KC, D)
        affine = [cut(HALF) for _ in range(2)]
        head_sum, head_var, head_rstd = ([cut(BATCH * 2 * HEADS) for _ in range(2)] for _ in range(3))
        at[0] = stack_at + GH * T
        by_cos = [cut(BATCH * 2 * D) for _ in range(2)]
        by_sin = [cut(BATCH * 2 * D) for _ in range(2)]
        w_qkv = [wr[0][k][:].rearrange("p (c n) -> p c n", c=KC) for k in range(2)]
        w_out = [wr[1][k][:, 0:KC * D].rearrange("p (c n) -> p c n", c=KC) for k in range(2)]
        MAX_UNITS = [(b, c, c * HALF, min(HALF, (b + 1) * P - c * HALF)) for b in range(TB) for c in range(b // 4 + 1)]
        EXP_UNITS = [(n, k, max(n * HALF, k * P), (n + 1) * HALF - max(n * HALF, k * P))
                     for n in range(NHALF) for k in range(4 * (n + 1))]
        wide, narrow = ([u for u in MAX_UNITS if (u[3] == HALF) == full] for full in (True, False))
        MAX_UNITS = [(narrow if EXP_UNITS[u - 1][3] == HALF else wide).pop(0) for u in range(len(EXP_UNITS))]
        NU = len(MAX_UNITS)
        assert NU == len(EXP_UNITS)
        LATE = NU + 1
        STEPS = GROUPS * NU + LATE
        ATTN1 = dict.fromkeys([*NORM, *("w_in w_hi w_lo zeroed table projected parts tok proj scores "
                                        "tok_half maxed negated neg_turned shifted e_scores exped weighted o_copied o_turned o_done "
                                        "x_done split stack_turned stack_copied cosines cleared repeated").split()])
        ATTN0 = dict.fromkeys([*ATTN1, *("var2 rstd2 var3 squared rstd3 scaled bias_added normed2 turned2 a_hi a_lo wo_done "
                                         "rotated centred gained squares length").split()])

        def attn_load(sp, s, kind, waits):
            for w in waits:
                sp.wait_ge(*w)
            k = kind
            loads = [(qkv_raw, a[k + "_wqkv"].rearrange("(c p) n -> p c n", p=P)),
                     (qkv_b[:], a[k + "_bqkv"].partition_broadcast(P)),
                     (cosine[:], a[k + "_cos"].rearrange("(b p) f -> p b f", p=P)),
                     (sine[:], a[k + "_sin"].rearrange("(b p) f -> p b f", p=P))]
            if kind == "attn0":
                loads += [(wo_raw, a["wo"].rearrange("(c p) n -> p c n", p=P)), (out_b[:], a["bo"].partition_broadcast(P)),
                          (head_g[:], a["head_g"].partition_broadcast(P)), (head_b[:], a["head_b"].partition_broadcast(P)),
                          (in_gb[:], a["in_gb"])]
            for dst, src in loads:
                sp.dma_start(dst, src).then_inc(s["w_in"], 16)

        def loaded(kind):
            return 16 * (9 if kind == "attn0" else 4)

        def attn_pool(pool, s, kind, waits, nxt):
            for w in waits:
                pool.wait_ge(*w)
            for i in range(2):
                pool.memset(stack_tok[i][:, :, PARTS:P], 0.0).then_inc(s["zeroed"], 1)
            pool.memset(v_tok[:, :, :, HD:HD + 1], 1.0).then_inc(s["zeroed"], 1)
            pool.wait_ge(*s.after("zeroed", 3))
            pool.memset(stack_tok[1][:, :, PARTS:PARTS + SHIFT], 1.0).then_inc(s["zeroed"], 1)
            if kind == "attn0":
                pool.wait_ge(*s.after("squares", NHALF))
                pool.tensor_tensor(xnorm[:], xnorm[:], half_pos[:, 0:TB], ALU.pow).then_inc(s["length"], 1)
            nb = TB // BATCH
            for t in range(nb + 3):
                if t < nb:
                    rotate_parts(pool, s, kind, t)
                if kind == "attn0":
                    if 0 <= t - 3 < nb:
                        i = t - 3
                        pool.wait_ge(*s.after("scaled", i + 1))
                        pool.tensor_tensor(heads(i), heads(i), bcast(head_g[:], 1, BATCH * 2 * HEADS), ALU.mult)\
                            .then_inc(s["gained"], 1)
            pool.wait_ge(*s.after("split", 4))
            pool.memset(neg_tok[:, :, :, :], 0.0).then_inc(s["zeroed"], 1)
            for g in range(1, GROUPS):
                for step in range(4):
                    split(pool, "pool", s, g, step)
            if kind == "attn0":
                pool.wait_ge(*s.after("normed", TB))
                pool.tensor_tensor(x[:], x[:], bcast(out_b[:], 1, TB), ALU.add).then_inc(s["bias_added"], 1)
            if nxt:
                head_weights_pool(pool, nxt[1], nxt[0])
                for n in range(NHALF):
                    head_pool(pool, nxt[1], nxt[0], n)

        def heads(i):
            return qk_tok[:, BATCH * i:BATCH * (i + 1), :].rearrange("p t (h d) -> p (t h) d", d=HD)

        def rotate_parts(pool, s, kind, i):
            pool.wait_ge(*s.after("table", 1))
            pool.wait_ge(*s.after("projected", BATCH * (i + 1)))
            if i >= 2:
                pool.wait_ge(*(s.after("var3", i - 1) if kind == "attn0" else s.after("tok", i - 1)))
            if kind == "attn0":
                times(pool, kind, i, by_cos, cosine)
            times(pool, kind, i, by_sin, sine).then_inc(s["parts"], 1)

        def times(eng, kind, i, dst, table):
            pairs_of, at_f, shape = (("p (h f two) -> p h f two", 3, [P, 2 * HEADS, HD // 2, 2]) if kind == "attn0" else
                                     ("p (h two f) -> p h two f", 1, [P, 2 * HEADS, 2, HD // 2]))
            for t in range(BATCH):
                b = BATCH * i + t
                ins = eng.tensor_tensor(dst[i % 2][:, t * 2 * D:(t + 1) * 2 * D].rearrange(pairs_of, two=2, f=HD // 2),
                                        qk_tok[:, b, :].rearrange(pairs_of, two=2, f=HD // 2),
                                        table[:, b, :].unsqueeze(1).unsqueeze(at_f).broadcast_to(shape), ALU.mult)
            return ins

        def split(eng, name, s, g, step):
            n, side = step // 2, step % 2
            count = 4 * g + step
            tile = stack_tok[side]
            block = lambda n: tile[:, :, n * HD:(n + 1) * HD]
            by_head = "p (t j) d -> p t j d"
            src = qk_tok[:, 4 * n:4 * n + 4, side * D + GH * HD * g:side * D + GH * HD * (g + 1)]\
                .rearrange("p t (j d) -> p t j d", j=GH)
            mid, low = ((3, 5), (1, 2))[side]
            if g == 0:
                eng.wait_ge(*s.after("tok", TB // BATCH // 2 * (n + 1)))
                eng.wait_ge(*s.after("zeroed", 4))
            if count >= 2:
                eng.wait_ge(*s.after("stack_turned", 2 * (count - 1)))
            link(eng, name, eng.tensor_copy(block(0).rearrange(by_head, j=GH), src))
            link(eng, name, eng.tensor_tensor(rest, src, block(0).rearrange(by_head, j=GH), ALU.subtract))
            link(eng, name, eng.tensor_copy(block(mid).rearrange(by_head, j=GH), rest))
            eng.tensor_tensor(block(low).rearrange(by_head, j=GH), rest, block(mid).rearrange(by_head, j=GH), ALU.subtract).then_inc(s["split"], 1)
            if g != 1:
                repeat_parts(eng, s, g, step, False)

        def repeat_parts(eng, s, g, step, act):
            side = step % 2
            block = lambda n: stack_tok[side][:, :, n * HD:(n + 1) * HD]
            eng.wait_ge(*s.after("split", 4 * g + step + 1))
            if 4 * g + step:
                eng.wait_ge(*s.after("repeated", 3 * (4 * g + step)))
            for to, of in (((1, 0), (2, 0), (4, 3)), ((3, 0), (5, 0), (4, 1)))[side]:
                (eng.activation(block(to), block(of), ACT.Copy) if act else eng.tensor_copy(block(to), block(of)))\
                    .then_inc(s["repeated"], 1)

        def affine_act(act, s, n):
            for c in range(KC):
                i = KC * n + c
                act.wait_ge(*s.after("turned", i + 1))
                for t in range(2):
                    if i >= 1:
                        act.wait_ge(*s.after("xt_lo", 2 * (i - 1) + t + 1))
                    link(act, "act", act.activation(affine[t], banks[4 + i][:], ACT.Identity, scale=in_gb[:, 2 * t, c:c + 1],
                                                    bias=in_gb[:, 2 * t + 1, c:c + 1]))
                    if n == 1:
                        act.wait_ge(*s.after("proj", TB // 2))
                    act.activation(xt_hi[:, c, t * HALF:(t + 1) * HALF], affine[t], ACT.Copy).then_inc(s["xt_hi"], 1)

        def affine_lo(dve, s, n):
            for c in range(KC):
                for t in range(2):
                    dve.wait_ge(*s.after("xt_hi", 2 * (KC * n + c) + t + 1))
                    q = slice(t * HALF, (t + 1) * HALF)
                    dve.tensor_tensor(xt_lo[:, c, q], affine[t], xt_hi[:, c, q].bitcast(F32), ALU.subtract)\
                       .then_inc(s["xt_lo"], 1)

        def attn_act(act, s, kind, nxt):
            if kind == "attn0":
                for i in range(TB // BATCH + 1):
                    if i < TB // BATCH:
                        act.wait_ge(*s.after("centred", i + 1))
                        act.activation(by_cos[i % 2], qk_tok[:, BATCH * i:BATCH * (i + 1), :].rearrange("p t n -> p (t n)"),
                                       ACT.Square).then_inc(s["squared"], 1)
                    if i >= 1:
                        act.wait_ge(*s.after("var3", i))
                        act.activation(head_rstd[(i - 1) % 2], head_var[(i - 1) % 2], ACT.Sqrt).then_inc(s["rstd3"], 1)
            for k in range(4):
                stack_copy(act, s, 0, 2 * k, True)
            for m in range(STEPS):
                g, u = m // NU, m % NU
                if u == 2 and g >= 2:
                    o_copy(act, s, g - 2, 1)
                if u == 6 and g >= 1:
                    o_copy(act, s, g - 1, 0)
                if u == 4 and g == GROUPS and nxt:
                    head_weights_act(act, nxt[1], nxt[0])
                if u == 8 and g == GROUPS and kind == "attn0":
                    outputs_hi(act, s, 0)
                unit = m - LATE
                if unit >= 0:
                    n, k, q0, w = EXP_UNITS[unit % NU]
                    for pair in range(2):
                        act.wait_ge(*s.after("e_scores", 2 * unit + pair + 1))
                        if pair == 0 and unit >= 2:
                            act.wait_ge(*s.after("weighted", unit - 1))
                        act.activation(probs[unit % 2][:, 2 * pair:2 * pair + 2, 0:w], pairs[pair][:, :, 0:w], ACT.Exp,
                                       scale=HD ** -0.5).then_inc(s["exped"], 1)
                        if u == 0 and 1 <= g <= GROUPS and pair == 0:
                            shift(act, s, g - 1, (2, 3), True)
                elif u == 0 and g == 1:
                    shift(act, s, 0, (2, 3), True)
                if g + 1 < GROUPS and 3 <= u < 11 and not dve_copies(g, u):
                    stack_copy(act, s, g + 1, u - 3, True)
                if m in (0, 2, 5, 7):
                    repeat_parts(act, s, 1, (0, 2, 5, 7).index(m), True)
            o_copy(act, s, GROUPS - 1, 1)
            if nxt:
                head_turn_act(act, nxt[1], nxt[0], 0)
            if kind == "attn0":
                outputs_hi(act, s, 1)
            if nxt:
                head_turn_act(act, nxt[1], nxt[0], 1)

        def outputs_hi(act, s, n):
            for c in range(KC):
                act.wait_ge(*s.after("turned2", KC * n + c + 1))
                act.activation(xt_hi[:, c, n * HALF:(n + 1) * HALF], banks[KC * n + c][:], ACT.Copy).then_inc(s["a_hi"], 1)

        def o_copy(act, s, g, n):
            act.wait_ge(*s.after("weighted", g * NU + (4 if n == 0 else NU)))
            if g or n:
                act.wait_ge(*s.after("o_turned", 2 * g + n))
            act.activation(o_wide, banks[6][:], ACT.Copy).then_inc(s["o_copied"], 1)

        def max_bank(job):
            ahead = 6 if job < NU * GH else 2
            return job % ahead, ahead

        def dve_copies(g, u):
            return g >= 1 and EXP_UNITS[u - 1][3] == HALF and MAX_UNITS[u][3] <= HALF // 2

        def stack_copy(eng, s, g, i, act):
            step, pair = i // 2, i % 2
            n, side = step // 2, step % 2
            q = slice(n * HALF + pair * 2 * P, n * HALF + (pair + 1) * 2 * P)
            dst = stacked[g % 3][:, side, :, q].rearrange("p j (t c) -> p t j c", c=P)
            src = banks[7 if g else i][:].bitcast(BF16).rearrange("p (t j c) -> p t j c", t=2, j=GH)
            eng.wait_ge(*s.after("stack_turned", 8 * g + i + 1))
            for t in range(2):
                args = (dst[:, t, :, :], src[:, t, :, :])
                ins = eng.activation(*args, ACT.Copy) if act else eng.tensor_copy(*args)
            ins.then_inc(s["stack_copied"], 1)

        def norm_again(dve, s, n):
            mine = slice(4 * n, 4 * n + 4)
            dve.wait_ge(*s.after("normed", 4 * (n + 1)))
            for b in range(4 * n, 4 * n + 4):
                ins = dve.bn_stats(stats[:, b, :], xn[:, b, :])
            link(dve, "dve", ins)
            for b in range(4 * n, 4 * n + 4):
                ins = dve.bn_aggr(meanvar[:, b, :], stats[:, b, :])
            link(dve, "dve", ins)
            dve.tensor_scalar(vareps[:, mine], meanvar[:, mine, 1], EPS, None, ALU.add).then_inc(s["var2"], 1)
            link(dve, "dve", dve.tensor_tensor(xnorm[:, mine], meanvar[:, mine, 0], meanvar[:, mine, 0], ALU.mult))
            link(dve, "dve", dve.tensor_tensor(xnorm[:, mine], xnorm[:, mine], meanvar[:, mine, 1], ALU.add))
            dve.tensor_scalar(xnorm[:, mine], xnorm[:, mine], D * HD ** -0.5, None, ALU.mult).then_inc(s["squares"], 1)
            dve.wait_ge(*s.after("rstd2", n + 1))
            for b in range(4 * n, 4 * n + 4):
                dve.tensor_scalar(xn[:, b, :], xn[:, b, :], meanvar[:, b, 0:1], rstd[:, b:b + 1],
                                  ALU.subtract, ALU.mult).then_inc(s["normed2"], 1)

        def attn_dve(dve, s, kind, nxt):
            if kind == "attn0":
                take(dve, s, 0)
                dve.wait_ge(*s.after("w_in", loaded(kind)))
                dve.wait_ge(*s.after("length", 1))
                dve.tensor_tensor(cosine[:], cosine[:], bcast(xnorm[:], 2, HD // 2), ALU.mult)
                dve.tensor_tensor(sine[:], sine[:], bcast(xnorm[:], 2, HD // 2), ALU.mult).then_inc(s["table"], 1)
                take(dve, s, 1)
                affine_lo(dve, s, 1)
            else:
                dve.wait_ge(*s.after("w_in", loaded(kind)))
                dve.memset(xnorm[:], 1.0).then_inc(s["table"], 1)
            nb = TB // BATCH
            for t in range(nb + (4 if kind == "attn0" else 1)):
                if t < nb and (t >= 2 or kind != "attn0"):
                    take(dve, s, t)
                if t < nb and kind != "attn0":
                    dve.wait_ge(*s.after("projected", BATCH * (t + 1)))
                    times(dve, kind, t, by_cos, cosine).then_inc(s["cosines"], 1)
                if 0 <= t - 1 < nb:
                    rotate(dve, s, kind, t - 1)
                if kind == "attn0":
                    if 0 <= t - 2 < nb:
                        head_variance(dve, s, t - 2)
                    if 0 <= t - 3 < nb:
                        i = t - 3
                        dve.wait_ge(*s.after("rstd3", i + 1))
                        dve.tensor_tensor(heads(i), heads(i), bcast(head_rstd[i % 2], 2, HD), ALU.mult).then_inc(s["scaled"], 1)
                    if 0 <= t - 4 < nb:
                        add_head_bias(dve, s, t - 4)
                        if t - 4 == nb // 2 - 1:
                            split(dve, "dve", s, 0, 0)
                            split(dve, "dve", s, 0, 1)
            if kind != "attn0":
                split(dve, "dve", s, 0, 0)
                split(dve, "dve", s, 0, 1)
            for k in range(4):
                if k < 2:
                    split(dve, "dve", s, 0, 2 + k)
                stack_copy(dve, s, 0, 2 * k + 1, False)
            link(dve, "dve", dve.memset(row_max[:, :, :, 1], SENTINEL))

            def split_outputs(n):
                for c in range(KC):
                    i = KC * n + c
                    dve.wait_ge(*s.after("a_hi", i + 1))
                    q = slice(n * HALF, (n + 1) * HALF)
                    dve.tensor_tensor(xt_lo[:, c, q], banks[i][:], xt_hi[:, c, q].bitcast(F32), ALU.subtract).then_inc(s["a_lo"], 1)

            def finish(n):
                if kind == "attn0":
                    dve.wait_ge(*s.after("bias_added", 1))
                dve.wait_ge(*s.after("o_done", 2 * GROUPS - 1 + n))
                for i in (2 * n, 2 * n + 1):
                    v = slice(2 * i, 2 * i + 2)
                    if kind == "attn0":
                        dve.wait_ge(*s.after("wo_done", i + 1))
                    added = banks[i + 4 * n][:].rearrange("p (b d) -> p b d", b=2) if kind == "attn0" else xn[:, v, :]
                    dve.tensor_tensor(x[:, v, :], added, x[:, v, :], ALU.add).then_inc(s["x_done"], 1)

            for m in range(STEPS):
                g, u = m // NU, m % NU
                if u == 0 and 2 <= g <= GROUPS:
                    normalise(dve, s, g - 2, 0)
                if g == GROUPS:
                    if u == 7:
                        normalise(dve, s, g - 1, 0)
                    if u == 8 and kind == "attn0":
                        split_outputs(0)
                    if u == (10 if kind == "attn0" else 8):
                        finish(0)
                        if nxt:
                            head_stats(dve, nxt[1], 0, [s.after("x_done", 2)])
                    if u == 11 and nxt:
                        head_norm(dve, nxt[1], nxt[0], 0)
                if u == 3 and g >= 2:
                    normalise(dve, s, g - 2, 1)
                if m == NU:
                    dve.wait_ge(*s.after("stack_copied", 8))
                    dve.memset(banks[6], 0.0).then_inc(s["cleared"], 1)
                if g < GROUPS:
                    b, c, k0, w = MAX_UNITS[u]
                    for j in range(GH):
                        job = m * GH + j
                        dve.wait_ge(*s.after("scores", job + 1))
                        dve.reduce_max(row_max[:, b, GH * g + j, c:c + 1], banks[max_bank(job)[0]][:, 0:w], axis=AX_X)\
                           .then_inc(s["maxed"], 1)
                        if u == 0 and g >= 1 and j == 1:
                            shift(dve, s, g - 1, (0, 1), False)
                elif u == 0 and g == GROUPS:
                    shift(dve, s, g - 1, (0, 1), False)
                if g + 1 < GROUPS and 3 <= u < 11 and dve_copies(g, u):
                    stack_copy(dve, s, g + 1, u - 3, False)
                if u == NU - 1 and g < GROUPS:
                    dve.wait_ge(*s.after("maxed", (g + 1) * NU * GH))
                    hs = slice(GH * g, GH * (g + 1))
                    link(dve, "dve", dve.tensor_tensor(group_max[:], row_max[:, :, hs, 0], row_max[:, :, hs, 1], ALU.max))
                    if g >= 1:
                        dve.wait_ge(*s.after("neg_turned", g))
                    else:
                        dve.wait_ge(*s.after("zeroed", 5))
                    part = lambda k: neg_tok[:, :, :, k]
                    link(dve, "dve", dve.tensor_scalar(part(0), group_max[:], -1.0, None, ALU.mult))
                    link(dve, "dve", dve.scalar_tensor_tensor(neg_rest, group_max[:], -1.0, part(0), ALU.mult, ALU.subtract))
                    link(dve, "dve", dve.tensor_copy(part(1), neg_rest))
                    dve.tensor_tensor(part(2), neg_rest, part(1), ALU.subtract).then_inc(s["negated"], 1)
            normalise(dve, s, GROUPS - 1, 1)
            if nxt:
                head_turn_dve(dve, nxt[1], nxt[0], 0)
            if kind == "attn0":
                split_outputs(1)
            finish(1)
            if nxt:
                head_stats(dve, nxt[1], 1, [s.after("x_done", 4)])
                head_norm(dve, nxt[1], nxt[0], 1)
                head_turn_dve(dve, nxt[1], nxt[0], 1)

        def shift(eng, s, g, heads_of, act):
            eng.wait_ge(*s.after("neg_turned", g + 1))
            for j in heads_of:
                args = (stacked[g % 3][PARTS:P, 0, j, :], banks[7][j * STRIP:(j + 1) * STRIP, :].bitcast(BF16))
                (eng.activation(*args, ACT.Copy) if act else eng.tensor_copy(*args)).then_inc(s["shifted"], 1)

        def normalise(dve, s, g, n):
            dve.wait_ge(*s.after("o_turned", 2 * g + n + 1))
            o = banks[7][:].rearrange("p (b j d) -> p b j d", b=4, j=GH)
            link(dve, "dve", dve.reciprocal(inv_den[:], o[:, :, :, HD]))
            dst = xn[:, 4 * n:4 * n + 4, GH * HD * g:GH * HD * (g + 1)].rearrange("p b (j d) -> p b j d", j=GH)
            dve.tensor_tensor(dst, o[:, :, :, 0:HD], bcast(inv_den[:], 3, HD), ALU.mult).then_inc(s["o_done"], 1)

        def take(dve, s, i):
            hv = "p (h d) -> p h d"
            for b in range(BATCH * i, BATCH * (i + 1)):
                bank_q, bank_kv = banks[2 * (b % 2)], banks[2 * (b % 2) + 1]
                dve.wait_ge(*s.after("proj", b + 1))
                dve.tensor_tensor(qk_tok[:, b, 0:D], bank_q[:, 0:D], qkv_b[:, 0:D], ALU.add)
                dve.tensor_tensor(qk_tok[:, b, D:2 * D], bank_kv[:, 0:D], qkv_b[:, D:2 * D], ALU.add)
                dve.tensor_tensor(v_tok[:, b, :, 0:HD], bank_kv[:, D:2 * D].rearrange(hv, d=HD),
                                  qkv_b[:, 2 * D:3 * D].rearrange(hv, d=HD), ALU.add).then_inc(s["projected"], 1)

        def rotate(dve, s, kind, i):
            if kind != "attn0":
                dve.wait_ge(*s.after("cosines", i + 1))
            dve.wait_ge(*s.after("parts", i + 1))
            if kind == "attn0":
                v = lambda t: t.rearrange("p h (f two) -> p h f two", two=2)
                first, second = (lambda t: t[:, :, :, 0]), (lambda t: t[:, :, :, 1])
            else:
                v = lambda t: t.rearrange("p h (two f) -> p h two f", two=2)
                first, second = (lambda t: t[:, :, 0, :]), (lambda t: t[:, :, 1, :])
            c, sn = (v(t[i % 2].rearrange("p (h d) -> p h d", d=HD)) for t in (by_cos, by_sin))
            done = "rotated" if kind == "attn0" else "tok_half"
            dve.tensor_tensor(first(v(heads(i))), first(c), second(sn), ALU.subtract).then_inc(s[done], 1)
            if kind != "attn0":
                dve.tensor_tensor(second(v(heads(i))), first(sn), second(c), ALU.add).then_inc(s["tok"], 1)
                return
            dve.tensor_tensor(second(v(heads(i))), first(sn), second(c), ALU.add).then_inc(s["rotated"], 1)
            dve.wait_ge(*s.after("rotated", 2 * (i + 1)))
            link(dve, "dve", dve.reduce_sum(head_sum[i % 2], heads(i), axis=AX_X))
            dve.scalar_tensor_tensor(heads(i), bcast(head_sum[i % 2], 2, HD), -1.0 / HD, heads(i), ALU.mult, ALU.add)\
               .then_inc(s["centred"], 1)

        def head_variance(dve, s, i):
            dve.wait_ge(*s.after("squared", i + 1))
            if i >= 2:
                dve.wait_ge(*s.after("rstd3", i - 1))
            link(dve, "dve", dve.reduce_sum(head_var[i % 2], by_cos[i % 2].rearrange("p (h d) -> p h d", d=HD), axis=AX_X))
            link(dve, "dve", dve.tensor_scalar(head_var[i % 2], head_var[i % 2], 1.0 / HD, EPS, ALU.mult, ALU.add))
            dve.reciprocal(head_var[i % 2], head_var[i % 2]).then_inc(s["var3"], 1)

        def add_head_bias(dve, s, i):
            dve.wait_ge(*s.after("gained", i + 1))
            dve.tensor_tensor(heads(i), heads(i), bcast(head_b[:], 1, BATCH * 2 * HEADS), ALU.add).then_inc(s["tok"], 1)

        def attn_pe(pe, s, kind, nxt):
            def project(b):
                par = b % 2
                if kind == "attn0":
                    pe.wait_ge(*s.after("xt_lo", 4 * (b // 4 + 1)))
                    q0, kv0 = (b % 4) * P, HALF + (b % 4) * P
                else:
                    pe.wait_ge(*s.after("xt_lo", 2 * (b // 4 + 1)))
                    q0 = kv0 = b * P
                pe.wait_ge(*s.after("w_lo", 1))
                if b >= 2:
                    pe.wait_ge(*s.after("projected", b - 1))
                three(pe, banks[2 * par][:, 0:D], [lambda k: xt_hi[:, k, q0:q0 + P], lambda k: xt_lo[:, k, q0:q0 + P]],
                      [lambda k: w_qkv[0][:, k, 0:D], lambda k: w_qkv[1][:, k, 0:D]], range(KC))
                three(pe, banks[2 * par + 1][:], [lambda k: xt_hi[:, k, kv0:kv0 + P], lambda k: xt_lo[:, k, kv0:kv0 + P]],
                      [lambda k: w_qkv[0][:, k, D:3 * D], lambda k: w_qkv[1][:, k, D:3 * D]], range(KC)).then_inc(s["proj"], 1)

            def turn_stack(g, i):
                step, pair = i // 2, i % 2
                side = step % 2
                count = 4 * g + step
                pe.wait_ge(*s.after("split", count + 1))
                pe.wait_ge(*s.after("repeated", 3 * (count + 1)))
                if g >= 3 and i == 0:
                    pe.wait_ge(*s.after("o_done", 2 * (g - 2)))
                if g:
                    pe.wait_ge(*s.after("stack_copied", 8 * g + i))
                dst = banks[7 if g else i][:].bitcast(BF16)
                for t in range(2 * GH):
                    ins = pe.transpose(dst[:, t * P:(t + 1) * P], stack_tok[side][:, 2 * GH * pair + t, :], ident_b[:])
                ins.then_inc(s["stack_turned"], 1)

            for b in range(TB):
                if b == 2:
                    head_turn_pe(pe, s, kind, 1)
                project(b)
            pe.wait_ge(*s.after("projected", TB))
            for i in range(8):
                turn_stack(0, i)
            pe.wait_ge(*s.after("stack_copied", 8))

            def max_scores(m, heads_of):
                g, u = m // NU, m % NU
                b, c, k0, w = MAX_UNITS[u]
                if u == 0:
                    pe.wait_ge(*s.after("stack_copied", 8 * (g + 1)))
                for j in heads_of:
                    job = m * GH + j
                    bank, ahead = max_bank(job)
                    if job >= ahead:
                        pe.wait_ge(*s.after("maxed", job - ahead + 1))
                    diagonal = k0 + w == (b + 1) * P
                    ins = pe.matmul(banks[bank][:, 0:w], stacked[g % 3][0:PARTS, 0, j, b * P:(b + 1) * P],
                                    stacked[g % 3][0:PARTS, 1, j, k0:k0 + w], start=True, stop=not diagonal)
                    if diagonal:
                        ins = pe.matmul(banks[bank][:, w - P:w], ident_b[:], mask_qk[:], start=False, stop=True)
                    ins.then_inc(s["scores"], 1)

            def exp_scores(unit, pair):
                g = unit // NU
                n, k, q0, w = EXP_UNITS[unit % NU]
                if unit >= 1:
                    pe.wait_ge(*s.after("exped", 2 * unit + pair - 1))
                diagonal = q0 == k * P
                for i in range(2):
                    j = 2 * pair + i
                    dst = pairs[pair][:, i, :]
                    ins = pe.matmul(dst[:, 0:w], stacked[g % 3][0:PARTS + SHIFT, 1, j, k * P:(k + 1) * P],
                                    stacked[g % 3][0:PARTS + SHIFT, 0, j, q0:q0 + w], start=True, stop=not diagonal)
                    if diagonal:
                        ins = pe.matmul(dst[:, 0:P], ident_b[:], mask_kq[:], start=False, stop=True)
                ins.then_inc(s["e_scores"], 1)

            def weigh(unit):
                g = unit // NU
                n, k, q0, w = EXP_UNITS[unit % NU]
                if unit == 0:
                    pe.wait_ge(*s.after("cleared", 1))
                if k == 0 and (g or n):
                    pe.wait_ge(*s.after("o_copied", 2 * g + n))
                pe.wait_ge(*s.after("exped", 2 * (unit + 1)))
                for j in range(GH):
                    ins = pe.matmul(banks[6][j * STRIP:j * STRIP + HD + 1, q0 - n * HALF:HALF], v_tok[:, k, GH * g + j, :],
                                    probs[unit % 2][:, j, 0:w], start=k == 0, stop=k == 4 * n + 3, tile_position=(0, j * STRIP),
                                    skip_group_check=True)
                ins.then_inc(s["weighted"], 1)

            def turn_max(g):
                pe.wait_ge(*s.after("negated", g + 1))
                if g + 1 < GROUPS:
                    pe.wait_ge(*s.after("stack_copied", 8 * (g + 2)))
                if g >= 1:
                    pe.wait_ge(*s.after("o_done", 2 * g - 1))
                dst = banks[7][:].bitcast(BF16)
                for b in range(TB):
                    ins = pe.transpose(dst[:, b * P:(b + 1) * P], neg_tok[:, b, :, :].rearrange("p j c -> p (j c)"), ident_b[:])
                ins.then_inc(s["neg_turned"], 1)

            def turn_o(g, n):
                pe.wait_ge(*s.after("o_copied", 2 * g + n + 1))
                pe.wait_ge(*s.after("shifted", GH * min(GROUPS, g + 1 + n)))
                pe.wait_ge(*s.after("stack_copied", 8 * min(GROUPS, g + 3)))
                if g or n:
                    pe.wait_ge(*s.after("o_done", 2 * g + n))
                for b in range(4):
                    ins = pe.transpose(banks[7][:, b * P:(b + 1) * P], o_wide[:, b * P:(b + 1) * P], ident[:])
                ins.then_inc(s["o_turned"], 1)

            def turn_outputs(n):
                pe.wait_ge(*s.after("o_done", 2 * GROUPS - 1 + n))
                for c in range(KC):
                    for b in range(4):
                        ins = pe.transpose(banks[KC * n + c][:, b * P:(b + 1) * P], xn[:, 4 * n + b, c * P:(c + 1) * P], ident[:])
                    ins.then_inc(s["turned2"], 1)

            def project_outputs(n):
                pe.wait_ge(*s.after("a_lo", KC * (n + 1)))
                pe.wait_ge(*s.after("w_lo", 2))
                for b in range(4 * n, 4 * n + 4):
                    q = slice(b * P, (b + 1) * P)
                    ins = three(pe, banks[b // 2 + 4 * n][:, (b % 2) * D:(b % 2 + 1) * D],
                                [lambda k: xt_hi[:, k, q], lambda k: xt_lo[:, k, q]],
                                [lambda k: w_out[0][:, k, :], lambda k: w_out[1][:, k, :]], range(KC))
                    if b % 2:
                        ins.then_inc(s["wo_done"], 1)

            for m in range(STEPS):
                g, u = m // NU, m % NU
                unit = m - LATE
                for pair in range(2):
                    if g < GROUPS:
                        max_scores(m, (2 * pair, 2 * pair + 1))
                    if unit >= 0:
                        if unit % NU == 0 and pair == 0:
                            pe.wait_ge(*s.after("shifted", GH * (unit // NU + 1)))
                        exp_scores(unit, pair)
                    if unit >= 1 and pair == (0 if g < GROUPS else 1):
                        weigh(unit - 1)
                    if u == 0 and 1 <= g <= GROUPS and pair == 0:
                        turn_max(g - 1)
                if g + 1 < GROUPS and 3 <= u < 11:
                    turn_stack(g + 1, u - 3)
                if u == 2 and g >= 2:
                    turn_o(g - 2, 1)
                if u == (11 if g < GROUPS else 6) and g >= 1:
                    turn_o(g - 1, 0)
                if g == GROUPS and kind == "attn0":
                    if u == 7:
                        turn_outputs(0)
                    if u == 9:
                        project_outputs(0)
            weigh(GROUPS * NU - 1)
            if nxt:
                head_turn_pe(pe, nxt[1], nxt[0], 0)
            turn_o(GROUPS - 1, 1)
            if kind == "attn0":
                turn_outputs(1)
                project_outputs(1)

        totals = {"ffn": FFN, "moe": MOE, "attn0": ATTN0, "attn1": ATTN1}
        plan, run = [], {}
        for kind in stages:
            run[kind] = Sems(kind, totals[kind], run.get(kind))
            plan.append((kind, run[kind]))
        assert plan[0][0] == "ffn"
        following = plan[1:] + [None]
        x_ready = [[(x_loaded, 16)]] + [[s.after("x_done", 4)] for _, s in plan]
        load_after = [x_ready[i - 1] if i and (plan[i - 1][0] == "ffn" or plan[i][0][:4] == "attn") else x_ready[i]
                      for i in range(len(plan))]
        for i in range(1, len(plan)):
            if plan[i][0] == "moe" and plan[i - 1][0][:4] == "attn":
                load_after[i] = [plan[i - 1][1].after("split", 4 * GROUPS)]
        load_after[1] = [(w2_lo, 4), (consts, 6)]
        stored = sem("stored")

        block = ctx.enter_context(nc.Block())

        @block.sync
        def _(sp):
            load_sync(sp)
            for i, (kind, s) in enumerate(plan):
                if kind == "moe":
                    moe_sync(sp, s, load_after[i])
                if kind[:4] == "attn":
                    attn_load(sp, s, kind, load_after[i])
            for w in x_ready[-1]:
                sp.wait_ge(*w)
            sp.dma_start(out.rearrange("(b p) d -> p b d", p=P), x[:]).then_inc(stored, 16)
            sp.wait_ge(stored, 16)

        first = plan[0][1]

        @block.scalar
        def _(act):
            load_act(act)
            prep_act(act)
            for n in range(NHALF):
                head_turn_act(act, first, "ffn", n)
            for i, (kind, s) in enumerate(plan):
                if kind == "ffn":
                    ffn_act(act, s, following[i], i == 0)
                if kind == "moe":
                    moe_act(act, s, following[i])
                if kind[:4] == "attn":
                    attn_act(act, s, kind, following[i])

        @block.gpsimd
        def _(pool):
            prep_pool(pool)
            pool.wait_ge(pool_consts, 4)
            for n in range(NHALF):
                head_pool(pool, first, "ffn", n)
            prep_late_pool(pool)
            for i, (kind, s) in enumerate(plan):
                if kind == "ffn":
                    ffn_pool(pool, s, following[i])
                if kind == "moe":
                    moe_pool(pool, s, following[i])
                if kind[:4] == "attn":
                    attn_pool(pool, s, kind, x_ready[i], following[i])

        @block.vector
        def _(dve):
            for n in range(NHALF):
                head_stats(dve, first, n, x_ready[0])
            for n in range(NHALF):
                head_norm(dve, first, "ffn", n)
            prep_w3_dve(dve)
            for n in range(NHALF):
                head_turn_dve(dve, first, "ffn", n)
            for i, (kind, s) in enumerate(plan):
                if kind == "ffn":
                    ffn_dve(dve, s, following[i], i == 0)
                if kind == "moe":
                    moe_dve(dve, s, following[i])
                if kind[:4] == "attn":
                    attn_dve(dve, s, kind, following[i])

        @block.tensor
        def _(pe):
            pe.wait_ge(ident_loaded, 16)
            for n in range(NHALF):
                head_turn_pe(pe, first, "ffn", n)
            for i, (kind, s) in enumerate(plan):
                if kind == "ffn":
                    ffn_pe(pe, s, following[i], i == 0)
                if kind == "moe":
                    moe_pe(pe, s, following[i])
                if kind[:4] == "attn":
                    attn_pe(pe, s, kind, following[i])


def causal_masks():
    q = np.arange(P)
    m = np.where(q[None, :] > q[:, None], np.float32(MASKED), np.float32(0.0)).astype(np.float32)
    return m, np.ascontiguousarray(m.T)


def rotations(freqs):
    angle = np.arange(T, dtype=np.float32)[:, None] * freqs.astype(np.float32)[None, :]
    return np.cos(angle).astype(np.float32), np.sin(angle).astype(np.float32)


def expert_rows(i):
    g = i["L1_ffn_gate_up_proj"].reshape(E, KC, P, D, 2).transpose(0, 2, 1, 4, 3).reshape(E, P, EW)
    b = i["L1_ffn_gate_up_proj_bias"].reshape(E, KC, P, 2).transpose(0, 2, 3, 1).reshape(E, P, EB)
    d = i["L1_ffn_down_proj"].reshape(E, KC, P, D).transpose(0, 2, 1, 3).reshape(E, P, ED)
    return np.concatenate([g, b, d], axis=2)


def hadamard():
    h = np.ones((1, 1), np.float32)
    while h.shape[0] < P:
        h = np.block([[h, h], [h, -h]])
    return np.ascontiguousarray(h, dtype=np.float32)


STAGES = ('ffn', 'attn0', 'ffn', 'moe', 'attn1', 'moe')


def kernel(**inputs):
    import concourse.bacc as bacc
    from concourse.bass_utils import run_bass_kernel_spmd as run

    i = {k: np.asarray(v) for k, v in inputs.items()}
    mask_qk, mask_kq = causal_masks()
    steps = np.arange(0, HD, 2, dtype=np.float32) / np.float32(HD)
    cos0, sin0 = rotations(steps * np.log(np.float32(30000.0)))
    cos1, sin1 = rotations(np.float32(1.0) / np.float32(10000.0) ** steps)
    arrays = {
        "x": i["L0_attn_x"][0], "w1t": i["L0_ffn_W1"].T, "w3t": i["L0_ffn_W3"].T, "w2t": i["L0_ffn_W2"].T,
        "ident": np.eye(P, dtype=np.float32), "hadamard": hadamard(), "mask_qk": mask_qk, "mask_kq": mask_kq,
        "router_t": i["L1_ffn_router_weight"].T, "router_b": i["L1_ffn_router_bias"], "down_b": i["L1_ffn_down_proj_bias"],
        "moe_w": expert_rows(i),
        "attn0_wqkv": np.concatenate([i["L0_attn_Wq"], i["L0_attn_Wkv"]], axis=1),
        "attn0_bqkv": np.concatenate([i["L0_attn_bq"], i["L0_attn_bkv"]]),
        "attn1_wqkv": i["L1_attn_w_qkv"].reshape(HEADS, 3, HD, D).transpose(3, 1, 0, 2).reshape(D, 3 * D),
        "attn1_bqkv": i["L1_attn_b_qkv"].reshape(HEADS, 3, HD).transpose(1, 0, 2).reshape(3 * D),
        "wo": i["L0_attn_Wo"], "bo": i["L0_attn_bo"], "head_g": i["L0_attn_ln_g"], "head_b": i["L0_attn_ln_b"],
        "in_gb": np.stack([i["L0_attn_" + k].reshape(KC, P).T for k in ("qn_g", "qn_b", "kvn_g", "kvn_b")], axis=1),
        "attn0_cos": cos0, "attn0_sin": sin0, "attn1_cos": cos1, "attn1_sin": sin1,
    }
    arrays = {k: np.ascontiguousarray(v) for k, v in arrays.items()}
    nc = bacc.Bacc("TRN2", target_bir_lowering=False, num_devices=1)
    aps = {k: nc.dram_tensor("in_" + k, v.shape, F32, kind="ExternalInput").ap() for k, v in arrays.items()}
    out = nc.dram_tensor("out", (T, D), F32, kind="ExternalOutput").ap()
    build(nc, aps, out, STAGES)
    r = run(nc, [{"in_" + k: v for k, v in arrays.items()}], core_ids=[0])
    return r.results[0]["out"].reshape(1, T, D)
```
